# Optimizing a Trainium2 kernel written in Bass

```python
import numpy as np
import jax
import jax.numpy as jnp

def _softmax(x, axis=-1):
    return jax.nn.softmax(x, axis=axis)

def _gelu(x):
    return jax.nn.gelu(x, approximate=True)

def _silu(x):
    return jax.nn.silu(x)

def _sigmoid(x):
    return jax.nn.sigmoid(x)

def _layernorm(x, axis=-1, eps=1e-05):
    m = jnp.mean(x, axis=axis, keepdims=True)
    v = jnp.var(x, axis=axis, keepdims=True)
    return (x - m) / jnp.sqrt(v + eps)

def _scatter_add(tgt, idx, src, axis=0):
    return tgt.at[idx].add(src)

def _segment_sum(src, seg, n):
    return jax.ops.segment_sum(src, seg, n)
kernel_name = 'mk_gnn_preln_d4_gnn_r8_c35749'

def setup_inputs(seed: int=0):
    np.random.seed(seed)
    _w = jnp.asarray

    def _rec_inputs():
        import jax
        import jax.numpy as jnp
        _gk = jax.random.key(seed)
        x = -0.0009044 + 1 * jax.random.normal(jax.random.fold_in(_gk, 1), (12500, 32), jnp.float32)
        src = jax.random.randint(jax.random.fold_in(_gk, 2), (200000,), 0, 12500, jnp.int32)
        dst = jax.random.randint(jax.random.fold_in(_gk, 3), (200000,), 0, 12500, jnp.int32)
        _o = jnp.argsort(dst, stable=True)
        src = src[_o]
        dst = dst[_o]
        edge_attr3_2x32 = -8.16379e-05 + 0.999858 * jax.random.normal(jax.random.fold_in(_gk, 12), (200000, 2, 32), jnp.float32)
        edge_attr_4 = 0.00086875 + 0.999764 * jax.random.normal(jax.random.fold_in(_gk, 13), (200000, 4), jnp.float32)
        edge_attr_8 = jax.random.uniform(jax.random.fold_in(_gk, 14), (200000, 8), jnp.float32, 0.0, 1)
        return (x, src, dst, edge_attr3_2x32, edge_attr_4, edge_attr_8)
    x, src, dst, edge_attr3_2x32, edge_attr_4, edge_attr_8 = _rec_inputs()

    def _L0_gnn_setup():
        import jax, jax.numpy as jnp
        import numpy as np
        N = 6250
        E = 200000
        H = 2
        F = 32
        IN = 32
        OUT = 32
        NEG_SLOPE = 0.2
        key = jax.random.key(seed)
        ks = jax.random.split(key, 11)
        s = 0.1
        return {'feat': jax.random.normal(ks[0], (N, IN), jnp.float32), 'r_feat': jax.random.normal(ks[1], (E, H, F), jnp.float32), 'src': jax.random.randint(ks[2], (E,), 0, N), 'dst': jax.random.randint(ks[3], (E,), 0, N), 'W1': jax.random.normal(ks[4], (IN, OUT), jnp.float32) * s, 'b1': jnp.zeros((OUT,), jnp.float32), 'W2s': jax.random.normal(ks[5], (IN, H * F), jnp.float32) * s, 'b2s': jnp.zeros((H * F,), jnp.float32), 'W2d': jax.random.normal(ks[6], (IN, H * F), jnp.float32) * s, 'b2d': jnp.zeros((H * F,), jnp.float32), 'attn': jax.random.normal(ks[7], (1, H, F), jnp.float32) * s}
    _L0_gnn_all = _L0_gnn_setup()
    _L0_gnn_in = {k: v for k, v in _L0_gnn_all.items() if k in ('W1', 'b1', 'W2s', 'b2s', 'W2d', 'b2d', 'attn')}
    del _L0_gnn_all

    def _L1_gnn_setup():
        import jax, jax.numpy as jnp
        import numpy as np
        N_NODES = 6250
        N_EDGES = 200000
        D_FEAT = 32
        key = jax.random.key(seed)
        kx, ke = jax.random.split(key)
        x = jax.random.normal(kx, (N_NODES, D_FEAT), dtype=jnp.float32)
        edge_index = jax.random.randint(ke, (2, N_EDGES), 0, N_NODES, dtype=jnp.int64)
        return {'x': x, 'edge_index': edge_index, 'num_nodes': N_NODES}
    _L1_gnn_all = _L1_gnn_setup()
    _L1_gnn_in = {k: v for k, v in _L1_gnn_all.items() if k in ()}
    del _L1_gnn_all

    def _L2_gnn_setup():
        import jax, jax.numpy as jnp
        import numpy as np
        N = 4096
        E = 65536
        MUL = 8
        NB = 8
        HR = 64
        NTP = 4 * MUL * MUL
        AVG_NEI = 16.0
        INV_SQRT3 = 1.0 / np.sqrt(3.0)
        ALPHA = 1.0 / np.sqrt(2.0 * MUL)
        key = jax.random.key(seed)
        ks = jax.random.split(key, 12)
        h = jax.random.normal(ks[0], (N, 4 * MUL), jnp.float32)
        edge_index = jax.random.randint(ks[1], (2, E), 0, N)
        edge_sh = jax.random.normal(ks[2], (E, 4), jnp.float32)
        edge_radial = jax.random.uniform(ks[3], (E, NB), jnp.float32)

        def lin(k, fi, fo):
            return (jax.random.normal(k, (fi, fo), jnp.float32) / np.sqrt(fi)).astype(jnp.float32)
        W1 = lin(ks[4], NB, HR)
        b1 = jnp.zeros((HR,), jnp.float32)
        W2 = lin(ks[5], HR, HR)
        b2 = jnp.zeros((HR,), jnp.float32)
        W3 = lin(ks[6], HR, NTP)
        b3 = jnp.zeros((NTP,), jnp.float32)
        Ws = jax.random.normal(ks[7], (MUL, MUL), jnp.float32)
        Wv = jax.random.normal(ks[8], (MUL, MUL), jnp.float32)
        return dict(h=h, edge_index=edge_index, edge_sh=edge_sh, edge_radial=edge_radial, n_atoms=N, W1=W1, b1=b1, W2=W2, b2=b2, W3=W3, b3=b3, Ws=Ws, Wv=Wv)
    _L2_gnn_all = _L2_gnn_setup()
    _L2_gnn_in = {k: v for k, v in _L2_gnn_all.items() if k in ('W1', 'b1', 'W2', 'b2', 'W3', 'b3', 'Ws', 'Wv')}
    del _L2_gnn_all

    def _L3_gnn_setup():
        import jax, jax.numpy as jnp
        import numpy as np
        N_NODES = 6250
        DEG = 16
        N_HEAD = 4
        F_IN = 32
        F_OUT = 32
        key = jax.random.key(seed)
        k_h, k_w, k_fw, k_fb = jax.random.split(key, 4)
        h = jax.random.normal(k_h, (N_NODES, F_IN), dtype=jnp.float32)
        src = jnp.repeat(jnp.arange(N_NODES, dtype=jnp.int64), DEG)
        offs = (jnp.arange(DEG, dtype=jnp.int64) + 1) * 97
        dst = (src.reshape(N_NODES, DEG) + offs[None, :]).reshape(-1) % N_NODES
        edge_index = jnp.stack([src, dst], axis=0)
        gain = 1.414
        bound_w = gain * np.sqrt(6.0 / (F_IN + F_OUT))
        w = jax.random.uniform(k_w, (N_HEAD, F_IN, F_OUT), jnp.float32, -bound_w, bound_w)
        bound_fc = np.sqrt(1.0 / (2 * F_OUT))
        fc_w = jax.random.uniform(k_fw, (1, 2 * F_OUT), jnp.float32, -bound_fc, bound_fc)
        fc_b = jax.random.uniform(k_fb, (1,), jnp.float32, -bound_fc, bound_fc)
        bias = jnp.zeros((F_OUT,), jnp.float32)
        return {'h': h, 'edge_index': edge_index, 'w': w, 'fc_w': fc_w, 'fc_b': fc_b, 'bias': bias}
    _L3_gnn_all = _L3_gnn_setup()
    _L3_gnn_in = {k: v for k, v in _L3_gnn_all.items() if k in ('w', 'fc_w', 'fc_b', 'bias')}
    del _L3_gnn_all
    return {'x': x, 'src': src, 'dst': dst, 'edge_attr3_2x32': edge_attr3_2x32, 'edge_attr_4': edge_attr_4, 'edge_attr_8': edge_attr_8, 'L0_gnn_W1': _L0_gnn_in['W1'], 'L0_gnn_b1': _L0_gnn_in['b1'], 'L0_gnn_W2s': _L0_gnn_in['W2s'], 'L0_gnn_b2s': _L0_gnn_in['b2s'], 'L0_gnn_W2d': _L0_gnn_in['W2d'], 'L0_gnn_b2d': _L0_gnn_in['b2d'], 'L0_gnn_attn': _L0_gnn_in['attn'], 'L2_gnn_W1': _L2_gnn_in['W1'], 'L2_gnn_b1': _L2_gnn_in['b1'], 'L2_gnn_W2': _L2_gnn_in['W2'], 'L2_gnn_b2': _L2_gnn_in['b2'], 'L2_gnn_W3': _L2_gnn_in['W3'], 'L2_gnn_b3': _L2_gnn_in['b3'], 'L2_gnn_Ws': _L2_gnn_in['Ws'], 'L2_gnn_Wv': _L2_gnn_in['Wv'], 'L3_gnn_w': _L3_gnn_in['w'], 'L3_gnn_fc_w': _L3_gnn_in['fc_w'], 'L3_gnn_fc_b': _L3_gnn_in['fc_b'], 'L3_gnn_bias': _L3_gnn_in['bias']}

def reference(x, src, dst, edge_attr3_2x32, edge_attr_4, edge_attr_8, L0_gnn_W1, L0_gnn_b1, L0_gnn_W2s, L0_gnn_b2s, L0_gnn_W2d, L0_gnn_b2d, L0_gnn_attn, L2_gnn_W1, L2_gnn_b1, L2_gnn_W2, L2_gnn_b2, L2_gnn_W3, L2_gnn_b3, L2_gnn_Ws, L2_gnn_Wv, L3_gnn_w, L3_gnn_fc_w, L3_gnn_fc_b, L3_gnn_bias):
    import jax
    import jax.numpy as jnp

    def _L0_gnn_ref(feat, r_feat, src, dst, W1, b1, W2s, b2s, W2d, b2d, attn):
        import jax, jax.numpy as jnp
        import numpy as np
        N = 6250
        E = 200000
        H = 2
        F = 32
        IN = 32
        OUT = 32
        NEG_SLOPE = 0.2
        n = feat.shape[0]
        feat_src = (feat @ W2s + b2s).reshape(n, H, F)
        feat_dst = (feat @ W2d + b2d).reshape(n, H, F)
        en = feat_src[src]
        ev = feat_dst[dst]
        e = jax.nn.leaky_relu(en + ev, negative_slope=NEG_SLOPE)
        e = jnp.sum(e * attn, axis=-1, keepdims=True)
        m = jax.ops.segment_max(e, dst, num_segments=n)
        m = jnp.where(jnp.isfinite(m), m, 0.0)
        ee = jnp.exp(e - m[dst])
        denom = jax.ops.segment_sum(ee, dst, num_segments=n)
        alpha = ee / jnp.maximum(denom[dst], 1e-09)
        msg = jax.nn.softmax(en * r_feat * alpha, axis=-1)
        g_agg = jax.ops.segment_sum(msg, dst, num_segments=n)
        g_sum = jnp.sum(g_agg, axis=1)
        rst = (feat + g_sum) @ W1 + b1
        return rst

    def _L1_gnn_ref(x, edge_index, num_nodes):
        import jax, jax.numpy as jnp
        import numpy as np
        N_NODES = 6250
        N_EDGES = 200000
        D_FEAT = 32
        src = edge_index[0]
        dst = edge_index[1]
        msgs = x[src]
        out = jax.ops.segment_sum(msgs, dst, num_segments=num_nodes)
        return out

    def _L2_gnn_ref(h, edge_index, edge_sh, edge_radial, n_atoms, W1, b1, W2, b2, W3, b3, Ws, Wv):
        import jax, jax.numpy as jnp
        import numpy as np
        N = 4096
        E = 65536
        MUL = 8
        NB = 8
        HR = 64
        NTP = 4 * MUL * MUL
        AVG_NEI = 16.0
        INV_SQRT3 = 1.0 / np.sqrt(3.0)
        ALPHA = 1.0 / np.sqrt(2.0 * MUL)
        src, dst = (edge_index[0], edge_index[1])
        x = jax.nn.silu(edge_radial @ W1 + b1)
        x = jax.nn.silu(x @ W2 + b2)
        tpw = x @ W3 + b3
        P = MUL * MUL
        W00 = tpw[:, 0 * P:1 * P].reshape(-1, MUL, MUL)
        W110 = tpw[:, 1 * P:2 * P].reshape(-1, MUL, MUL)
        W01 = tpw[:, 2 * P:3 * P].reshape(-1, MUL, MUL)
        W10 = tpw[:, 3 * P:4 * P].reshape(-1, MUL, MUL)
        hs = h[:, :MUL]
        hv = h[:, MUL:].reshape(-1, MUL, 3)
        hs_e = hs[src]
        hv_e = hv[src]
        sh0 = edge_sh[:, 0]
        sh1 = edge_sh[:, 1:4]
        m0 = ALPHA * (jnp.einsum('eu,euw->ew', hs_e * sh0[:, None], W00) + INV_SQRT3 * jnp.einsum('eui,ei,euw->ew', hv_e, sh1, W110))
        m1 = ALPHA * (jnp.einsum('eu,ei,euw->ewi', hs_e, sh1, W01) + jnp.einsum('eui,euw->ewi', hv_e * sh0[:, None, None], W10))
        messages = jnp.concatenate([m0, m1.reshape(-1, 3 * MUL)], axis=-1)
        agg = jax.ops.segment_sum(messages, dst, num_segments=n_atoms) / np.sqrt(AVG_NEI)
        self0 = hs @ Ws / np.sqrt(MUL)
        self1 = jnp.einsum('nui,uw->nwi', hv, Wv) / np.sqrt(MUL)
        h_self = jnp.concatenate([self0, self1.reshape(-1, 3 * MUL)], axis=-1)
        return h_self + agg

    def _L3_gnn_ref(h, edge_index, w, fc_w, fc_b, bias):
        import jax, jax.numpy as jnp
        import numpy as np
        N_NODES = 6250
        DEG = 16
        N_HEAD = 4
        F_IN = 32
        F_OUT = 32
        n_head, f_in, f_out = w.shape
        n = h.shape[0]
        src, dst = (edge_index[0], edge_index[1])
        hp = jnp.einsum('nf,hfo->hno', h, w)
        w_src = fc_w[0, :f_out]
        w_dst = fc_w[0, f_out:]
        a_src = jnp.einsum('hnf,f->hn', hp, w_src)
        a_dst = jnp.einsum('hnf,f->hn', hp, w_dst)
        e = a_src[:, src] + a_dst[:, dst] + fc_b[0]
        e = jax.nn.leaky_relu(e, negative_slope=0.2)
        seg_max = jax.ops.segment_max(e.T, src, num_segments=n)
        e = jnp.exp(e - seg_max.T[:, src])
        seg_sum = jax.ops.segment_sum(e.T, src, num_segments=n)
        att = e / seg_sum.T[:, src]
        msg = att[:, :, None] * hp[:, dst, :]
        agg = jax.vmap(lambda m: jax.ops.segment_sum(m, src, num_segments=n))(msg)
        out = agg.mean(axis=0) + bias
        return out
    edge_index = jnp.stack([src, dst])
    h = jnp.maximum(_layernorm(x, axis=-1), 0.0)
    x = x + _L0_gnn_ref(h, edge_attr3_2x32, src, dst, L0_gnn_W1, L0_gnn_b1, L0_gnn_W2s, L0_gnn_b2s, L0_gnn_W2d, L0_gnn_b2d, L0_gnn_attn)
    h = jnp.maximum(_layernorm(x, axis=-1), 0.0)
    x = x + _L1_gnn_ref(h, edge_index, 12500)
    h = jnp.maximum(_layernorm(x, axis=-1), 0.0)
    x = x + _L2_gnn_ref(h, edge_index, edge_attr_4, edge_attr_8, 12500, L2_gnn_W1, L2_gnn_b1, L2_gnn_W2, L2_gnn_b2, L2_gnn_W3, L2_gnn_b3, L2_gnn_Ws, L2_gnn_Wv)
    h = jnp.maximum(_layernorm(x, axis=-1), 0.0)
    x = x + _L3_gnn_ref(h, edge_index, L3_gnn_w, L3_gnn_fc_w, L3_gnn_fc_b, L3_gnn_bias)
    return x

_drawn_inputs = setup_inputs


def setup_inputs(seed=0):
    import zlib

    import numpy as np

    out = dict(_drawn_inputs(seed))
    spreads = {'L0_gnn_b1': (0.0, 0.1),
     'L0_gnn_b2s': (0.0, 0.8),
     'L0_gnn_b2d': (0.0, 2.0),
     'L2_gnn_b1': (0.0, 0.8),
     'L2_gnn_b2': (0.0, 2.0),
     'L2_gnn_b3': (0.0, 2.0),
     'L3_gnn_bias': (0.0, 2.0)}
    factors = {'edge_attr3_2x32': 8.0,
     'edge_attr_4': 3.409,
     'edge_attr_8': 8.0,
     'L0_gnn_W2s': 8.0,
     'L0_gnn_W2d': 8.0,
     'L0_gnn_attn': 8.0,
     'L2_gnn_W1': 4.125,
     'L2_gnn_W2': 3.942,
     'L2_gnn_W3': 3.946,
     'L3_gnn_fc_w': 200.0,
     'L2_gnn_Ws': 60.92,
     'L2_gnn_Wv': 30.067,
     'L3_gnn_w': 35.775}
    for name, (base, spread) in spreads.items():
        noise = np.random.default_rng([zlib.crc32(name.encode()), seed]).standard_normal(out[name].shape)
        drawn = base * np.exp(spread * noise) if base else spread * noise
        out[name] = jnp.asarray(drawn.astype(out[name].dtype))
    for name, factor in factors.items():
        out[name] = (out[name] * factor).astype(out[name].dtype)
    return out
```

```python
import concourse.bass as bass
from concourse import mybir
from contextlib import ExitStack

F32 = mybir.dt.float32
I32 = mybir.dt.int32
BF16 = mybir.dt.bfloat16
ALU = mybir.AluOpType
ACT = mybir.ActivationFunctionType
AX = mybir.AxisListType

NODES, EDGES, FEAT = 12500, 200000, 32
EP = 125
COLS = EDGES // EP
CH = 16
PAIRS = COLS // (2 * CH)
NP = 128
NB = -(-NODES // NP)
TAIL = NODES - (NB - 1) * NP
NPAD = NB * NP
NG = 7
GR = 4
GROUPS = CH // GR
BIG = 1.0e30
HEADS0, HEADS3 = 2, 4


class Chain:

    def __init__(self, eng, sem):
        self.eng, self.sem, self.n = eng, sem, 0

    def link(self, ins):
        self.n += 1
        return ins.then_inc(self.sem, 1)

    def join(self):
        self.eng.wait_ge(self.sem, self.n)

    def step(self, ins):
        self.link(ins)
        self.join()

    def restart(self):
        if self.n:
            self.join()
            self.eng.sem_clear(self.sem)
            self.n = 0


class Kernel:

    def __init__(self, nc, stack):
        self.nc, self.stack, self.sems, self.used, self.owned = nc, stack, {}, [], 0

    def sem(self, name):
        if name not in self.sems:
            self.sems[name] = self.stack.enter_context(self.nc.semaphore(name))
        if name not in self.used:
            self.used.append(name)
        return self.sems[name]

    def own(self, name):
        self.owned += 1
        return self.stack.enter_context(self.nc.semaphore(f"{name}_{self.owned}"))

    def recycle(self):
        names, self.used = self.used, []
        with self.nc.Block() as block:
            @block.sync
            def _(sp):
                for name in names:
                    sp.sem_clear(self.sems[name])

    def wait(self, eng, who, sem, value):
        if isinstance(value, int):
            if value > 0:
                eng.wait_ge(sem, value)
            return
        eng.wait_ge(sem, value)
        eng.sem_inc(self.sem("tick_" + who), 1)


def pairs(eng, body, first=0, end=PAIRS, ahead=False):
    if first == 0:
        body(0)
        first = 1
    with eng.Fori(first, end - ahead) as i:
        body(i)
    if ahead:
        body(end - 1)


def known_ge(t, n):
    return isinstance(t, int) and t >= n


def first_chunk(t):
    return isinstance(t, int) and t == 0


def cols(t):
    return bass.ds(t * CH, CH)


def build(nc, A, out):
    top = ExitStack()
    with top:
        K = Kernel(nc, top)

        names = {}

        def once(name):
            names[name] = names.get(name, 0) + 1
            return name if names[name] == 1 else f"{name}_{names[name]}"

        def sb(stack, name, shape, dt=F32):
            return stack.enter_context(nc.sbuf_tensor(once(name), shape, dt))

        def ps(stack, name, shape, dt=F32):
            return stack.enter_context(nc.psum_tensor(once(name), shape, dt))

        def dram(name, shape, dt=F32):
            return nc.dram_tensor(name, shape, dt, kind="Internal").ap()

        x = sb(top, "x", [NP, NB, FEAT])
        h = sb(top, "h", [NP, NB, FEAT])
        ident = sb(top, "ident", [128, 128])
        identb = sb(top, "identb", [128, 128], BF16)
        ones = sb(top, "ones", [128, 128])
        before = sb(top, "before", [128, 128])
        iota_row = sb(top, "iota_row", [128, 128], BF16)
        pbase = sb(top, "pbase", [128, 1])
        zbias = sb(top, "zbias", [NP, 128])
        zeros = sb(top, "zeros", [EP, 640])
        src_i = sb(top, "src_i", [EP, COLS], I32)
        dst_i = sb(top, "dst_i", [EP, COLS], I32)
        cont = sb(top, "cont", [EP, COLS])
        first_seg = sb(top, "first_seg", [EP, COLS])
        last_seg = sb(top, "last_seg", [EP, COLS])
        endrow = sb(top, "endrow", [EP, 1], I32)
        fwd_row = sb(top, "fwd_row", [128, EP])
        fwd_all = sb(top, "fwd_all", [128, EP])
        bwd_row = sb(top, "bwd_row", [128, EP])
        bwd_all = sb(top, "bwd_all", [128, EP])
        last_dst = sb(top, "last_dst", [NP, NB], I32)
        has_dst = sb(top, "has_dst", [NP, NB])
        first_dst = sb(top, "first_dst", [NP, NB], I32)
        first_src = sb(top, "first_src", [NP, NB], I32)
        last_src = sb(top, "last_src", [NP, NB], I32)
        has_src = sb(top, "has_src", [NP, NB])
        base_src = sb(top, "base_src", [NP, NB])

        tab_s0 = dram("tab_s0", (NPAD, 64))
        tab_d0 = dram("tab_d0", (NPAD, 64))
        tab_h = dram("tab_h", (NPAD, FEAT))
        tab_h3 = dram("tab_h3", (NPAD, FEAT + HEADS3))
        tab_a3 = dram("tab_a3", (NPAD, HEADS3))
        en_rows = dram("en_rows", (EDGES, 64))
        h_rows = dram("h_rows", (EDGES, FEAT))
        ev_rows = dram("ev_rows", (EDGES + NP, 64))
        own_rows = dram("own_rows", (EDGES + NP, HEADS3))
        sums = dram("sums", (EDGES, FEAT))
        sums3 = dram("sums3", (EDGES, HEADS3 * FEAT))
        by_src = dram("by_src", (EDGES, 2), I32)

        def edge_rows(ap):
            if len(ap.shape) == 1:
                return ap.rearrange("(p c) -> p c", p=EP)
            if len(ap.shape) == 2:
                return ap.rearrange("(p c) f -> p c f", p=EP)
            return ap.rearrange("(p c) h f -> p c h f", p=EP)

        def node_rows(ap):
            return ap.rearrange("(b l) f -> l b f", l=NP)

        with ExitStack() as st:
            iota_i = sb(st, "iota_i", [128, 128], I32)
            pbase_i = sb(st, "pbase_i", [128, 1], I32)
            loaded, made, iotas = K.sem("loaded"), K.sem("made"), K.sem("iotas")
            chain_v, chain_p = K.sem("chain_v"), K.sem("chain_p")
            zeroed = K.sem("zeroed")
            block = st.enter_context(nc.Block())

            @block.sync
            def _(sp):
                sp.dma_start(src_i[:, :], edge_rows(A["src"])).then_inc(loaded, 16)
                sp.dma_start(dst_i[:, :], edge_rows(A["dst"])).then_inc(loaded, 16)
                full = (NB - 1) * NP
                sp.dma_start(x[:, 0:NB - 1, :], A["x"][0:full, :].rearrange("(b l) f -> l b f", l=NP)).then_inc(loaded, 16)
                sp.wait_ge(zeroed, 1)
                sp.dma_start(x[0:TAIL, NB - 1, :], A["x"][full:NODES, :]).then_inc(loaded, 16)
                sp.wait_ge(loaded, 64)

            @block.gpsimd
            def _(pool):
                c = Chain(pool, chain_p)
                nc.gpsimd.iota(iota_i[:, :], [[1, 128]], base=0, channel_multiplier=0).then_inc(iotas, 1)
                nc.gpsimd.iota(pbase_i[:, :], [[0, 1]], base=0, channel_multiplier=COLS).then_inc(iotas, 1)
                c.link(nc.gpsimd.memset(ident[:, :], 0.0))
                c.step(nc.gpsimd.memset(before[:, :], 0.0))
                nc.gpsimd.affine_select(out=ident[:, :], in_=ident[:, :], compare_op=ALU.not_equal, fill=1.0,
                                        base=0, pattern=[[-1, 128]], channel_multiplier=1).then_inc(made, 1)
                nc.gpsimd.affine_select(out=before[:, :], in_=before[:, :], compare_op=ALU.is_ge, fill=1.0,
                                        base=0, pattern=[[-1, 128]], channel_multiplier=1).then_inc(made, 1)
                c.restart()

            @block.vector
            def _(dve):
                nc.vector.memset(zeros[:, :], 0.0)
                nc.vector.memset(x[:, NB - 1, :], 0.0).then_inc(zeroed, 1)
                nc.vector.memset(zbias[:, :], 0.0)
                nc.vector.memset(ones[:, :], 1.0)
                dve.wait_ge(iotas, 2)
                nc.vector.tensor_copy(iota_row[:, :], iota_i[:, :])
                nc.vector.tensor_copy(pbase[:, :], pbase_i[:, :])
                dve.wait_ge(made, 2)
                nc.vector.tensor_copy(identb[:, :], ident[:, :])
        K.recycle()

        def edge_masks(key_i, first_keys, last_keys):
            with ExitStack() as st:
                key = sb(st, "key", [EP, COLS])
                nxt_i = sb(st, "nxt_i", [EP, 1], I32)
                nxt = sb(st, "nxt", [EP, 1])
                prv_i = sb(st, "prv_i", [EP, 1], I32)
                prv = sb(st, "prv", [EP, 1])
                goes_on = sb(st, "goes_on", [EP, 4])
                length = sb(st, "length", [EP, 1])
                diag = sb(st, "diag", [EP, 2, EP])
                rows = ps(st, "rows", [128, 2, 512])
                loaded, filled, diags, rowed, chain_v = (K.sem(n) for n in ("loaded", "filled", "diags", "rowed", "chain_v"))
                block = st.enter_context(nc.Block())

                @block.sync
                def _(sp):
                    sp.wait_ge(filled, 1)
                    sp.dma_start(nxt_i[0:EP - 1, :], first_keys[1:EP, :], allow_slow_non_contiguous=True).then_inc(loaded, 16)
                    sp.dma_start(prv_i[1:EP, :], last_keys[0:EP - 1, :], allow_slow_non_contiguous=True).then_inc(loaded, 16)

                @block.tensor
                def _(pe):
                    pe.wait_ge(diags, 2)
                    for k in range(2):
                        nc.tensor.matmul(rows[:, k, 0:EP], ones[0:EP, :], diag[:, k, :], start=True, stop=True).then_inc(rowed, 1)

                @block.vector
                def _(dve):
                    c = Chain(dve, chain_v)
                    c.step(nc.vector.memset(prv_i[:, :], -1))
                    nc.vector.memset(nxt_i[:, :], -1).then_inc(filled, 1)
                    c.step(nc.vector.tensor_copy(key[:, :], key_i))
                    c.step(nc.vector.tensor_tensor(cont[:, 1:COLS], key[:, 1:COLS], key[:, 0:COLS - 1], ALU.is_equal))
                    c.link(nc.vector.memset(first_seg[:, 0:1], 1.0))
                    c.link(nc.vector.memset(last_seg[:, COLS - 1:COLS], 1.0))
                    c.link(nc.vector.tensor_tensor_scan(first_seg[:, 1:COLS], cont[:, 1:COLS], cont[:, 1:COLS], 1.0, ALU.mult, ALU.min))
                    c.step(nc.vector.tensor_tensor_scan(last_seg[:, 0:COLS - 1][:, ::-1], cont[:, 1:COLS][:, ::-1], cont[:, 1:COLS][:, ::-1],
                                                        1.0, ALU.mult, ALU.min))
                    c.step(nc.vector.reduce_sum(length[:, :], first_seg[:, :], axis=AX.X))
                    c.step(nc.vector.scalar_tensor_tensor(length[:, :], length[:, :], -1.0, pbase[0:EP, :], ALU.add, ALU.add))
                    c.link(nc.vector.tensor_copy(endrow[:, :], length[:, :]))
                    dve.wait_ge(loaded, 32)
                    c.link(nc.vector.tensor_copy(prv[:, :], prv_i[:, :]))
                    c.step(nc.vector.tensor_copy(nxt[:, :], nxt_i[:, :]))
                    c.link(nc.vector.tensor_tensor(cont[:, 0:1], key[:, 0:1], prv[:, :], ALU.is_equal))
                    c.step(nc.vector.tensor_tensor(goes_on[:, 0:1], key[:, COLS - 1:COLS], nxt[:, :], ALU.is_equal))
                    nc.vector.tensor_scalar(diag[:, 0, :], ident[0:EP, 0:EP], goes_on[:, 0:1], None, ALU.mult).then_inc(diags, 1)
                    nc.vector.tensor_scalar(diag[:, 1, :], ident[0:EP, 0:EP], first_seg[:, COLS - 1:COLS], None, ALU.mult).then_inc(diags, 1)
                    dve.wait_ge(rowed, 2)
                    c.link(nc.vector.memset(bwd_row[:, 0:1], 0.0))
                    c.link(nc.vector.tensor_copy(bwd_row[:, 1:EP], rows[:, 0, 0:EP - 1]))
                    c.step(nc.vector.tensor_copy(fwd_row[:, :], rows[:, 0, 0:EP]))
                    c.link(nc.vector.tensor_tensor(fwd_all[:, :], fwd_row[:, :], rows[:, 1, 0:EP], ALU.mult))
                    c.link(nc.vector.tensor_tensor(bwd_all[:, :], bwd_row[:, :], rows[:, 1, 0:EP], ALU.mult))
                    c.restart()
            K.recycle()

        def normalize():
            with ExitStack() as st:
                d = sb(st, "d", [NP, NB, FEAT])
                sq = sb(st, "sq", [NP, NB, FEAT])
                mean = sb(st, "mean", [NP, NB])
                var = sb(st, "var", [NP, NB])
                std = sb(st, "std", [NP, NB])
                varied, rooted, chain_v = K.sem("varied"), K.sem("rooted"), K.sem("chain_v")
                block = st.enter_context(nc.Block())

                def wide(ap):
                    return ap[:, :].unsqueeze(2).to_broadcast([NP, NB, FEAT])

                @block.scalar
                def _(act):
                    act.wait_ge(varied, 1)
                    nc.scalar.activation(std[:, :], var[:, :], ACT.Sqrt).then_inc(rooted, 1)

                @block.vector
                def _(dve):
                    c = Chain(dve, chain_v)
                    c.step(nc.vector.reduce_sum(mean[:, :], x[:, :, :], axis=AX.X))
                    c.step(nc.vector.tensor_scalar(mean[:, :], mean[:, :], 1.0 / FEAT, None, ALU.mult))
                    c.step(nc.vector.tensor_tensor(d[:, :, :], x[:, :, :], wide(mean), ALU.subtract))
                    c.step(nc.vector.tensor_tensor(sq[:, :, :], d[:, :, :], d[:, :, :], ALU.mult))
                    c.step(nc.vector.reduce_sum(var[:, :], sq[:, :, :], axis=AX.X))
                    nc.vector.tensor_scalar(var[:, :], var[:, :], 1.0 / FEAT, 1e-5, ALU.mult, ALU.add).then_inc(varied, 1)
                    dve.wait_ge(rooted, 1)
                    c.step(nc.vector.reciprocal(mean[:, :], std[:, :]))
                    c.step(nc.vector.scalar_tensor_tensor(h[:, :, :], d[:, :, :], 0.0, wide(mean), ALU.max, ALU.mult))
                    c.restart()
            K.recycle()

        def node_product(src, width, weights, n_out, put):
            per_bank = 512 // n_out
            with ExitStack() as st:
                turned_ps = [ps(st, f"turned_ps{k}", [128, 2, 512]) for k in range(2)]
                turned = [sb(st, f"turned{k}", [width, 2, 512]) for k in range(2)]
                prod = [ps(st, f"prod{k}", [NP, 2, 512]) for k in range(2)]
                stage = [sb(st, f"stage{k}", [NP, NG, width]) for k in range(2)]
                n_staged = K.sem("n_staged")
                n_turned, n_copied, n_prod, n_put = (K.sem(n) for n in ("n_turned", "n_copied", "n_prod", "n_put"))
                chain_v = K.sem("chain_v")
                block = st.enter_context(nc.Block())
                steps = NB // NG

                def place(j):
                    return (0, j) if j < 4 else (1, j - 4)

                @block.tensor
                def _(pe):
                    def turn(g, k):
                        for j in range(NG):
                            a, b = place(j)
                            last = nc.tensor.transpose(turned_ps[k][0:width, a, b * 128:(b + 1) * 128], stage[k][:, j, :], ident[:, :])
                        last.then_inc(n_turned, 1)

                    def body(i):
                        for k in range(2):
                            g = 2 * i + k
                            K.wait(pe, "pe", n_copied, g - 1)
                            K.wait(pe, "pe", n_staged, g + 1)
                            turn(g, k)
                            K.wait(pe, "pe", n_copied, g + 1)
                            K.wait(pe, "pe", n_put, g - 1)
                            for j in range(NG):
                                a, b = place(j)
                                q, r = j // per_bank, j % per_bank
                                last = nc.tensor.matmul(prod[k][:, q, r * n_out:(r + 1) * n_out],
                                                        turned[k][:, a, b * 128:(b + 1) * 128], weights, start=True, stop=True)
                            last.then_inc(n_prod, 1)
                    body(0)
                    with pe.Fori(1, steps // 2) as i:
                        body(i)

                @block.scalar
                def _(act):
                    def body(i):
                        for k in range(2):
                            g = 2 * i + k
                            K.wait(act, "act", n_turned, g - 1)
                            nc.scalar.copy(stage[k][:, :, :], src[:, bass.ds(g * NG, NG), :]).then_inc(n_staged, 1)
                            K.wait(act, "act", n_turned, g + 1)
                            K.wait(act, "act", n_prod, g - 1)
                            nc.scalar.copy(turned[k][:, 0, :], turned_ps[k][0:width, 0, :])
                            nc.scalar.copy(turned[k][:, 1, 0:(NG - 4) * 128],
                                           turned_ps[k][0:width, 1, 0:(NG - 4) * 128]).then_inc(n_copied, 1)
                    body(0)
                    with act.Fori(1, steps // 2) as i:
                        body(i)

                @block.vector
                def _(dve):
                    def body(i):
                        for k in range(2):
                            g = 2 * i + k
                            K.wait(dve, "dve", n_prod, g + 1)
                            views = []
                            j = 0
                            while j < NG:
                                m = min(per_bank, NG - j)
                                views.append((j, m, prod[k][:, j // per_bank, 0:m * n_out].rearrange("p (j o) -> p j o", o=n_out)))
                                j += m
                            put(dve, views, g).then_inc(n_put, 1)
                    body(0)
                    with dve.Fori(1, steps // 2) as i:
                        body(i)
            K.recycle()

        def segment_ends(table, width, last_rows, target):
            final = edge_rows(table)[:, COLS - 1, :]
            with ExitStack() as st:
                tails = sb(st, "tails", [EP, width])
                tails_t = sb(st, "tails_t", [width, EP])
                carry_t = sb(st, "carry_t", [width, EP + 1])
                ends = sb(st, "ends", [EP, width])
                fixed = sb(st, "fixed", [EP, width])
                turn = ps(st, "turn", [width, EP])
                back = ps(st, "back", [EP, width])
                loaded, turned, scanned, backed, mended, chain_v = (K.sem(n) for n in (
                    "loaded", "turned", "scanned", "backed", "mended", "chain_v"))
                got, put_back, gathered = (K.own(n) for n in ("got", "put_back", "gathered"))
                block = st.enter_context(nc.Block())

                @block.sync
                def _(sp):
                    sp.dma_start(tails[:, :], final).then_inc(loaded, 16)

                @block.tensor
                def _(pe):
                    pe.wait_ge(loaded, 16)
                    nc.tensor.transpose(turn[:, :], tails[:, :], ident[0:EP, 0:EP]).then_inc(turned, 1)
                    pe.wait_ge(scanned, 1)
                    nc.tensor.transpose(back[:, :], carry_t[:, 0:EP], ident[0:width, 0:width]).then_inc(backed, 1)

                @block.vector
                def _(dve):
                    c = Chain(dve, chain_v)
                    dve.wait_ge(turned, 1)
                    c.link(nc.vector.memset(carry_t[:, 0:1], 0.0))
                    c.step(nc.vector.tensor_tensor(tails_t[:, :], turn[:, :], fwd_row[0:width, :], ALU.mult))
                    nc.vector.tensor_tensor_scan(carry_t[:, 1:EP + 1], fwd_all[0:width, :], tails_t[:, :], 0.0,
                                                 ALU.mult, ALU.add).then_inc(scanned, 1)
                    dve.wait_ge(backed, 1)
                    dve.wait_ge(got, 16)
                    nc.vector.tensor_tensor(fixed[:, :], back[:, :], ends[:, :], ALU.add).then_inc(mended, 1)
                    c.restart()

                @block.gpsimd
                def _(pool):
                    pool.indirect_dma_start(ends[:, :], None, table, bass.IndirectOffsetOnAxis(ap=endrow[:, 0:1], axis=0)).then_inc(got, 16)
                    pool.wait_ge(mended, 1)
                    pool.wait_ge(loaded, 16)
                    pool.indirect_dma_start(table, bass.IndirectOffsetOnAxis(ap=endrow[:, 0:1], axis=0), fixed[:, :], None).then_inc(put_back, 16)
                    pool.wait_ge(put_back, 16)
                    for b in range(NB):
                        pool.indirect_dma_start(target[:, b, :], None, table,
                                                bass.IndirectOffsetOnAxis(ap=last_rows[:, b:b + 1], axis=0)).then_inc(gathered, 16)
                    pool.wait_ge(gathered, 16 * NB)
            K.recycle()

        class SegmentSums:

            def __init__(self, st, width, table):
                self.width, self.table = width, edge_rows(table)
                self.fresh = [sb(st, f"fresh{k}", [EP, width, CH + 1]) for k in range(2)]
                self.keep = [sb(st, f"keep{k}", [EP, width, CH + 1]) for k in range(2)]
                self.run = [sb(st, f"run{k}", [EP, width, CH + 1]) for k in range(2)]
                self.rows = [sb(st, f"rows{k}", [EP, CH, width]) for k in range(2)]
                self.kept, self.scanned, self.copied = K.sem("kept"), K.sem("scanned"), K.sem("copied")
                self.stored = [K.sem(f"stored{k}") for k in range(2)]

            def message(self, k):
                return self.fresh[k][:, :, 1:CH + 1]

            def start(self):
                for k in range(2):
                    last = nc.vector.memset(self.keep[k][:, :, 0], 0.0)
                return [last, nc.vector.memset(self.run[1][:, :, CH], 0.0)]

            def mask(self, act, t, k):
                K.wait(act, "act", self.scanned, t - 1)
                flags = cont[:, cols(t)].unsqueeze(1).to_broadcast([EP, self.width, CH])
                nc.scalar.copy(self.keep[k][:, :, 1:CH + 1], flags).then_inc(self.kept, 1)

            def scan(self, dve, c, t, k):
                c.step(nc.vector.tensor_copy(self.fresh[k][:, :, 0], self.run[1 - k][:, :, CH]))
                K.wait(dve, "dve", self.kept, t + 1)
                K.wait(dve, "dve", self.copied, t - 1)
                flat = lambda ap: ap[:, :, :].rearrange("p f c -> p (f c)")
                nc.vector.tensor_tensor_scan(flat(self.run[k]), flat(self.keep[k]), flat(self.fresh[k]), 0.0,
                                             ALU.mult, ALU.add).then_inc(self.scanned, 1)
                K.wait(dve, "dve", self.scanned, t + 1)

            def store(self, act, t, k, i):
                K.wait(act, "act", self.scanned, t + 1)
                K.wait(act, "act", self.stored[k], i * 16)
                nc.scalar.copy(self.rows[k][:, :, :], self.run[k][:, :, 1:CH + 1].rearrange("p f c -> p c f")).then_inc(self.copied, 1)
                K.wait(act, "act", self.copied, t + 1)
                act.dma_start(self.table[:, cols(t), :], self.rows[k][:, :, :]).then_inc(self.stored[k], 16)

            def finish(self, act):
                for k in range(2):
                    act.wait_ge(self.stored[k], 16 * PAIRS)

        class Spread:

            def __init__(self, st, width, table):
                self.width, self.whole, self.table = width, table, edge_rows(table[0:EDGES, :])
                self.raw = [sb(st, f"raw{k}", [EP, CH, width]) for k in range(2)]
                self.fresh = [sb(st, f"sfresh{k}", [EP, width, CH + 1]) for k in range(2)]
                self.keep = [sb(st, f"skeep{k}", [EP, width, CH + 1]) for k in range(2)]
                self.run = [sb(st, f"srun{k}", [EP, width, CH + 1]) for k in range(2)]
                self.init = sb(st, "sinit", [EP, width])
                self.raw_in = [K.sem(f"raw_in{k}") for k in range(2)]
                self.laid, self.spread = K.sem("spread_laid"), K.sem("spread_done")

            def rows(self, k):
                return self.run[k][:, :, 1:CH + 1].rearrange("p f c -> p c f")

            def place(self, pool, nodes, first_rows, table_of_nodes, first_key, scattered):
                for b in range(NB):
                    pool.indirect_dma_start(self.whole, bass.IndirectOffsetOnAxis(ap=first_rows[:, b:b + 1], axis=0),
                                            nodes(b), None).then_inc(scattered, 16)
                pool.indirect_dma_start(self.init[:, :], None, table_of_nodes,
                                        bass.IndirectOffsetOnAxis(ap=first_key, axis=0)).then_inc(scattered, 16)

            PLACED = 16 * (NB + 1)

            def start(self):
                for k in range(2):
                    last = nc.vector.memset(self.keep[k][:, :, 0], 0.0)
                return [last, nc.vector.tensor_copy(self.run[1][:, :, CH], self.init[:, :])]

            def load(self, eng, t, k):
                eng.dma_start(self.raw[k][:, :, :], self.table[:, cols(t), :]).then_inc(self.raw_in[k], 16)

            def lay(self, act, t, k, i):
                K.wait(act, "act", self.spread, t - 1)
                flags = cont[:, cols(t)].unsqueeze(1).to_broadcast([EP, self.width, CH])
                nc.scalar.copy(self.keep[k][:, :, 1:CH + 1], flags)
                K.wait(act, "act", self.raw_in[k], i * 16 + 16)
                nc.scalar.copy(self.fresh[k][:, :, 1:CH + 1], self.raw[k][:, :, :].rearrange("p c f -> p f c")).then_inc(self.laid, 1)

            def scan(self, dve, c, t, k):
                c.step(nc.vector.tensor_copy(self.fresh[k][:, :, 0], self.run[1 - k][:, :, CH]))
                K.wait(dve, "dve", self.laid, t + 1)
                flat = lambda ap: ap[:, :, :].rearrange("p f c -> p (f c)")
                nc.vector.tensor_tensor_scan(flat(self.run[k]), flat(self.keep[k]), flat(self.fresh[k]), 0.0,
                                             ALU.mult, ALU.add).then_inc(self.spread, 1)
                K.wait(dve, "dve", self.spread, t + 1)

        def segment_softmax(e, n_heads, floor):
            with ExitStack() as st:
                neg_cont = sb(st, "neg_cont", [EP, COLS])
                neg_first = sb(st, "neg_first", [EP, COLS])
                neg_last = sb(st, "neg_last", [EP, COLS])
                is_last = sb(st, "is_last", [EP, COLS])
                nxt = sb(st, "nxt_same", [EP, COLS])
                run = sb(st, "run", [EP, n_heads, COLS])
                tot = sb(st, "tot", [EP, n_heads, COLS])
                edge_t = sb(st, "edge_t", [n_heads, 2, EP])
                flags_t = sb(st, "flags_t", [n_heads, 4, EP])
                carry_t = sb(st, "carry_t", [n_heads, 2, EP + 1])
                carry = sb(st, "carry", [EP, 2, n_heads])
                turn = ps(st, "turn", [n_heads, 2, 512])
                back = ps(st, "back", [EP, 2, 512])
                tot_done, turned, scanned, backed, shifted, exped, chain_v = (K.sem(n) for n in (
                    "tot_done", "turned", "scanned", "backed", "shifted", "exped", "chain_v"))
                block = st.enter_context(nc.Block())

                @block.tensor
                def _(pe):
                    for r in range(2):
                        pe.wait_ge(tot_done, r + 1)
                        nc.tensor.transpose(turn[:, 0, 0:EP], tot[:, :, COLS - 1], ident[0:EP, 0:EP])
                        nc.tensor.transpose(turn[:, 1, 0:EP], tot[:, :, 0], ident[0:EP, 0:EP]).then_inc(turned, 1)
                        pe.wait_ge(scanned, r + 1)
                        nc.tensor.transpose(back[:, 0, 0:n_heads], carry_t[:, 0, 0:EP], ident[0:n_heads, 0:n_heads])
                        nc.tensor.transpose(back[:, 1, 0:n_heads], carry_t[:, 1, 1:EP + 1], ident[0:n_heads, 0:n_heads]).then_inc(backed, 1)

                @block.scalar
                def _(act):
                    act.wait_ge(shifted, 1)
                    nc.scalar.activation(e[:, :, :], e[:, :, :], ACT.Exp).then_inc(exped, 1)

                @block.vector
                def _(dve):
                    c = Chain(dve, chain_v)

                    def totals(r, cmul, op0, op1):
                        for j in range(n_heads):
                            c.link(nc.vector.tensor_tensor_scan(run[:, j, :], cmul[:, :], e[:, j, :], -BIG if op1 == ALU.max else 0.0, op0, op1))
                        c.join()
                        ends = is_last[:, :].unsqueeze(1).to_broadcast([EP, n_heads, COLS])
                        c.step(nc.vector.tensor_tensor(run[:, :, :], run[:, :, :], ends, ALU.mult))
                        for j in range(n_heads):
                            c.link(nc.vector.tensor_tensor_scan(tot[:, j, ::-1], nxt[:, ::-1], run[:, j, ::-1], 0.0, ALU.mult, ALU.add))
                        c.join()
                        dve.sem_inc(tot_done, 1)
                        dve.wait_ge(turned, r + 1)
                        comb = ALU.add if op1 == ALU.max else ALU.mult
                        c.link(nc.vector.tensor_tensor(edge_t[:, 0, :], turn[:, 0, 0:EP], flags_t[:, 0, :], comb))
                        c.link(nc.vector.tensor_tensor(edge_t[:, 1, :], turn[:, 1, 0:EP], flags_t[:, 1, :], comb))
                        none = -BIG if op1 == ALU.max else 0.0
                        c.link(nc.vector.memset(carry_t[:, 0, 0:1], none))
                        c.step(nc.vector.memset(carry_t[:, 1, EP:EP + 1], none))
                        c.link(nc.vector.tensor_tensor_scan(carry_t[:, 0, 1:EP + 1], flags_t[:, 2, :], edge_t[:, 0, :], none, comb, op1))
                        c.step(nc.vector.tensor_tensor_scan(carry_t[:, 1, 0:EP][:, ::-1], flags_t[:, 3, ::-1], edge_t[:, 1, ::-1], none, comb, op1))
                        dve.sem_inc(scanned, 1)
                        dve.wait_ge(backed, r + 1)
                        c.step(nc.vector.tensor_copy(carry[:, :, :], back[:, :, 0:n_heads]))
                        for side, member in enumerate((neg_first, neg_last) if op1 == ALU.max else (first_seg, last_seg)):
                            for j in range(n_heads):
                                c.link(nc.vector.scalar_tensor_tensor(tot[:, j, :], member[:, :], carry[:, side, j:j + 1], tot[:, j, :], comb, op1))
                            c.join()

                    flag_rows = (fwd_row, bwd_row, fwd_all, bwd_all)
                    for src_mask, dst_mask in ((cont, neg_cont), (first_seg, neg_first), (last_seg, neg_last)):
                        c.link(nc.vector.tensor_scalar(dst_mask[:, :], src_mask[:, :], BIG, -BIG, ALU.mult, ALU.add))
                    for n, row in enumerate(flag_rows):
                        c.link(nc.vector.tensor_scalar(flags_t[:, n, :], row[0:n_heads, :], BIG, -BIG, ALU.mult, ALU.add))
                    c.link(nc.vector.tensor_copy(nxt[:, 0:COLS - 1], cont[:, 1:COLS]))
                    c.link(nc.vector.memset(nxt[:, COLS - 1:COLS], 0.0))
                    c.join()
                    c.step(nc.vector.tensor_scalar(is_last[:, :], nxt[:, :], -1.0, 1.0, ALU.mult, ALU.add))
                    totals(0, neg_cont, ALU.add, ALU.max)
                    nc.vector.tensor_tensor(e[:, :, :], e[:, :, :], tot[:, :, :], ALU.subtract).then_inc(shifted, 1)
                    for n, row in enumerate(flag_rows):
                        c.link(nc.vector.tensor_copy(flags_t[:, n, :], row[0:n_heads, :]))
                    c.join()
                    dve.wait_ge(exped, 1)
                    totals(1, cont, ALU.mult, ALU.add)
                    c.step(nc.vector.tensor_scalar(tot[:, :, :], tot[:, :, :], floor, None, ALU.max))
                    c.step(nc.vector.reciprocal(run[:, :, :], tot[:, :, :]))
                    c.step(nc.vector.tensor_tensor(e[:, :, :], e[:, :, :], run[:, :, :], ALU.mult))
                    c.restart()
            K.recycle()

        def load(pairs_):
            loaded = K.sem("loaded")
            with nc.Block() as block:
                @block.sync
                def _(sp):
                    for target, source in pairs_:
                        sp.dma_start(target, source, allow_slow_non_contiguous=True).then_inc(loaded, 16)
                    sp.wait_ge(loaded, 16 * len(pairs_))
            K.recycle()

        def on_all(ap, n=NP):
            return ap.unsqueeze(0).to_broadcast([n, ap.shape[0]])

        def store_table(pairs_):
            stored = K.sem("stored0")
            with nc.Block() as block:
                @block.sync
                def _(sp):
                    for target, source in pairs_:
                        sp.dma_start(target, source, allow_slow_non_contiguous=True).then_inc(stored, 16)
                    sp.wait_ge(stored, 16 * len(pairs_))
            K.recycle()

        def masked_add(has, scale):
            chain_v = K.sem("chain_v")
            with nc.Block() as block:
                @block.vector
                def _(dve):
                    c = Chain(dve, chain_v)
                    wide = has[:, :].unsqueeze(2).to_broadcast([NP, NB, FEAT])
                    c.step(nc.vector.tensor_tensor(agg[:, :, :], agg[:, :, :], wide, ALU.mult))
                    c.step(nc.vector.scalar_tensor_tensor(x[:, :, :], agg[:, :, :], scale, x[:, :, :], ALU.mult, ALU.add))
                    c.restart()
            K.recycle()

        edge_masks(dst_i[:, :], edge_rows(A["dst"])[:, 0:1], edge_rows(A["dst"])[:, COLS - 1:COLS])
        normalize()
        e0 = ExitStack()
        alpha = sb(e0, "alpha", [EP, HEADS0, COLS])
        lo_s = sb(e0, "lo_s", [EP, COLS], BF16)
        hi_s = sb(e0, "hi_s", [EP, COLS], BF16)
        fd_stack = ExitStack()
        f_d = sb(fd_stack, "f_d", [NP, NB, 64])
        with ExitStack() as st:
            w = sb(st, "w_sd", [FEAT, 128])
            bias = sb(st, "b_sd", [NP, 128])
            f_s = sb(st, "f_s", [NP, NB, 64])
            load([(w[:, 0:64], A["L0_gnn_W2s"]), (w[:, 64:128], A["L0_gnn_W2d"]),
                  (bias[:, 0:64], on_all(A["L0_gnn_b2s"])), (bias[:, 64:128], on_all(A["L0_gnn_b2d"]))])

            def put(dve, views, g):
                for j, m, v in views:
                    at = bass.ds(g * NG + j, m)
                    for half, f in enumerate((f_s, f_d)):
                        side = slice(64 * half, 64 * half + 64)
                        last = nc.vector.tensor_tensor(f[:, at, :], v[:, :, side], bias[:, side].unsqueeze(1).to_broadcast([NP, m, 64]), ALU.add)
                return last
            node_product(h, FEAT, w[:, :], 128, put)
            store_table([(node_rows(tab_s0), f_s[:, :, :]), (node_rows(tab_d0), f_d[:, :, :])])

        FILL = 6400
        PIECES = COLS * 64 // FILL + COLS * HEADS3 // FILL
        EARLY = 11
        with ExitStack() as st:
            lo_d = sb(st, "lo_d", [EP, COLS], BF16)
            hi_d = sb(st, "hi_d", [EP, COLS], BF16)
            bits = sb(st, "bits", [EP, COLS], I32)
            attn = sb(st, "attn", [EP, 64])
            idx = [sb(st, f"idx{k}", [EP, CH], I32) for k in range(2)]
            en = [sb(st, f"en{k}", [EP, CH, 64]) for k in range(2)]
            en_back = [sb(st, f"en_back{k}", [EP, CH, 64]) for k in range(2)]
            zw = sb(st, "zw", [EP, CH, 64])
            hot_lo = [sb(st, f"hot_lo{k}", [EP, CH, 128], BF16) for k in range(2)]
            hot_hi = [sb(st, f"hot_hi{k}", [EP, CH, NB], BF16) for k in range(2)]
            counts = sb(st, "counts", [NP, NB])
            block_tot = sb(st, "block_tot", [NP, NB])
            start_of = sb(st, "start_of", [NP, NB])
            end_f = sb(st, "end_f", [NP, NB])
            lane = sb(st, "lane", [NP, 1])
            cnt_ps = [ps(st, f"cnt_ps{k}", [NP, NB]) for k in range(2)]
            tot_ps = ps(st, "tot_ps", [NP, NB])
            pre_ps = ps(st, "pre_ps", [NP, NB])
            ev = Spread(st, 64, ev_rows)
            idx_in = [K.sem(f"idx_in{k}") for k in range(2)]
            gathered = [K.own(f"gathered{k}") for k in range(2)]
            placed = K.own("placed")
            stored = [K.sem(f"stored{k}") for k in range(2)]
            back_in = [K.sem(f"back_in{k}") for k in range(2)]
            cleared, scored, hots, counted, copied, summed, starts, chain_v, loaded = (
                K.sem(n) for n in ("cleared", "scored", "hots", "counted", "copied", "summed", "starts", "chain_v", "loaded"))
            block = st.enter_context(nc.Block())
            src_rows = edge_rows(A["src"])

            @block.sync
            def _(sp):
                sp.dma_start(attn[:, :], on_all(A["L0_gnn_attn"].rearrange("a h f -> (a h f)"), EP)).then_inc(loaded, 16)
                for k in range(2):
                    sp.dma_start(idx[k][:, :], src_rows[:, cols(k)]).then_inc(idx_in[k], 16)

                def body(i):
                    for k in range(2):
                        t = 2 * i + k
                        K.wait(sp, "sp", gathered[k], (i + 1) * (16 * CH))
                        sp.dma_start(edge_rows(en_rows)[:, cols(t), :], en[k][:, :, :]).then_inc(stored[k], 16)
                        if not known_ge(t, 2 * PAIRS - 2):
                            sp.dma_start(idx[k][:, :], src_rows[:, cols(t + 2)]).then_inc(idx_in[k], 16)
                pairs(sp, body, ahead=True)
                for k in range(2):
                    sp.wait_ge(stored[k], 16 * PAIRS)

            @block.gpsimd
            def _(pool):
                def body(i):
                    for k in range(2):
                        K.wait(pool, "pool", idx_in[k], i * 16 + 16)
                        K.wait(pool, "pool", stored[k], i * 16)
                        for g in range(CH):
                            pool.indirect_dma_start(en[k][:, g, :], None, tab_s0,
                                                    bass.IndirectOffsetOnAxis(ap=idx[k][:, g:g + 1], axis=0)).then_inc(gathered[k], 16)
                pairs(pool, body, end=EARLY)
                pool.wait_ge(cleared, 16 * PIECES)
                pool.wait_ge(starts, 1)
                ev.place(pool, lambda b: f_d[:, b, :], first_dst, tab_d0, dst_i[:, 0:1], placed)
                pairs(pool, body, first=EARLY)

            @block.scalar
            def _(act):
                zeroed_pieces = 0

                def bring(t, k, i):
                    K.wait(act, "act", scored, t - 1)
                    K.wait(act, "act", stored[k], i * 16 + 16)
                    act.dma_start(en_back[k][:, :, :], edge_rows(en_rows)[:, cols(t), :]).then_inc(back_in[k], 16)
                    ev.load(act, t, k)
                for table, width in ((ev_rows, 64), (own_rows, HEADS3)):
                    filled = edge_rows(table[0:EDGES, :]).rearrange("p c f -> p (c f)")
                    for n in range(COLS * width // FILL):
                        act.dma_start(filled[:, n * FILL:(n + 1) * FILL].rearrange("p (n r) -> p n r", r=zeros.shape[1]),
                                      zeros[:, :].unsqueeze(1).to_broadcast([EP, FILL // zeros.shape[1], zeros.shape[1]])).then_inc(cleared, 16)
                        zeroed_pieces += 1
                        act.wait_ge(cleared, 16 * zeroed_pieces)
                act.wait_ge(placed, ev.PLACED)
                bring(0, 0, 0)
                bring(1, 1, 0)
                ev.lay(act, 0, 0, 0)

                def body(i):
                    for k in range(2):
                        t = 2 * i + k
                        if not known_ge(t, 2 * PAIRS - 1):
                            ev.lay(act, t + 1, 1 - k, i + k)
                        if not known_ge(t, 2 * PAIRS - 2):
                            bring(t + 2, k, i + 1)
                pairs(act, body, ahead=True)

            @block.tensor
            def _(pe):
                for q in range(2):
                    nc.tensor.matmul(cnt_ps[q][:, :], zbias[:, :], zbias[:, 0:NB], start=True, stop=False)

                    def body(i):
                        for k in range(2):
                            t = 2 * i + k
                            K.wait(pe, "pe", hots, t + 1 + q * (2 * PAIRS))
                            for g in range(CH):
                                last = nc.tensor.matmul(cnt_ps[q][:, :], hot_lo[k][:, g, :], hot_hi[k][:, g, :], start=False, stop=False)
                            last.then_inc(counted, 1)
                    pairs(pe, body)
                    nc.tensor.matmul(cnt_ps[q][:, :], zbias[:, :], zbias[:, 0:NB], start=False, stop=True).then_inc(counted, 1)
                    pe.wait_ge(copied, q + 1)
                    nc.tensor.matmul(tot_ps[:, :], ones[:, :], counts[:, :], start=True, stop=True)
                    nc.tensor.matmul(pre_ps[:, :], before[:, :], counts[:, :], start=True, stop=True).then_inc(summed, 1)

            @block.vector
            def _(dve):
                c = Chain(dve, chain_v)
                for key, lo, hi in ((src_i, lo_s, hi_s), (dst_i, lo_d, hi_d)):
                    c.step(nc.vector.tensor_scalar(bits[:, :], key[:, :], 127, None, ALU.bitwise_and))
                    c.step(nc.vector.tensor_copy(lo[:, :], bits[:, :]))
                    c.step(nc.vector.tensor_scalar(bits[:, :], key[:, :], 7, None, ALU.arith_shift_right))
                    c.step(nc.vector.tensor_copy(hi[:, :], bits[:, :]))
                c.step(nc.vector.tensor_scalar(lane[:, :], pbase[:, :], 1.0 / COLS, None, ALU.mult))
                dve.wait_ge(loaded, 16)
                c.restart()

                def hot(lo, hi, t, k):
                    nc.vector.tensor_tensor(hot_lo[k][:, :, :], iota_row[0:EP, :].unsqueeze(1).to_broadcast([EP, CH, 128]),
                                            lo[:, cols(t)].unsqueeze(2).to_broadcast([EP, CH, 128]), ALU.is_equal)
                    nc.vector.tensor_tensor(hot_hi[k][:, :, :], iota_row[0:EP, 0:NB].unsqueeze(1).to_broadcast([EP, CH, NB]),
                                            hi[:, cols(t)].unsqueeze(2).to_broadcast([EP, CH, NB]), ALU.is_equal).then_inc(hots, 1)

                def prefix(q, first, last, has, base):
                    dve.wait_ge(counted, (q + 1) * (2 * PAIRS + 1))
                    c.step(nc.vector.tensor_copy(counts[:, :], cnt_ps[q][:, :]))
                    dve.sem_inc(copied, 1)
                    dve.wait_ge(summed, q + 1)
                    c.step(nc.vector.tensor_copy(block_tot[:, :], tot_ps[:, :]))
                    c.link(nc.vector.memset(start_of[:, 0:1], 0.0))
                    c.step(nc.vector.tensor_tensor_scan(start_of[:, 1:NB], ones[:, 0:NB - 1], block_tot[:, 0:NB - 1], 0.0, ALU.mult, ALU.add))
                    c.step(nc.vector.tensor_tensor(start_of[:, :], start_of[:, :], pre_ps[:, :], ALU.add))
                    c.step(nc.vector.scalar_tensor_tensor(end_f[:, :], start_of[:, :], -1.0, counts[:, :], ALU.add, ALU.add))
                    c.step(nc.vector.tensor_scalar(end_f[:, :], end_f[:, :], 0.0, None, ALU.max))
                    c.link(nc.vector.tensor_copy(last[:, :], end_f[:, :]))
                    if base is not None:
                        c.link(nc.vector.tensor_copy(base[:, :], start_of[:, :]))
                    c.step(nc.vector.tensor_scalar(has[:, :], counts[:, :], 0.0, None, ALU.is_gt))
                    c.step(nc.vector.scalar_tensor_tensor(start_of[:, :], start_of[:, :], -float(EDGES), has[:, :], ALU.add, ALU.mult))
                    c.step(nc.vector.tensor_scalar(start_of[:, :], start_of[:, :], float(EDGES), None, ALU.add))
                    c.step(nc.vector.tensor_scalar(end_f[:, :], has[:, :], -1.0, 1.0, ALU.mult, ALU.add))
                    c.step(nc.vector.scalar_tensor_tensor(start_of[:, :], end_f[:, :], lane[:, 0:1], start_of[:, :], ALU.mult, ALU.add))
                    c.step(nc.vector.tensor_copy(first[:, :], start_of[:, :]))
                    dve.sem_inc(starts, 1)
                    c.restart()

                def count_dst(i):
                    for k in range(2):
                        t = 2 * i + k
                        K.wait(dve, "dve", counted, t - 1)
                        hot(lo_d, hi_d, t, k)
                pairs(dve, count_dst)
                prefix(0, first_dst, last_dst, has_dst, None)
                dve.wait_ge(placed, ev.PLACED)
                for ins in ev.start():
                    c.link(ins)
                c.restart()

                def body(i):
                    for k in range(2):
                        t = 2 * i + k
                        K.wait(dve, "dve", counted, t + 2 * PAIRS)
                        hot(lo_s, hi_s, t, k)
                        ev.scan(dve, c, t, k)
                        K.wait(dve, "dve", back_in[k], i * 16 + 16)
                        c.step(nc.vector.tensor_tensor(zw[:, :, :], en_back[k][:, :, :], ev.rows(k), ALU.add))
                        c.step(nc.vector.scalar_tensor_tensor(zw[:, :, :], zw[:, :, :], 0.2, zw[:, :, :], ALU.mult, ALU.max))
                        c.step(nc.vector.tensor_tensor(zw[:, :, :], zw[:, :, :], attn[:, :].unsqueeze(1).to_broadcast([EP, CH, 64]), ALU.mult))
                        nc.vector.tensor_reduce(alpha[:, :, cols(t)].rearrange("p h c -> p c h"),
                                                zw[:, :, :].rearrange("p c (h f) -> p c h f", h=HEADS0), AX.X, ALU.add).then_inc(scored, 1)
                        K.wait(dve, "dve", scored, t + 1)
                        c.restart()
                pairs(dve, body)
                prefix(1, first_src, last_src, has_src, base_src)
        fd_stack.close()
        K.recycle()

        segment_softmax(alpha, HEADS0, 1e-9)

        with ExitStack() as st:
            en = [sb(st, f"en{k}", [EP, CH, 64]) for k in range(2)]
            r = [sb(st, f"r{k}", [EP, CH, 64]) for k in range(2)]
            z = [sb(st, f"z{k}", [EP, CH, 64]) for k in range(2)]
            top_z = sb(st, "top_z", [EP, CH, HEADS0])
            hot_lo = [sb(st, f"hot_lo{k}", [EP, CH, 128], BF16) for k in range(2)]
            hot_hi = [sb(st, f"hot_hi{k}", [EP, CH, NB], BF16) for k in range(2)]
            hot_t = [sb(st, f"hot_t{k}", [NP, GR, EP]) for k in range(2)]
            hot_tb = [sb(st, f"hot_tb{k}", [NP, GR, EP], BF16) for k in range(2)]
            place_sb = [sb(st, f"place_sb{k}", [NP, NB]) for k in range(2)]
            own_same = [sb(st, f"own_same{k}", [EP, GR, EP], BF16) for k in range(2)]
            cross_same = [sb(st, f"cross_same{k}", [EP, 2, 3 * EP], BF16) for k in range(2)]
            picked = sb(st, "picked", [EP, NB])
            pos = [sb(st, f"pos{k}", [EP, CH]) for k in range(2)]
            pos_i = [sb(st, f"pos_i{k}", [EP, CH], I32) for k in range(2)]
            ends = [sb(st, f"ends{k}", [EP, CH, 2], I32) for k in range(2)]
            place_ps = ps(st, "place_ps", [NP, NB])
            turn_ps = [ps(st, f"turn_ps{k}", [NP, GR, 128], BF16) for k in range(2)]
            own_ps = ps(st, "own_ps", [EP, GR, EP])
            cross_ps = ps(st, "cross_ps", [EP, 2, 512])
            rank_ps = [ps(st, f"rank_ps{k}", [EP, GR, NB]) for k in range(2)]
            S = SegmentSums(st, FEAT, sums)
            rows_in = [K.sem(f"rows_in{k}") for k in range(2)]
            sent = [K.own(f"sent{k}") for k in range(2)]
            (scaled, exped, multiplied, hots, turned, turned_sb, samed, copied_same, masked, ranked, selected, placed, place_out, posed,
             chain_v) = (K.sem(n) for n in (
                 "scaled", "exped", "multiplied", "hots", "turned", "turned_sb", "samed", "copied_same", "masked", "ranked",
                 "selected", "placed", "place_out", "posed", "chain_v"))
            block = st.enter_context(nc.Block())
            last_group = GROUPS * 2 * PAIRS

            def cross(a, b):
                return (0, (b - 1) * EP) if a == 0 else (1, (b - 2 if a == 1 else 2) * EP)

            @block.sync
            def _(sp):
                def body(i):
                    for k in range(2):
                        t = 2 * i + k
                        K.wait(sp, "sp", multiplied, t - 1)
                        sp.dma_start(en[k][:, :, :], edge_rows(en_rows)[:, cols(t), :]).then_inc(rows_in[k], 16)
                        sp.dma_start(r[k][:, :, :], edge_rows(A["edge_attr3_2x32"])[:, cols(t), :, :].rearrange("p c h f -> p c (h f)")).then_inc(rows_in[k], 16)
                pairs(sp, body)

            @block.gpsimd
            def _(pool):
                def body(i):
                    for k in range(2):
                        t = 2 * i + k
                        K.wait(pool, "pool", posed, t + 1)
                        for g in range(CH):
                            pool.indirect_dma_start(by_src, bass.IndirectOffsetOnAxis(ap=pos_i[k][:, g:g + 1], axis=0),
                                                    ends[k][:, g, :], None).then_inc(sent[k], 16)
                pairs(pool, body)
                for k in range(2):
                    pool.wait_ge(sent[k], 16 * CH * PAIRS)

            @block.tensor
            def _(pe):
                def turn(n, k, q, s):
                    K.wait(pe, "pe", turned_sb, n - 1)
                    for g in range(GR):
                        last = nc.tensor.transpose(turn_ps[s][:, g, 0:EP], hot_lo[k][:, q * GR + g, :], identb[0:EP, 0:EP])
                    last.then_inc(turned, 1)

                def body(i):
                    for k in range(2):
                        for q in range(GROUPS):
                            t = 2 * i + k
                            n, s = t * GROUPS + q, q % 2
                            if q < GROUPS - 1:
                                turn(n + 1, k, q + 1, 1 - s)
                            elif not known_ge(t, 2 * PAIRS - 1):
                                K.wait(pe, "pe", hots, t + 2)
                                K.wait(pe, "pe", turned_sb, n)
                                for g in range(GR):
                                    last = nc.tensor.transpose(turn_ps[1 - s][:, g, 0:EP], hot_lo[1 - k][:, g, :], identb[0:EP, 0:EP])
                                last.then_inc(turned, 1)
                            K.wait(pe, "pe", turned_sb, n + 1)
                            K.wait(pe, "pe", masked, n)
                            K.wait(pe, "pe", copied_same, n)
                            for a in range(GR):
                                last = nc.tensor.matmul(own_ps[:, a, :], hot_tb[s][:, a, :], hot_tb[s][:, a, :], start=True, stop=True)
                            for a in range(GR - 1):
                                bank, at = cross(a, a + 1)
                                later = hot_tb[s][:, a + 1:GR, :].rearrange("p c e -> p (c e)")
                                last = nc.tensor.matmul(cross_ps[:, bank, at:at + (GR - 1 - a) * EP], hot_tb[s][:, a, :], later, start=True, stop=True)
                            last.then_inc(samed, 1)
                            K.wait(pe, "pe", place_out, n + 1)
                            nc.tensor.matmul(place_ps[:, :], ident[:, :], place_sb[s][:, :], start=True, stop=False)
                            for g in range(GR):
                                last = nc.tensor.matmul(place_ps[:, :], hot_lo[k][:, q * GR + g, :], hot_hi[k][:, q * GR + g, :],
                                                        start=False, stop=g == GR - 1)
                            last.then_inc(placed, 1)
                            K.wait(pe, "pe", selected, n - 1)
                            K.wait(pe, "pe", masked, n + 1)
                            K.wait(pe, "pe", copied_same, n + 1)
                            for b in range(GR):
                                o = rank_ps[s][:, b, :]
                                nc.tensor.matmul(o, hot_t[s][:, b, :], place_sb[s][:, :], start=True, stop=False)
                                for a in range(b):
                                    bank, at = cross(a, b)
                                    nc.tensor.matmul(o, cross_same[s][:, bank, at:at + EP], hot_hi[k][:, q * GR + a, :], start=False, stop=False)
                                last = nc.tensor.matmul(o, own_same[s][:, b, :], hot_hi[k][:, q * GR + b, :], start=False, stop=True)
                            last.then_inc(ranked, 1)
                K.wait(pe, "pe", hots, 1)
                for g in range(GR):
                    last = nc.tensor.transpose(turn_ps[0][:, g, 0:EP], hot_lo[0][:, g, :], identb[0:EP, 0:EP])
                last.then_inc(turned, 1)
                pairs(pe, body, ahead=True)

            @block.scalar
            def _(act):
                nc.scalar.copy(place_sb[0][:, :], base_src[:, :]).then_inc(place_out, 1)

                def take_turned(n, s):
                    K.wait(act, "act", turned, n + 1)
                    K.wait(act, "act", ranked, n - 1)
                    nc.scalar.copy(hot_tb[s][:, :, :], turn_ps[s][:, :, 0:EP])
                    nc.scalar.copy(hot_t[s][:, :, :], turn_ps[s][:, :, 0:EP]).then_inc(turned_sb, 1)

                def body(i):
                    for k in range(2):
                        t = 2 * i + k
                        S.mask(act, t, k)
                        for q in range(GROUPS):
                            n, s = t * GROUPS + q, q % 2
                            if q < GROUPS - 1 or not known_ge(t, 2 * PAIRS - 1):
                                take_turned(n + 1, 1 - s)
                            K.wait(act, "act", samed, n + 1)
                            K.wait(act, "act", ranked, n - 1)
                            nc.scalar.copy(cross_same[s][:, :, :], cross_ps[:, :, 0:3 * EP]).then_inc(copied_same, 1)
                            K.wait(act, "act", placed, n + 1)
                            K.wait(act, "act", ranked, n)
                            nc.scalar.copy(place_sb[1 - s][:, :], place_ps[:, :]).then_inc(place_out, 1)
                            if q == 1:
                                K.wait(act, "act", scaled, t + 1)
                                nc.scalar.activation(z[k][:, :, :], z[k][:, :, :], ACT.Exp).then_inc(exped, 1)
                        if not first_chunk(t):
                            S.store(act, t - 1, 1 - k, i - 1 + k)
                take_turned(0, 0)
                pairs(act, body, ahead=True)
                S.store(act, 2 * PAIRS - 1, 1, PAIRS - 1)
                S.finish(act)

            @block.vector
            def _(dve):
                c = Chain(dve, chain_v)
                for ins in S.start():
                    c.link(ins)
                c.restart()

                def per_head(ap):
                    return ap.unsqueeze(3).to_broadcast([EP, CH, HEADS0, FEAT])

                def hot(t, k):
                    K.wait(dve, "dve", ranked, (t - 1) * GROUPS)
                    nc.vector.tensor_tensor(hot_lo[k][:, :, :], iota_row[0:EP, :].unsqueeze(1).to_broadcast([EP, CH, 128]),
                                            lo_s[:, cols(t)].unsqueeze(2).to_broadcast([EP, CH, 128]), ALU.is_equal)
                    nc.vector.tensor_tensor(hot_hi[k][:, :, :], iota_row[0:EP, 0:NB].unsqueeze(1).to_broadcast([EP, CH, NB]),
                                            hi_s[:, cols(t)].unsqueeze(2).to_broadcast([EP, CH, NB]), ALU.is_equal).then_inc(hots, 1)

                def mask(n, s):
                    K.wait(dve, "dve", samed, n + 1)
                    K.wait(dve, "dve", ranked, n - 1)
                    tri = before[0:EP, 0:EP].unsqueeze(1).to_broadcast([EP, GR, EP])
                    nc.vector.tensor_tensor(own_same[s][:, :, :], own_ps[:, :, :], tri, ALU.mult).then_inc(masked, 1)

                def pick(n, k, q, s):
                    K.wait(dve, "dve", ranked, n + 1)
                    for g in range(GR):
                        at = q * GR + g
                        c.step(nc.vector.scalar_tensor_tensor(picked[:, :], rank_ps[s][:, g, :], 1.0, hot_hi[k][:, at, :], ALU.mult, ALU.mult,
                                                              accum_out=pos[k][:, at:at + 1]))
                    dve.sem_inc(selected, 1)

                def send(t, k, i):
                    K.wait(dve, "dve", sent[k], i * (16 * CH))
                    c.link(nc.vector.tensor_copy(ends[k][:, :, 0], src_i[:, cols(t)]))
                    c.link(nc.vector.tensor_copy(ends[k][:, :, 1], dst_i[:, cols(t)]))
                    c.step(nc.vector.tensor_copy(pos_i[k][:, :], pos[k][:, :]))
                    dve.sem_inc(posed, 1)

                def body(i):
                    for k in range(2):
                        t = 2 * i + k
                        z4 = z[k][:, :, :].rearrange("p c (h f) -> p c h f", h=HEADS0)
                        n = t * GROUPS
                        mask(n, 0)
                        K.wait(dve, "dve", rows_in[k], i * 32 + 32)
                        c.step(nc.vector.tensor_tensor(z[k][:, :, :], en[k][:, :, :], r[k][:, :, :], ALU.mult))
                        if not first_chunk(t):
                            pick(n - 1, 1 - k, GROUPS - 1, 1)
                            send(t - 1, 1 - k, i - 1 + k)
                        nc.vector.tensor_tensor(z4, z4, per_head(alpha[:, :, cols(t)].rearrange("p h c -> p c h")), ALU.mult).then_inc(multiplied, 1)
                        if not known_ge(t, 2 * PAIRS - 1):
                            hot(t + 1, 1 - k)
                        mask(n + 1, 1)
                        K.wait(dve, "dve", multiplied, t + 1)
                        c.step(nc.vector.tensor_reduce(top_z[:, :, :], z4, AX.X, ALU.max))
                        nc.vector.tensor_tensor(z4, z4, per_head(top_z[:, :, :]), ALU.subtract).then_inc(scaled, 1)
                        pick(n, k, 0, 0)
                        mask(n + 2, 0)
                        pick(n + 1, k, 1, 1)
                        mask(n + 3, 1)
                        K.wait(dve, "dve", exped, t + 1)
                        c.step(nc.vector.tensor_reduce(top_z[:, :, :], z4, AX.X, ALU.add))
                        c.step(nc.vector.reciprocal(top_z[:, :, :], top_z[:, :, :]))
                        c.step(nc.vector.tensor_tensor(z4, z4, per_head(top_z[:, :, :]), ALU.mult))
                        pick(n + 2, k, 2, 0)
                        c.link(nc.vector.tensor_tensor(S.message(k), z[k][:, :, 0:FEAT].rearrange("p c f -> p f c"),
                                                       z[k][:, :, FEAT:2 * FEAT].rearrange("p c f -> p f c"), ALU.add))
                        S.scan(dve, c, t, k)
                        c.restart()
                hot(0, 0)
                pairs(dve, body, ahead=True)
                pick(last_group - 1, 1, GROUPS - 1, 1)
                send(2 * PAIRS - 1, 1, PAIRS - 1)
                c.restart()
        K.recycle()
        e0.close()
        agg = sb(top, "agg", [NP, NB, FEAT])

        segment_ends(sums, FEAT, last_dst, agg)
        with ExitStack() as st:
            w = sb(st, "w1", [FEAT, FEAT])
            bias = sb(st, "b1", [NP, FEAT])
            load([(w[:, :], A["L0_gnn_W1"]), (bias[:, :], on_all(A["L0_gnn_b1"]))])
            chain_v = K.sem("chain_v")
            with nc.Block() as block:
                @block.vector
                def _(dve):
                    c = Chain(dve, chain_v)
                    c.step(nc.vector.tensor_tensor(agg[:, :, :], agg[:, :, :], has_dst[:, :].unsqueeze(2).to_broadcast([NP, NB, FEAT]), ALU.mult))
                    c.link(nc.vector.tensor_tensor(agg[:, :, :], agg[:, :, :], h[:, :, :], ALU.add))
                    c.link(nc.vector.tensor_tensor(x[:, :, :], x[:, :, :], bias[:, :].unsqueeze(1).to_broadcast([NP, NB, FEAT]), ALU.add))
                    c.restart()
            K.recycle()

            def put(dve, views, g):
                for j, m, v in views:
                    xs = x[:, bass.ds(g * NG + j, m), :]
                    last = nc.vector.tensor_tensor(xs, xs, v, ALU.add)
                return last
            node_product(agg, FEAT, w[:, :], FEAT, put)

        normalize()
        store_table([(node_rows(tab_h), h[:, :, :])])

        def gather_rows(st):
            idx = [sb(st, f"idx{k}", [EP, CH], I32) for k in range(2)]
            rows = [sb(st, f"hs{k}", [EP, CH, FEAT]) for k in range(2)]
            idx_in = [K.sem(f"idx_in{k}") for k in range(2)]
            gathered = [K.own(f"gathered{k}") for k in range(2)]

            def load_idx(sp, t, k, i):
                K.wait(sp, "sp", gathered[k], i * (16 * CH))
                sp.dma_start(idx[k][:, :], edge_rows(A["src"])[:, cols(t)]).then_inc(idx_in[k], 16)

            def gather(pool, t, k, i):
                K.wait(pool, "pool", idx_in[k], i * 16 + 16)
                for g in range(CH):
                    pool.indirect_dma_start(rows[k][:, g, :], None, tab_h,
                                            bass.IndirectOffsetOnAxis(ap=idx[k][:, g:g + 1], axis=0)).then_inc(gathered[k], 16)
            return rows, gathered, load_idx, gather

        with ExitStack() as st:
            rows, gathered, load_idx, gather = gather_rows(st)
            S = SegmentSums(st, FEAT, sums)
            laid, started, chain_v = K.sem("laid"), K.sem("started"), K.sem("chain_v")
            block = st.enter_context(nc.Block())

            @block.sync
            def _(sp):
                def body(i):
                    for k in range(2):
                        load_idx(sp, 2 * i + k, k, i)
                pairs(sp, body)

            @block.gpsimd
            def _(pool):
                def body(i):
                    for k in range(2):
                        t = 2 * i + k
                        K.wait(pool, "pool", laid, t - 1)
                        gather(pool, t, k, i)
                pairs(pool, body)

            @block.scalar
            def _(act):
                def body(i):
                    for k in range(2):
                        t = 2 * i + k
                        S.mask(act, t, k)
                        K.wait(act, "act", gathered[k], (i + 1) * (16 * CH))
                        nc.scalar.copy(S.message(k), rows[k][:, :, :].rearrange("p c f -> p f c")).then_inc(laid, 1)
                        S.store(act, t, k, i)
                pairs(act, body)
                S.finish(act)

            @block.vector
            def _(dve):
                c = Chain(dve, chain_v)
                for ins in S.start():
                    c.link(ins)
                c.restart()

                def body(i):
                    for k in range(2):
                        t = 2 * i + k
                        K.wait(dve, "dve", laid, t + 1)
                        S.scan(dve, c, t, k)
                        c.restart()
                pairs(dve, body)
        K.recycle()
        segment_ends(sums, FEAT, last_dst, agg)
        masked_add(has_dst, 1.0)

        normalize()
        store_table([(node_rows(tab_h), h[:, :, :])])
        MUL, HID, TPW = 8, 64, 256
        with ExitStack() as st:
            w1 = sb(st, "w1_pairs", [128, CH // 2, 128])
            w2 = sb(st, "w2_pair", [128, 128])
            w3 = sb(st, "w3_pair", [128, 2, TPW])
            b1 = sb(st, "b1_pair", [128, 1])
            b2 = sb(st, "b2_pair", [128, 1])
            b3 = sb(st, "b3", [1, TPW])
            b3_part = [sb(st, f"b3_part{n}", [1, TPW], BF16) for n in range(3)]
            b3_rest = sb(st, "b3_rest", [1, TPW])
            b3_rows = sb(st, "b3_rows", [3, 2, TPW], BF16)
            ones_b = sb(st, "ones_b", [3, EP], BF16)
            zero = [w1, w2, w3]
            loaded, zeroed, split, chain_v = K.sem("loaded"), K.sem("zeroed"), K.sem("split"), K.sem("chain_v")
            with nc.Block() as block:
                @block.vector
                def _(dve):
                    c = Chain(dve, chain_v)
                    nc.vector.memset(w1[:, :, :], 0.0).then_inc(zeroed, 1)
                    nc.vector.memset(w2[:, :], 0.0).then_inc(zeroed, 1)
                    nc.vector.memset(w3[:, :, :], 0.0).then_inc(zeroed, 1)
                    nc.vector.memset(ones_b[:, :], 1.0)
                    dve.wait_ge(loaded, 16)
                    c.step(nc.vector.tensor_scalar(b3[:, 64:128], b3[:, 64:128], 3.0 ** -0.5, None, ALU.mult))
                    c.step(nc.vector.tensor_copy(b3_part[0][:, :], b3[:, :]))
                    c.step(nc.vector.tensor_tensor(b3_rest[:, :], b3[:, :], b3_part[0][:, :], ALU.subtract))
                    c.step(nc.vector.tensor_copy(b3_part[1][:, :], b3_rest[:, :]))
                    c.step(nc.vector.tensor_tensor(b3_rest[:, :], b3_rest[:, :], b3_part[1][:, :], ALU.subtract))
                    c.step(nc.vector.tensor_copy(b3_part[2][:, :], b3_rest[:, :]))
                    dve.sem_inc(split, 1)
                    c.restart()

                @block.sync
                def _(sp):
                    sp.dma_start(b3[:, :], A["L2_gnn_b3"].unsqueeze(0)).then_inc(loaded, 16)
                    sp.wait_ge(zeroed, 3)
                    sp.wait_ge(loaded, 16)
                    n = 1
                    for c_ in range(CH):
                        o = (c_ % 2) * HID
                        sp.dma_start(w1[c_ * MUL:(c_ + 1) * MUL, c_ // 2, o:o + HID], A["L2_gnn_W1"]).then_inc(loaded, 16)
                        n += 1
                    for o in range(2):
                        at = slice(o * HID, (o + 1) * HID)
                        sp.dma_start(w2[at, at], A["L2_gnn_W2"]).then_inc(loaded, 16)
                        sp.dma_start(w3[at, o, :], A["L2_gnn_W3"]).then_inc(loaded, 16)
                        sp.dma_start(b1[at, :], A["L2_gnn_b1"].unsqueeze(1)).then_inc(loaded, 16)
                        sp.dma_start(b2[at, :], A["L2_gnn_b2"].unsqueeze(1)).then_inc(loaded, 16)
                        n += 4
                    sp.wait_ge(split, 1)
                    for m in range(3):
                        for o in range(2):
                            sp.dma_start(b3_rows[m:m + 1, o, :], b3_part[m][:, :]).then_inc(loaded, 16)
                            n += 1
                    sp.wait_ge(loaded, 16 * n)
            K.recycle()
            with nc.Block() as block:
                @block.vector
                def _(dve):
                    nc.vector.tensor_scalar(w3[:, :, 64:128], w3[:, :, 64:128], 3.0 ** -0.5, None, ALU.mult)

            rows, gathered, load_idx, gather = gather_rows(st)
            S = SegmentSums(st, FEAT, sums)
            radial = [sb(st, f"radial{k}", [EP, CH * MUL]) for k in range(2)]
            sh = [sb(st, f"sh{k}", [EP, CH, 4]) for k in range(2)]
            radial_t = sb(st, "radial_t", [128, EP])
            x1 = sb(st, "x1", [128, 2, 4 * EP])
            x2 = [sb(st, f"x2_{k}", [128, 2, 4 * EP]) for k in range(2)]
            hv1 = sb(st, "hv1", [EP, CH, MUL, 3])
            zz = [sb(st, f"zz{k}", [EP, CH, 3, MUL]) for k in range(2)]
            zv = [sb(st, f"zv{k}", [EP, CH, 3, MUL]) for k in range(2)]
            zv_wide = [sb(st, f"zv_wide{k}", [EP, CH, 3, MUL, MUL]) for k in range(2)]
            prod_a = [sb(st, f"prod_a{k}", [EP, 4, MUL, 3, MUL]) for k in range(2)]
            prod_b = [sb(st, f"prod_b{k}", [EP, 4, 3, MUL, MUL]) for k in range(2)]
            res_a = sb(st, "res_a", [EP, CH, MUL, 3])
            res_b = sb(st, "res_b", [EP, CH, 3, MUL])
            cross = sb(st, "cross", [EP, CH, MUL, 3])
            radial_ps = ps(st, "radial_ps", [128, EP])
            hid_ps = ps(st, "hid_ps", [128, 2, 512])
            tp_ps = [ps(st, f"tp_ps{k}", [EP, 2, 512]) for k in range(2)]
            attr_in = [K.sem(f"attr_in{k}") for k in range(2)]
            (turned, turned_sb, hid1, act1, hid2, act2, tpw, taken, chain_v, used, scaled, widened) = (
                K.sem(n) for n in ("turned", "turned_sb", "hid1", "act1", "hid2", "act2", "tpw", "taken", "chain_v", "used", "scaled", "widened"))
            block = st.enter_context(nc.Block())

            @block.sync
            def _(sp):
                def body(i):
                    for k in range(2):
                        t = 2 * i + k
                        load_idx(sp, t, k, i)
                        K.wait(sp, "sp", used, t - 1)
                        K.wait(sp, "sp", turned, t - 1)
                        sp.dma_start(radial[k][:, :], edge_rows(A["edge_attr_8"])[:, cols(t), :].rearrange("p c f -> p (c f)")).then_inc(attr_in[k], 16)
                        sp.dma_start(sh[k][:, :, :], edge_rows(A["edge_attr_4"])[:, cols(t), :]).then_inc(attr_in[k], 16)
                pairs(sp, body)

            @block.gpsimd
            def _(pool):
                def body(i):
                    for k in range(2):
                        t = 2 * i + k
                        K.wait(pool, "pool", used, t - 1)
                        gather(pool, t, k, i)
                pairs(pool, body)

            @block.tensor
            def _(pe):
                def turn(t, k, i):
                    K.wait(pe, "pe", attr_in[k], i * 32 + 32)
                    K.wait(pe, "pe", turned_sb, t)
                    nc.tensor.transpose(radial_ps[:, :], radial[k][:, :], ident[0:EP, 0:EP]).then_inc(turned, 1)

                def hidden1(t):
                    K.wait(pe, "pe", turned_sb, t + 1)
                    K.wait(pe, "pe", act2, 2 * t)
                    for a in range(2):
                        for b in range(4):
                            last = nc.tensor.matmul(hid_ps[:, a, b * EP:(b + 1) * EP], w1[:, a * 4 + b, :], radial_t[:, :], start=True, stop=True)
                        last.then_inc(hid1, 1)

                def hidden2(t, a):
                    K.wait(pe, "pe", act1, 2 * t + a + 1)
                    nc.tensor.matmul(hid_ps[:, a, 0:4 * EP], w2[:, :], x1[:, a, :], start=True, stop=True).then_inc(hid2, 1)

                def products(t, k, q):
                    a = q // 2
                    if q % 2 == 0:
                        K.wait(pe, "pe", act2, 2 * t + a + 1)
                    K.wait(pe, "pe", taken, 4 * t + q - 1)
                    for j in range(2):
                        b = (q % 2) * 2 + j
                        o = tp_ps[q % 2][:, j, :]
                        nc.tensor.matmul(o, x2[k][:, a, b * EP:(b + 1) * EP], w3[:, :, :].rearrange("p o n -> p (o n)"), start=True, stop=False)
                        last = nc.tensor.matmul(o, ones_b[:, :], b3_rows[:, :, :].rearrange("p o n -> p (o n)"), start=False, stop=True)
                    last.then_inc(tpw, 1)

                turn(0, 0, 0)
                hidden1(0)
                hidden2(0, 0)
                hidden2(0, 1)

                def body(i):
                    for k in range(2):
                        t = 2 * i + k
                        more = not known_ge(t, 2 * PAIRS - 1)
                        if more:
                            turn(t + 1, 1 - k, i + k)
                        products(t, k, 0)
                        products(t, k, 1)
                        products(t, k, 2)
                        if more:
                            hidden1(t + 1)
                        products(t, k, 3)
                        if more:
                            hidden2(t + 1, 0)
                            hidden2(t + 1, 1)
                pairs(pe, body, ahead=True)

            @block.scalar
            def _(act):
                def take_turned(t):
                    K.wait(act, "act", turned, t + 1)
                    K.wait(act, "act", hid1, 2 * t)
                    nc.scalar.copy(radial_t[:, :], radial_ps[:, :]).then_inc(turned_sb, 1)

                def layer1(t):
                    for a in range(2):
                        K.wait(act, "act", hid1, 2 * t + a + 1)
                        K.wait(act, "act", hid2, 2 * t + a - 1)
                        nc.scalar.activation(x1[:, a, :], hid_ps[:, a, 0:4 * EP], ACT.Silu, bias=b1[:, 0:1]).then_inc(act1, 1)

                def layer2(t, k):
                    for a in range(2):
                        K.wait(act, "act", hid2, 2 * t + a + 1)
                        K.wait(act, "act", tpw, 4 * (t - 1))
                        nc.scalar.activation(x2[k][:, a, :], hid_ps[:, a, 0:4 * EP], ACT.Silu, bias=b2[:, 0:1]).then_inc(act2, 1)
                take_turned(0)
                layer1(0)
                layer2(0, 0)

                def body(i):
                    for k in range(2):
                        t = 2 * i + k
                        more = not known_ge(t, 2 * PAIRS - 1)
                        K.wait(act, "act", gathered[k], (i + 1) * (16 * CH))
                        K.wait(act, "act", used, t - 1)
                        nc.scalar.copy(zz[k][:, :, 2, :], rows[k][:, :, 0:MUL])
                        K.wait(act, "act", scaled, t + 1)
                        nc.scalar.copy(zv_wide[k][:, :, :, :, :].rearrange("p c i u w -> p (c i u) w"),
                                       zv[k][:, :, :, :].rearrange("p c i u -> p (c i u)").unsqueeze(2).to_broadcast([EP, CH * 3 * MUL, MUL])).then_inc(widened, 1)
                        S.mask(act, t, k)
                        if more:
                            take_turned(t + 1)
                        if not first_chunk(t):
                            S.store(act, t - 1, 1 - k, i - 1 + k)
                        if more:
                            layer1(t + 1)
                            layer2(t + 1, 1 - k)
                pairs(act, body, ahead=True)
                S.store(act, 2 * PAIRS - 1, 1, PAIRS - 1)
                S.finish(act)

            @block.vector
            def _(dve):
                c = Chain(dve, chain_v)
                for ins in S.start():
                    c.link(ins)
                c.restart()

                def body(i):
                    for k in range(2):
                        t = 2 * i + k
                        K.wait(dve, "dve", gathered[k], (i + 1) * (16 * CH))
                        K.wait(dve, "dve", attr_in[k], i * 32 + 32)
                        hs = rows[k][:, :, 0:MUL]
                        hv = rows[k][:, :, MUL:FEAT].rearrange("p c (u i) -> p c u i", i=3)
                        sh0 = sh[k][:, :, 0:1]
                        sh1 = sh[k][:, :, 1:4].unsqueeze(2).to_broadcast([EP, CH, MUL, 3])
                        K.wait(dve, "dve", widened, t - 1)
                        nc.vector.tensor_tensor(zv[k][:, :, :, :], hv.rearrange("p c u i -> p c i u"),
                                                sh0.unsqueeze(3).to_broadcast([EP, CH, 3, MUL]), ALU.mult).then_inc(scaled, 1)
                        c.link(nc.vector.tensor_tensor(hv1[:, :, :, :], hv, sh1, ALU.mult))
                        c.step(nc.vector.tensor_tensor(zz[k][:, :, 0, :], hs, sh0.to_broadcast([EP, CH, MUL]), ALU.mult))
                        c.step(nc.vector.tensor_reduce(zz[k][:, :, 1, :], hv1[:, :, :, :], AX.X, ALU.add))
                        K.wait(dve, "dve", widened, t + 1)

                        def total(q, done):
                            dve.wait_ge(chain_v, done)
                            dve.sem_inc(taken, 1)
                            four = slice(4 * q, 4 * q + 4)
                            c.link(nc.vector.tensor_reduce(res_a[:, four, :, :].rearrange("p c w b -> p (c w b)"),
                                                           prod_a[q % 2][:, :, :, :, :].rearrange("p c w b u -> p (c w b) u"), AX.X, ALU.add))
                            c.link(nc.vector.tensor_reduce(res_b[:, four, :, :].rearrange("p c i w -> p (c i) w"),
                                                           prod_b[q % 2][:, :, :, :, :].rearrange("p c i u w -> p (c i) w u"), AX.X, ALU.add))
                        done = 0
                        for q in range(4):
                            K.wait(dve, "dve", tpw, 4 * t + q + 1)
                            four = slice(4 * q, 4 * q + 4)
                            wts = tp_ps[q % 2][:, :, :].rearrange("p j (o n) -> p (j o) n", o=2)
                            shape = [EP, 4, MUL, 3 * MUL]
                            if q >= 2:
                                dve.wait_ge(chain_v, summed)
                            c.link(nc.vector.tensor_tensor(prod_a[q % 2][:, :, :, :, :].rearrange("p c w b u -> p c w (b u)"),
                                                           wts[:, :, 0:192].rearrange("p c (n w) -> p c w n", w=MUL),
                                                           zz[k][:, four, :, :].rearrange("p c b u -> p c (b u)").unsqueeze(2).to_broadcast(shape), ALU.mult))
                            c.link(nc.vector.tensor_tensor(prod_b[q % 2][:, :, :, :, :].rearrange("p c i u w -> p c i (u w)"),
                                                           wts[:, :, 192:256].unsqueeze(2).to_broadcast([EP, 4, 3, MUL * MUL]),
                                                           zv_wide[k][:, four, :, :, :].rearrange("p c i u w -> p c i (u w)"), ALU.mult))
                            made = c.n
                            if q:
                                total(q - 1, done)
                                summed = c.n
                            done = made
                        total(3, done)
                        c.join()
                        msg = S.message(k)
                        c.link(nc.vector.tensor_tensor(msg[:, 0:MUL, :], res_a[:, :, :, 0].rearrange("p c w -> p w c"),
                                                       res_a[:, :, :, 1].rearrange("p c w -> p w c"), ALU.add))
                        c.step(nc.vector.tensor_tensor(cross[:, :, :, :], sh1, res_a[:, :, :, 2].unsqueeze(3).to_broadcast([EP, CH, MUL, 3]), ALU.mult))
                        dve.sem_inc(used, 1)
                        c.link(nc.vector.tensor_tensor(msg[:, MUL:FEAT, :].rearrange("p (w i) c -> p w i c", i=3),
                                                       cross[:, :, :, :].rearrange("p c w i -> p w i c"),
                                                       res_b[:, :, :, :].rearrange("p c i w -> p w i c"), ALU.add))
                        S.scan(dve, c, t, k)
                        c.restart()
                pairs(dve, body)
        K.recycle()
        segment_ends(sums, FEAT, last_dst, agg)
        masked_add(has_dst, 1.0 / 16)
        with ExitStack() as st:
            w = sb(st, "w_self", [FEAT, FEAT])
            zeroed, loaded = K.sem("zeroed"), K.sem("loaded")
            with nc.Block() as block:
                @block.vector
                def _(dve):
                    nc.vector.memset(w[:, :], 0.0).then_inc(zeroed, 1)

                @block.sync
                def _(sp):
                    sp.wait_ge(zeroed, 1)
                    sp.dma_start(w[0:MUL, 0:MUL], A["L2_gnn_Ws"]).then_inc(loaded, 16)
                    for u in range(MUL):
                        for m in range(3):
                            at = MUL + 3 * u + m
                            sp.dma_start(w[at:at + 1, MUL + m:FEAT:3], A["L2_gnn_Wv"][u:u + 1, :], allow_slow_non_contiguous=True).then_inc(loaded, 16)
                    sp.wait_ge(loaded, 16 * (1 + 3 * MUL))
            K.recycle()

            def put(dve, views, g):
                for j, m, v in views:
                    xs = x[:, bass.ds(g * NG + j, m), :]
                    last = nc.vector.scalar_tensor_tensor(xs, v, MUL ** -0.5, xs, ALU.mult, ALU.add)
                return last
            node_product(h, FEAT, w[:, :], FEAT, put)

        normalize()
        a_src = sb(top, "a_src", [NP, NB, HEADS3])
        first_key = sb(top, "first_key", [EP, 1], I32)
        with ExitStack() as st:
            w = sb(st, "w3h", [FEAT, HEADS3, FEAT])
            fc = sb(st, "fc", [FEAT, 2, FEAT])
            part = sb(st, "part", [FEAT, 2, HEADS3, FEAT])
            w_sd = sb(st, "w_sd3", [FEAT, 2, HEADS3])
            h3 = sb(st, "h3", [NP, NB, FEAT + HEADS3])
            load([(w[:, :, :], A["L3_gnn_w"].rearrange("h f o -> f h o")),
                  (fc[:, :, :].rearrange("p s o -> p (s o)"), on_all(A["L3_gnn_fc_w"][0, :], FEAT))])
            chain_v = K.sem("chain_v")
            with nc.Block() as block:
                @block.vector
                def _(dve):
                    c = Chain(dve, chain_v)
                    for s in range(2):
                        c.link(nc.vector.tensor_tensor(part[:, s, :, :], w[:, :, :], fc[:, s, :].unsqueeze(1).to_broadcast([FEAT, HEADS3, FEAT]), ALU.mult))
                    c.join()
                    c.step(nc.vector.tensor_reduce(w_sd[:, :, :], part[:, :, :, :], AX.X, ALU.add))
                    c.restart()
            K.recycle()

            def put(dve, views, g):
                for j, m, v in views:
                    at = bass.ds(g * NG + j, m)
                    nc.vector.tensor_copy(a_src[:, at, :], v[:, :, 0:HEADS3])
                    last = nc.vector.tensor_copy(h3[:, at, FEAT:], v[:, :, HEADS3:])
                return last
            node_product(h, FEAT, w_sd[:, :, :].rearrange("p s h -> p (s h)"), 2 * HEADS3, put)
            with nc.Block() as block:
                @block.vector
                def _(dve):
                    nc.vector.tensor_copy(h3[:, :, 0:FEAT], h[:, :, :])
            store_table([(node_rows(tab_h3), h3[:, :, :]), (node_rows(tab_a3), a_src[:, :, :])])

        with ExitStack() as st:
            key = sb(st, "key_src", [EP, COLS, 2], I32)
            load([(key[:, :, :], edge_rows(by_src)), (first_key[:, :], edge_rows(by_src)[:, 0, 0:1])])
            edge_masks(key[:, :, 0], edge_rows(by_src)[:, 0, 0:1], edge_rows(by_src)[:, COLS - 1, 0:1])

        with ExitStack() as e3:
            att = sb(e3, "att", [EP, HEADS3, COLS])
            fcb = sb(e3, "fcb3", [EP, 1])
            load([(fcb[:, :], on_all(A["L3_gnn_fc_b"], EP))])
            with ExitStack() as st:
                idx = [sb(st, f"idx{k}", [EP, CH, 2], I32) for k in range(2)]
                rows = [sb(st, f"hs{k}", [EP, CH, FEAT + HEADS3]) for k in range(2)]
                own = Spread(st, HEADS3, own_rows)
                placed = K.own("placed")
                score = sb(st, "score", [EP, CH, HEADS3])
                idx_in = [K.sem(f"idx_in{k}") for k in range(2)]
                gathered = [K.own(f"gathered{k}") for k in range(2)]
                stored = [K.sem(f"stored{k}") for k in range(2)]
                scored, chain_v = K.sem("scored"), K.sem("chain_v")
                block = st.enter_context(nc.Block())

                @block.sync
                def _(sp):
                    def body(i):
                        for k in range(2):
                            t = 2 * i + k
                            K.wait(sp, "sp", gathered[k], i * (16 * CH))
                            sp.dma_start(idx[k][:, :, :], edge_rows(by_src)[:, cols(t), :]).then_inc(idx_in[k], 16)
                    pairs(sp, body)

                @block.gpsimd
                def _(pool):
                    own.place(pool, lambda b: a_src[:, b, :], first_src, tab_a3, first_key[:, 0:1], placed)

                    def body(i):
                        for k in range(2):
                            t = 2 * i + k
                            K.wait(pool, "pool", idx_in[k], i * 16 + 16)
                            K.wait(pool, "pool", scored, t - 1)
                            K.wait(pool, "pool", stored[k], i * 16)
                            for g in range(CH):
                                pool.indirect_dma_start(rows[k][:, g, :], None, tab_h3,
                                                        bass.IndirectOffsetOnAxis(ap=idx[k][:, g, 1:2], axis=0)).then_inc(gathered[k], 16)
                    pairs(pool, body)

                @block.scalar
                def _(act):
                    act.wait_ge(placed, own.PLACED)
                    own.load(act, 0, 0)
                    own.load(act, 1, 1)
                    own.lay(act, 0, 0, 0)

                    def body(i):
                        for k in range(2):
                            t = 2 * i + k
                            if not known_ge(t, 2 * PAIRS - 1):
                                own.lay(act, t + 1, 1 - k, i + k)
                            if not known_ge(t, 2 * PAIRS - 2):
                                K.wait(act, "act", own.laid, t + 1)
                                own.load(act, t + 2, k)
                            K.wait(act, "act", gathered[k], (i + 1) * (16 * CH))
                            act.dma_start(edge_rows(h_rows)[:, cols(t), :], rows[k][:, :, 0:FEAT]).then_inc(stored[k], 16)
                    pairs(act, body, ahead=True)
                    for k in range(2):
                        act.wait_ge(stored[k], 16 * PAIRS)

                @block.vector
                def _(dve):
                    c = Chain(dve, chain_v)
                    dve.wait_ge(placed, own.PLACED)
                    for ins in own.start():
                        c.link(ins)
                    c.restart()

                    def body(i):
                        for k in range(2):
                            t = 2 * i + k
                            own.scan(dve, c, t, k)
                            K.wait(dve, "dve", gathered[k], (i + 1) * (16 * CH))
                            c.step(nc.vector.tensor_tensor(score[:, :, :], own.rows(k), rows[k][:, :, FEAT:], ALU.add))
                            c.step(nc.vector.tensor_scalar(score[:, :, :], score[:, :, :], fcb[:, 0:1], None, ALU.add))
                            nc.vector.scalar_tensor_tensor(att[:, :, cols(t)].rearrange("p h c -> p c h"), score[:, :, :], 0.2,
                                                           score[:, :, :], ALU.mult, ALU.max).then_inc(scored, 1)
                            K.wait(dve, "dve", scored, t + 1)
                            c.restart()
                    pairs(dve, body)
            K.recycle()

            segment_softmax(att, HEADS3, 0.0)

            with ExitStack() as st:
                rows = [sb(st, f"hs{k}", [EP, CH, FEAT]) for k in range(2)]
                S = SegmentSums(st, HEADS3 * FEAT, sums3)
                rows_in = [K.sem(f"rows_in{k}") for k in range(2)]
                used, chain_v = K.sem("used"), K.sem("chain_v")
                block = st.enter_context(nc.Block())

                @block.sync
                def _(sp):
                    def body(i):
                        for k in range(2):
                            t = 2 * i + k
                            K.wait(sp, "sp", used, t - 1)
                            sp.dma_start(rows[k][:, :, :], edge_rows(h_rows)[:, cols(t), :]).then_inc(rows_in[k], 16)
                    pairs(sp, body)

                @block.scalar
                def _(act):
                    def body(i):
                        for k in range(2):
                            t = 2 * i + k
                            S.mask(act, t, k)
                            S.store(act, t, k, i)
                    pairs(act, body)
                    S.finish(act)

                @block.vector
                def _(dve):
                    c = Chain(dve, chain_v)
                    for ins in S.start():
                        c.link(ins)
                    c.restart()

                    def body(i):
                        for k in range(2):
                            t = 2 * i + k
                            K.wait(dve, "dve", rows_in[k], i * 16 + 16)
                            shape = [EP, HEADS3, FEAT, CH]
                            c.step(nc.vector.tensor_tensor(S.message(k).rearrange("p (h f) c -> p h f c", h=HEADS3),
                                                           rows[k][:, :, :].rearrange("p c f -> p f c").unsqueeze(1).to_broadcast(shape),
                                                           att[:, :, cols(t)].unsqueeze(2).to_broadcast(shape), ALU.mult))
                            dve.sem_inc(used, 1)
                            S.scan(dve, c, t, k)
                            c.restart()
                    pairs(dve, body)
            K.recycle()

        with ExitStack() as st:
            agg3 = sb(st, "agg3", [NP, NB, HEADS3 * FEAT])
            segment_ends(sums3, HEADS3 * FEAT, last_src, agg3)
            w = sb(st, "w_out", [HEADS3 * FEAT, FEAT])
            bias = sb(st, "b_out", [NP, FEAT])
            load([(w[:, :], A["L3_gnn_w"].rearrange("h f o -> (h f) o")), (bias[:, :], on_all(A["L3_gnn_bias"]))])
            chain_v = K.sem("chain_v")
            with nc.Block() as block:
                @block.vector
                def _(dve):
                    c = Chain(dve, chain_v)
                    wide = [NP, NB, HEADS3 * FEAT]
                    c.link(nc.vector.tensor_tensor(agg3[:, :, :], agg3[:, :, :], has_src[:, :].unsqueeze(2).to_broadcast(wide), ALU.mult))
                    c.link(nc.vector.tensor_tensor(x[:, :, :], x[:, :, :], bias[:, :].unsqueeze(1).to_broadcast([NP, NB, FEAT]), ALU.add))
                    c.restart()
            K.recycle()

            def put(dve, views, g):
                for j, m, v in views:
                    xs = x[:, bass.ds(g * NG + j, m), :]
                    last = nc.vector.scalar_tensor_tensor(xs, v, 1.0 / HEADS3, xs, ALU.mult, ALU.add)
                return last
            node_product(agg3, HEADS3 * FEAT, w[:, :], FEAT, put)
        full = (NB - 1) * NP
        store_table([(out[0:full, :].rearrange("(b l) f -> l b f", l=NP), x[:, 0:NB - 1, :]),
                     (out[full:NODES, :], x[0:TAIL, NB - 1, :])])


_INS = ['x', 'src', 'dst', 'edge_attr3_2x32', 'edge_attr_4', 'edge_attr_8', 'L0_gnn_W1', 'L0_gnn_b1', 'L0_gnn_W2s', 'L0_gnn_b2s',
        'L0_gnn_W2d', 'L0_gnn_b2d', 'L0_gnn_attn', 'L2_gnn_W1', 'L2_gnn_b1', 'L2_gnn_W2', 'L2_gnn_b2', 'L2_gnn_W3', 'L2_gnn_b3',
        'L2_gnn_Ws', 'L2_gnn_Wv', 'L3_gnn_w', 'L3_gnn_fc_w', 'L3_gnn_fc_b', 'L3_gnn_bias']


def kernel(**inputs):
    import numpy as _np
    import concourse.bacc as _bacc
    from concourse import mybir as _mybir
    from concourse.bass_utils import run_bass_kernel_spmd as _run

    nc = _bacc.Bacc("TRN2", target_bir_lowering=False, num_devices=1)
    arrays, args = {}, {}
    for name in _INS:
        a = _np.ascontiguousarray(inputs[name])
        arrays[f"in_{name}"] = a
        args[name] = nc.dram_tensor(f"in_{name}", a.shape, _mybir.dt.from_np(a.dtype), kind="ExternalInput").ap()
    out = nc.dram_tensor("out_x", (NODES, FEAT), F32, kind="ExternalOutput").ap()
    build(nc, args, out)
    r = _run(nc, [arrays], core_ids=[0])
    return r.results[0]["out_x"]
```

```python
import concourse.bass as bass
from concourse import mybir
from contextlib import ExitStack

F32 = mybir.dt.float32
I32 = mybir.dt.int32
BF16 = mybir.dt.bfloat16
ALU = mybir.AluOpType
ACT = mybir.ActivationFunctionType
AX = mybir.AxisListType

NODES, EDGES, FEAT = 12500, 200000, 32
EP = 125
COLS = EDGES // EP
CH = 16
PAIRS = COLS // (2 * CH)
NP = 128
NB = -(-NODES // NP)
TAIL = NODES - (NB - 1) * NP
NPAD = NB * NP
NG = 7
GR = 4
GROUPS = CH // GR
BIG = 1.0e30
HEADS0, HEADS3 = 2, 4
ATT = HEADS3 * FEAT
ATT_SUMS = ATT + HEADS3
ATT_ROW = ATT_SUMS + HEADS3


class Chain:

    def __init__(self, eng, sem):
        self.eng, self.sem, self.n = eng, sem, 0

    def link(self, ins):
        self.n += 1
        return ins.then_inc(self.sem, 1)

    def join(self):
        self.eng.wait_ge(self.sem, self.n)

    def step(self, ins):
        self.link(ins)
        self.join()

    def restart(self):
        if self.n:
            self.join()
            self.eng.sem_clear(self.sem)
            self.n = 0


class Kernel:

    def __init__(self, nc, stack):
        self.nc, self.stack, self.sems, self.used, self.owned = nc, stack, {}, [], 0

    def sem(self, name):
        if name not in self.sems:
            self.sems[name] = self.stack.enter_context(self.nc.semaphore(name))
        if name not in self.used:
            self.used.append(name)
        return self.sems[name]

    def own(self, name):
        self.owned += 1
        return self.stack.enter_context(self.nc.semaphore(f"{name}_{self.owned}"))

    def recycle(self):
        names, self.used = self.used, []
        with self.nc.Block() as block:
            @block.sync
            def _(sp):
                for name in names:
                    sp.sem_clear(self.sems[name])

    def wait(self, eng, who, sem, value):
        if isinstance(value, int):
            if value > 0:
                eng.wait_ge(sem, value)
            return
        eng.wait_ge(sem, value)
        eng.sem_inc(self.sem("tick_" + who), 1)


def pairs(eng, body, first=0, end=PAIRS, ahead=False):
    if first == 0:
        body(0)
        first = 1
    with eng.Fori(first, end - ahead) as i:
        body(i)
    if ahead:
        body(end - 1)


def known_ge(t, n):
    return isinstance(t, int) and t >= n


def first_chunk(t):
    return isinstance(t, int) and t == 0


def cols(t):
    return bass.ds(t * CH, CH)


def build(nc, A, out):
    top = ExitStack()
    with top:
        K = Kernel(nc, top)

        names = {}

        def once(name):
            names[name] = names.get(name, 0) + 1
            return name if names[name] == 1 else f"{name}_{names[name]}"

        def sb(stack, name, shape, dt=F32):
            return stack.enter_context(nc.sbuf_tensor(once(name), shape, dt))

        def ps(stack, name, shape, dt=F32):
            return stack.enter_context(nc.psum_tensor(once(name), shape, dt))

        def dram(name, shape, dt=F32):
            return nc.dram_tensor(name, shape, dt, kind="Internal").ap()

        x = sb(top, "x", [NP, NB, FEAT])
        h = sb(top, "h", [NP, NB, FEAT])
        ident = sb(top, "ident", [128, 128])
        identb = sb(top, "identb", [128, 128], BF16)
        ones = sb(top, "ones", [128, 128])
        before = sb(top, "before", [128, 128])
        iota_row = sb(top, "iota_row", [128, 128], BF16)
        pbase = sb(top, "pbase", [128, 1])
        zbias = sb(top, "zbias", [NP, 128])
        zeros = sb(top, "zeros", [EP, 640])
        src_i = sb(top, "src_i", [EP, COLS], I32)
        dst_i = sb(top, "dst_i", [EP, COLS], I32)
        cont = sb(top, "cont", [EP, COLS])
        first_seg = sb(top, "first_seg", [EP, COLS])
        last_seg = sb(top, "last_seg", [EP, COLS])
        endrow = sb(top, "endrow", [EP, 1], I32)
        fwd_row = sb(top, "fwd_row", [128, EP])
        fwd_all = sb(top, "fwd_all", [128, EP])
        bwd_row = sb(top, "bwd_row", [128, EP])
        bwd_all = sb(top, "bwd_all", [128, EP])
        last_dst = sb(top, "last_dst", [NP, NB], I32)
        has_dst = sb(top, "has_dst", [NP, NB])
        first_dst = sb(top, "first_dst", [NP, NB], I32)
        first_src = sb(top, "first_src", [NP, NB], I32)
        last_src = sb(top, "last_src", [NP, NB], I32)
        has_src = sb(top, "has_src", [NP, NB])
        base_src = sb(top, "base_src", [NP, NB])

        tab_s0 = dram("tab_s0", (NPAD, 64))
        tab_d0 = dram("tab_d0", (NPAD, 64))
        tab_h = dram("tab_h", (NPAD, FEAT))
        tab_h3 = dram("tab_h3", (NPAD, FEAT + HEADS3))
        tab_a3 = dram("tab_a3", (NPAD, HEADS3))
        en_rows = dram("en_rows", (EDGES, 64))
        ev_rows = dram("ev_rows", (EDGES + NP, 64))
        own_rows = dram("own_rows", (EDGES + NP, HEADS3))
        sums = dram("sums", (EDGES, FEAT))
        sums3 = dram("sums3", (EDGES, ATT_ROW))
        by_src = dram("by_src", (EDGES, 2), I32)

        def edge_rows(ap):
            if len(ap.shape) == 1:
                return ap.rearrange("(p c) -> p c", p=EP)
            if len(ap.shape) == 2:
                return ap.rearrange("(p c) f -> p c f", p=EP)
            return ap.rearrange("(p c) h f -> p c h f", p=EP)

        def node_rows(ap):
            return ap.rearrange("(b l) f -> l b f", l=NP)

        with ExitStack() as st:
            iota_i = sb(st, "iota_i", [128, 128], I32)
            pbase_i = sb(st, "pbase_i", [128, 1], I32)
            loaded, made, iotas = K.sem("loaded"), K.sem("made"), K.sem("iotas")
            chain_v, chain_p = K.sem("chain_v"), K.sem("chain_p")
            zeroed = K.sem("zeroed")
            block = st.enter_context(nc.Block())

            @block.sync
            def _(sp):
                sp.dma_start(src_i[:, :], edge_rows(A["src"])).then_inc(loaded, 16)
                sp.dma_start(dst_i[:, :], edge_rows(A["dst"])).then_inc(loaded, 16)
                full = (NB - 1) * NP
                sp.dma_start(x[:, 0:NB - 1, :], A["x"][0:full, :].rearrange("(b l) f -> l b f", l=NP)).then_inc(loaded, 16)
                sp.wait_ge(zeroed, 1)
                sp.dma_start(x[0:TAIL, NB - 1, :], A["x"][full:NODES, :]).then_inc(loaded, 16)
                sp.wait_ge(loaded, 64)

            @block.gpsimd
            def _(pool):
                c = Chain(pool, chain_p)
                nc.gpsimd.iota(iota_i[:, :], [[1, 128]], base=0, channel_multiplier=0).then_inc(iotas, 1)
                nc.gpsimd.iota(pbase_i[:, :], [[0, 1]], base=0, channel_multiplier=COLS).then_inc(iotas, 1)
                c.link(nc.gpsimd.memset(ident[:, :], 0.0))
                c.step(nc.gpsimd.memset(before[:, :], 0.0))
                nc.gpsimd.affine_select(out=ident[:, :], in_=ident[:, :], compare_op=ALU.not_equal, fill=1.0,
                                        base=0, pattern=[[-1, 128]], channel_multiplier=1).then_inc(made, 1)
                nc.gpsimd.affine_select(out=before[:, :], in_=before[:, :], compare_op=ALU.is_ge, fill=1.0,
                                        base=0, pattern=[[-1, 128]], channel_multiplier=1).then_inc(made, 1)
                c.restart()

            @block.vector
            def _(dve):
                nc.vector.memset(zeros[:, :], 0.0)
                nc.vector.memset(x[:, NB - 1, :], 0.0).then_inc(zeroed, 1)
                nc.vector.memset(zbias[:, :], 0.0)
                nc.vector.memset(ones[:, :], 1.0)
                dve.wait_ge(iotas, 2)
                nc.vector.tensor_copy(iota_row[:, :], iota_i[:, :])
                nc.vector.tensor_copy(pbase[:, :], pbase_i[:, :])
                dve.wait_ge(made, 2)
                nc.vector.tensor_copy(identb[:, :], ident[:, :])
        K.recycle()

        def edge_masks(key_i, first_keys, last_keys):
            with ExitStack() as st:
                key = sb(st, "key", [EP, COLS])
                nxt_i = sb(st, "nxt_i", [EP, 1], I32)
                nxt = sb(st, "nxt", [EP, 1])
                prv_i = sb(st, "prv_i", [EP, 1], I32)
                prv = sb(st, "prv", [EP, 1])
                goes_on = sb(st, "goes_on", [EP, 4])
                length = sb(st, "length", [EP, 1])
                diag = sb(st, "diag", [EP, 2, EP])
                rows = ps(st, "rows", [128, 2, 512])
                loaded, filled, diags, rowed, chain_v = (K.sem(n) for n in ("loaded", "filled", "diags", "rowed", "chain_v"))
                block = st.enter_context(nc.Block())

                @block.sync
                def _(sp):
                    sp.wait_ge(filled, 1)
                    sp.dma_start(nxt_i[0:EP - 1, :], first_keys[1:EP, :], allow_slow_non_contiguous=True).then_inc(loaded, 16)
                    sp.dma_start(prv_i[1:EP, :], last_keys[0:EP - 1, :], allow_slow_non_contiguous=True).then_inc(loaded, 16)

                @block.tensor
                def _(pe):
                    pe.wait_ge(diags, 2)
                    for k in range(2):
                        nc.tensor.matmul(rows[:, k, 0:EP], ones[0:EP, :], diag[:, k, :], start=True, stop=True).then_inc(rowed, 1)

                @block.vector
                def _(dve):
                    c = Chain(dve, chain_v)
                    c.step(nc.vector.memset(prv_i[:, :], -1))
                    nc.vector.memset(nxt_i[:, :], -1).then_inc(filled, 1)
                    c.step(nc.vector.tensor_copy(key[:, :], key_i))
                    c.step(nc.vector.tensor_tensor(cont[:, 1:COLS], key[:, 1:COLS], key[:, 0:COLS - 1], ALU.is_equal))
                    c.link(nc.vector.memset(first_seg[:, 0:1], 1.0))
                    c.link(nc.vector.memset(last_seg[:, COLS - 1:COLS], 1.0))
                    c.link(nc.vector.tensor_tensor_scan(first_seg[:, 1:COLS], cont[:, 1:COLS], cont[:, 1:COLS], 1.0, ALU.mult, ALU.min))
                    c.step(nc.vector.tensor_tensor_scan(last_seg[:, 0:COLS - 1][:, ::-1], cont[:, 1:COLS][:, ::-1], cont[:, 1:COLS][:, ::-1],
                                                        1.0, ALU.mult, ALU.min))
                    c.step(nc.vector.reduce_sum(length[:, :], first_seg[:, :], axis=AX.X))
                    c.step(nc.vector.scalar_tensor_tensor(length[:, :], length[:, :], -1.0, pbase[0:EP, :], ALU.add, ALU.add))
                    c.link(nc.vector.tensor_copy(endrow[:, :], length[:, :]))
                    dve.wait_ge(loaded, 32)
                    c.link(nc.vector.tensor_copy(prv[:, :], prv_i[:, :]))
                    c.step(nc.vector.tensor_copy(nxt[:, :], nxt_i[:, :]))
                    c.link(nc.vector.tensor_tensor(cont[:, 0:1], key[:, 0:1], prv[:, :], ALU.is_equal))
                    c.step(nc.vector.tensor_tensor(goes_on[:, 0:1], key[:, COLS - 1:COLS], nxt[:, :], ALU.is_equal))
                    nc.vector.tensor_scalar(diag[:, 0, :], ident[0:EP, 0:EP], goes_on[:, 0:1], None, ALU.mult).then_inc(diags, 1)
                    nc.vector.tensor_scalar(diag[:, 1, :], ident[0:EP, 0:EP], first_seg[:, COLS - 1:COLS], None, ALU.mult).then_inc(diags, 1)
                    dve.wait_ge(rowed, 2)
                    c.link(nc.vector.memset(bwd_row[:, 0:1], 0.0))
                    c.link(nc.vector.tensor_copy(bwd_row[:, 1:EP], rows[:, 0, 0:EP - 1]))
                    c.step(nc.vector.tensor_copy(fwd_row[:, :], rows[:, 0, 0:EP]))
                    c.link(nc.vector.tensor_tensor(fwd_all[:, :], fwd_row[:, :], rows[:, 1, 0:EP], ALU.mult))
                    c.link(nc.vector.tensor_tensor(bwd_all[:, :], bwd_row[:, :], rows[:, 1, 0:EP], ALU.mult))
                    c.restart()
            K.recycle()

        def normalize():
            with ExitStack() as st:
                d = sb(st, "d", [NP, NB, FEAT])
                sq = sb(st, "sq", [NP, NB, FEAT])
                mean = sb(st, "mean", [NP, NB])
                var = sb(st, "var", [NP, NB])
                std = sb(st, "std", [NP, NB])
                varied, rooted, chain_v = K.sem("varied"), K.sem("rooted"), K.sem("chain_v")
                block = st.enter_context(nc.Block())

                def wide(ap):
                    return ap[:, :].unsqueeze(2).to_broadcast([NP, NB, FEAT])

                @block.scalar
                def _(act):
                    act.wait_ge(varied, 1)
                    nc.scalar.activation(std[:, :], var[:, :], ACT.Sqrt).then_inc(rooted, 1)

                @block.vector
                def _(dve):
                    c = Chain(dve, chain_v)
                    c.step(nc.vector.reduce_sum(mean[:, :], x[:, :, :], axis=AX.X))
                    c.step(nc.vector.tensor_scalar(mean[:, :], mean[:, :], 1.0 / FEAT, None, ALU.mult))
                    c.step(nc.vector.tensor_tensor(d[:, :, :], x[:, :, :], wide(mean), ALU.subtract))
                    c.step(nc.vector.tensor_tensor(sq[:, :, :], d[:, :, :], d[:, :, :], ALU.mult))
                    c.step(nc.vector.reduce_sum(var[:, :], sq[:, :, :], axis=AX.X))
                    nc.vector.tensor_scalar(var[:, :], var[:, :], 1.0 / FEAT, 1e-5, ALU.mult, ALU.add).then_inc(varied, 1)
                    dve.wait_ge(rooted, 1)
                    c.step(nc.vector.reciprocal(mean[:, :], std[:, :]))
                    c.step(nc.vector.scalar_tensor_tensor(h[:, :, :], d[:, :, :], 0.0, wide(mean), ALU.max, ALU.mult))
                    c.restart()
            K.recycle()

        def node_product(src, width, weights, n_out, put):
            per_bank = 512 // n_out
            with ExitStack() as st:
                turned_ps = [ps(st, f"turned_ps{k}", [128, 2, 512]) for k in range(2)]
                turned = [sb(st, f"turned{k}", [width, 2, 512]) for k in range(2)]
                prod = [ps(st, f"prod{k}", [NP, 2, 512]) for k in range(2)]
                stage = [sb(st, f"stage{k}", [NP, NG, width]) for k in range(2)]
                n_staged = K.sem("n_staged")
                n_turned, n_copied, n_prod, n_put = (K.sem(n) for n in ("n_turned", "n_copied", "n_prod", "n_put"))
                chain_v = K.sem("chain_v")
                block = st.enter_context(nc.Block())
                steps = NB // NG

                def place(j):
                    return (0, j) if j < 4 else (1, j - 4)

                @block.tensor
                def _(pe):
                    def turn(g, k):
                        for j in range(NG):
                            a, b = place(j)
                            last = nc.tensor.transpose(turned_ps[k][0:width, a, b * 128:(b + 1) * 128], stage[k][:, j, :], ident[:, :])
                        last.then_inc(n_turned, 1)

                    def body(i):
                        for k in range(2):
                            g = 2 * i + k
                            K.wait(pe, "pe", n_copied, g - 1)
                            K.wait(pe, "pe", n_staged, g + 1)
                            turn(g, k)
                            K.wait(pe, "pe", n_copied, g + 1)
                            K.wait(pe, "pe", n_put, g - 1)
                            for j in range(NG):
                                a, b = place(j)
                                q, r = j // per_bank, j % per_bank
                                last = nc.tensor.matmul(prod[k][:, q, r * n_out:(r + 1) * n_out],
                                                        turned[k][:, a, b * 128:(b + 1) * 128], weights, start=True, stop=True)
                            last.then_inc(n_prod, 1)
                    body(0)
                    with pe.Fori(1, steps // 2) as i:
                        body(i)

                @block.scalar
                def _(act):
                    def body(i):
                        for k in range(2):
                            g = 2 * i + k
                            K.wait(act, "act", n_turned, g - 1)
                            nc.scalar.copy(stage[k][:, :, :], src[:, bass.ds(g * NG, NG), :]).then_inc(n_staged, 1)
                            K.wait(act, "act", n_turned, g + 1)
                            K.wait(act, "act", n_prod, g - 1)
                            nc.scalar.copy(turned[k][:, 0, :], turned_ps[k][0:width, 0, :])
                            nc.scalar.copy(turned[k][:, 1, 0:(NG - 4) * 128],
                                           turned_ps[k][0:width, 1, 0:(NG - 4) * 128]).then_inc(n_copied, 1)
                    body(0)
                    with act.Fori(1, steps // 2) as i:
                        body(i)

                @block.vector
                def _(dve):
                    def body(i):
                        for k in range(2):
                            g = 2 * i + k
                            K.wait(dve, "dve", n_prod, g + 1)
                            views = []
                            j = 0
                            while j < NG:
                                m = min(per_bank, NG - j)
                                views.append((j, m, prod[k][:, j // per_bank, 0:m * n_out].rearrange("p (j o) -> p j o", o=n_out)))
                                j += m
                            put(dve, views, g).then_inc(n_put, 1)
                    body(0)
                    with dve.Fori(1, steps // 2) as i:
                        body(i)
            K.recycle()

        def segment_ends(table, width, last_rows, target):
            final = edge_rows(table)[:, COLS - 1, :]
            with ExitStack() as st:
                tails = sb(st, "tails", [EP, width])
                tails_t = sb(st, "tails_t", [width, EP])
                carry_t = sb(st, "carry_t", [width, EP + 1])
                ends = sb(st, "ends", [EP, width])
                fixed = sb(st, "fixed", [EP, width])
                turn = ps(st, "turn", [width, EP])
                back = ps(st, "back", [EP, width])
                loaded, turned, scanned, backed, mended, chain_v = (K.sem(n) for n in (
                    "loaded", "turned", "scanned", "backed", "mended", "chain_v"))
                got, put_back, gathered = (K.own(n) for n in ("got", "put_back", "gathered"))
                block = st.enter_context(nc.Block())

                @block.sync
                def _(sp):
                    sp.dma_start(tails[:, :], final).then_inc(loaded, 16)

                @block.tensor
                def _(pe):
                    pe.wait_ge(loaded, 16)
                    nc.tensor.transpose(turn[:, :], tails[:, :], ident[0:EP, 0:EP]).then_inc(turned, 1)
                    pe.wait_ge(scanned, 1)
                    nc.tensor.transpose(back[:, :], carry_t[:, 0:EP], ident[0:width, 0:width]).then_inc(backed, 1)

                @block.vector
                def _(dve):
                    c = Chain(dve, chain_v)
                    dve.wait_ge(turned, 1)
                    c.link(nc.vector.memset(carry_t[:, 0:1], 0.0))
                    c.step(nc.vector.tensor_tensor(tails_t[:, :], turn[:, :], fwd_row[0:width, :], ALU.mult))
                    nc.vector.tensor_tensor_scan(carry_t[:, 1:EP + 1], fwd_all[0:width, :], tails_t[:, :], 0.0,
                                                 ALU.mult, ALU.add).then_inc(scanned, 1)
                    dve.wait_ge(backed, 1)
                    dve.wait_ge(got, 16)
                    nc.vector.tensor_tensor(fixed[:, :], back[:, :], ends[:, :], ALU.add).then_inc(mended, 1)
                    c.restart()

                @block.gpsimd
                def _(pool):
                    pool.indirect_dma_start(ends[:, :], None, table, bass.IndirectOffsetOnAxis(ap=endrow[:, 0:1], axis=0)).then_inc(got, 16)
                    pool.wait_ge(mended, 1)
                    pool.wait_ge(loaded, 16)
                    pool.indirect_dma_start(table, bass.IndirectOffsetOnAxis(ap=endrow[:, 0:1], axis=0), fixed[:, :], None).then_inc(put_back, 16)
                    pool.wait_ge(put_back, 16)
                    for b in range(NB):
                        pool.indirect_dma_start(target[:, b, :], None, table,
                                                bass.IndirectOffsetOnAxis(ap=last_rows[:, b:b + 1], axis=0)).then_inc(gathered, 16)
                    pool.wait_ge(gathered, 16 * NB)
            K.recycle()

        class SegmentSums:

            def __init__(self, st, width, table, beside=None):
                self.width, self.table, self.beside = width, edge_rows(table), beside
                self.fresh = [sb(st, f"fresh{k}", [EP, width, CH + 1]) for k in range(2)]
                self.keep = [sb(st, f"keep{k}", [EP, width, CH + 1]) for k in range(2)]
                self.run = [sb(st, f"run{k}", [EP, width, CH + 1]) for k in range(2)]
                self.rows = [sb(st, f"rows{k}", [EP, CH, table.shape[1]]) for k in range(2)]
                self.kept, self.scanned, self.copied = K.sem("kept"), K.sem("scanned"), K.sem("copied")
                self.stored = [K.sem(f"stored{k}") for k in range(2)]

            def message(self, k):
                return self.fresh[k][:, :, 1:CH + 1]

            def start(self):
                for k in range(2):
                    last = nc.vector.memset(self.keep[k][:, :, 0], 0.0)
                return [last, nc.vector.memset(self.run[1][:, :, CH], 0.0)]

            def mask(self, act, t, k):
                K.wait(act, "act", self.scanned, t - 1)
                flags = cont[:, cols(t)].unsqueeze(1).to_broadcast([EP, self.width, CH])
                nc.scalar.copy(self.keep[k][:, :, 1:CH + 1], flags).then_inc(self.kept, 1)

            def scan(self, dve, c, t, k):
                c.step(nc.vector.tensor_copy(self.fresh[k][:, :, 0], self.run[1 - k][:, :, CH]))
                K.wait(dve, "dve", self.kept, t + 1)
                K.wait(dve, "dve", self.copied, t - 1)
                flat = lambda ap: ap[:, :, :].rearrange("p f c -> p (f c)")
                nc.vector.tensor_tensor_scan(flat(self.run[k]), flat(self.keep[k]), flat(self.fresh[k]), 0.0,
                                             ALU.mult, ALU.add).then_inc(self.scanned, 1)
                K.wait(dve, "dve", self.scanned, t + 1)

            def store(self, act, t, k, i):
                K.wait(act, "act", self.scanned, t + 1)
                K.wait(act, "act", self.stored[k], i * 16)
                if self.beside:
                    nc.scalar.copy(self.rows[k][:, :, self.width:], self.beside[k])
                nc.scalar.copy(self.rows[k][:, :, 0:self.width], self.run[k][:, :, 1:CH + 1].rearrange("p f c -> p c f")).then_inc(self.copied, 1)
                K.wait(act, "act", self.copied, t + 1)
                act.dma_start(self.table[:, cols(t), :], self.rows[k][:, :, :]).then_inc(self.stored[k], 16)

            def finish(self, act):
                for k in range(2):
                    act.wait_ge(self.stored[k], 16 * PAIRS)

        class Spread:

            def __init__(self, st, width, table):
                self.width, self.whole, self.table = width, table, edge_rows(table[0:EDGES, :])
                self.raw = [sb(st, f"raw{k}", [EP, CH, width]) for k in range(2)]
                self.fresh = [sb(st, f"sfresh{k}", [EP, width, CH + 1]) for k in range(2)]
                self.keep = [sb(st, f"skeep{k}", [EP, width, CH + 1]) for k in range(2)]
                self.run = [sb(st, f"srun{k}", [EP, width, CH + 1]) for k in range(2)]
                self.init = sb(st, "sinit", [EP, width])
                self.raw_in = [K.sem(f"raw_in{k}") for k in range(2)]
                self.laid, self.spread = K.sem("spread_laid"), K.sem("spread_done")

            def rows(self, k):
                return self.run[k][:, :, 1:CH + 1].rearrange("p f c -> p c f")

            def place(self, pool, nodes, first_rows, table_of_nodes, first_key, scattered):
                for b in range(NB):
                    pool.indirect_dma_start(self.whole, bass.IndirectOffsetOnAxis(ap=first_rows[:, b:b + 1], axis=0),
                                            nodes(b), None).then_inc(scattered, 16)
                pool.indirect_dma_start(self.init[:, :], None, table_of_nodes,
                                        bass.IndirectOffsetOnAxis(ap=first_key, axis=0)).then_inc(scattered, 16)

            PLACED = 16 * (NB + 1)

            def start(self):
                for k in range(2):
                    last = nc.vector.memset(self.keep[k][:, :, 0], 0.0)
                return [last, nc.vector.tensor_copy(self.run[1][:, :, CH], self.init[:, :])]

            def load(self, eng, t, k):
                eng.dma_start(self.raw[k][:, :, :], self.table[:, cols(t), :]).then_inc(self.raw_in[k], 16)

            def lay(self, act, t, k, i):
                K.wait(act, "act", self.spread, t - 1)
                flags = cont[:, cols(t)].unsqueeze(1).to_broadcast([EP, self.width, CH])
                nc.scalar.copy(self.keep[k][:, :, 1:CH + 1], flags)
                K.wait(act, "act", self.raw_in[k], i * 16 + 16)
                nc.scalar.copy(self.fresh[k][:, :, 1:CH + 1], self.raw[k][:, :, :].rearrange("p c f -> p f c")).then_inc(self.laid, 1)

            def scan(self, dve, c, t, k):
                c.step(nc.vector.tensor_copy(self.fresh[k][:, :, 0], self.run[1 - k][:, :, CH]))
                K.wait(dve, "dve", self.laid, t + 1)
                flat = lambda ap: ap[:, :, :].rearrange("p f c -> p (f c)")
                nc.vector.tensor_tensor_scan(flat(self.run[k]), flat(self.keep[k]), flat(self.fresh[k]), 0.0,
                                             ALU.mult, ALU.add).then_inc(self.spread, 1)
                K.wait(dve, "dve", self.spread, t + 1)

        def segment_softmax(e, n_heads, floor):
            with ExitStack() as st:
                neg_cont = sb(st, "neg_cont", [EP, COLS])
                neg_first = sb(st, "neg_first", [EP, COLS])
                neg_last = sb(st, "neg_last", [EP, COLS])
                is_last = sb(st, "is_last", [EP, COLS])
                nxt = sb(st, "nxt_same", [EP, COLS])
                run = sb(st, "run", [EP, n_heads, COLS])
                tot = sb(st, "tot", [EP, n_heads, COLS])
                edge_t = sb(st, "edge_t", [n_heads, 2, EP])
                flags_t = sb(st, "flags_t", [n_heads, 4, EP])
                carry_t = sb(st, "carry_t", [n_heads, 2, EP + 1])
                carry = sb(st, "carry", [EP, 2, n_heads])
                turn = ps(st, "turn", [n_heads, 2, 512])
                back = ps(st, "back", [EP, 2, 512])
                tot_done, turned, scanned, backed, shifted, exped, chain_v = (K.sem(n) for n in (
                    "tot_done", "turned", "scanned", "backed", "shifted", "exped", "chain_v"))
                block = st.enter_context(nc.Block())

                @block.tensor
                def _(pe):
                    for r in range(2):
                        pe.wait_ge(tot_done, r + 1)
                        nc.tensor.transpose(turn[:, 0, 0:EP], tot[:, :, COLS - 1], ident[0:EP, 0:EP])
                        nc.tensor.transpose(turn[:, 1, 0:EP], tot[:, :, 0], ident[0:EP, 0:EP]).then_inc(turned, 1)
                        pe.wait_ge(scanned, r + 1)
                        nc.tensor.transpose(back[:, 0, 0:n_heads], carry_t[:, 0, 0:EP], ident[0:n_heads, 0:n_heads])
                        nc.tensor.transpose(back[:, 1, 0:n_heads], carry_t[:, 1, 1:EP + 1], ident[0:n_heads, 0:n_heads]).then_inc(backed, 1)

                @block.scalar
                def _(act):
                    act.wait_ge(shifted, 1)
                    nc.scalar.activation(e[:, :, :], e[:, :, :], ACT.Exp).then_inc(exped, 1)

                @block.vector
                def _(dve):
                    c = Chain(dve, chain_v)

                    def totals(r, cmul, op0, op1):
                        for j in range(n_heads):
                            c.link(nc.vector.tensor_tensor_scan(run[:, j, :], cmul[:, :], e[:, j, :], -BIG if op1 == ALU.max else 0.0, op0, op1))
                        c.join()
                        ends = is_last[:, :].unsqueeze(1).to_broadcast([EP, n_heads, COLS])
                        c.step(nc.vector.tensor_tensor(run[:, :, :], run[:, :, :], ends, ALU.mult))
                        for j in range(n_heads):
                            c.link(nc.vector.tensor_tensor_scan(tot[:, j, ::-1], nxt[:, ::-1], run[:, j, ::-1], 0.0, ALU.mult, ALU.add))
                        c.join()
                        dve.sem_inc(tot_done, 1)
                        dve.wait_ge(turned, r + 1)
                        comb = ALU.add if op1 == ALU.max else ALU.mult
                        c.link(nc.vector.tensor_tensor(edge_t[:, 0, :], turn[:, 0, 0:EP], flags_t[:, 0, :], comb))
                        c.link(nc.vector.tensor_tensor(edge_t[:, 1, :], turn[:, 1, 0:EP], flags_t[:, 1, :], comb))
                        none = -BIG if op1 == ALU.max else 0.0
                        c.link(nc.vector.memset(carry_t[:, 0, 0:1], none))
                        c.step(nc.vector.memset(carry_t[:, 1, EP:EP + 1], none))
                        c.link(nc.vector.tensor_tensor_scan(carry_t[:, 0, 1:EP + 1], flags_t[:, 2, :], edge_t[:, 0, :], none, comb, op1))
                        c.step(nc.vector.tensor_tensor_scan(carry_t[:, 1, 0:EP][:, ::-1], flags_t[:, 3, ::-1], edge_t[:, 1, ::-1], none, comb, op1))
                        dve.sem_inc(scanned, 1)
                        dve.wait_ge(backed, r + 1)
                        c.step(nc.vector.tensor_copy(carry[:, :, :], back[:, :, 0:n_heads]))
                        for side, member in enumerate((neg_first, neg_last) if op1 == ALU.max else (first_seg, last_seg)):
                            for j in range(n_heads):
                                c.link(nc.vector.scalar_tensor_tensor(tot[:, j, :], member[:, :], carry[:, side, j:j + 1], tot[:, j, :], comb, op1))
                            c.join()

                    flag_rows = (fwd_row, bwd_row, fwd_all, bwd_all)
                    for src_mask, dst_mask in ((cont, neg_cont), (first_seg, neg_first), (last_seg, neg_last)):
                        c.link(nc.vector.tensor_scalar(dst_mask[:, :], src_mask[:, :], BIG, -BIG, ALU.mult, ALU.add))
                    for n, row in enumerate(flag_rows):
                        c.link(nc.vector.tensor_scalar(flags_t[:, n, :], row[0:n_heads, :], BIG, -BIG, ALU.mult, ALU.add))
                    c.link(nc.vector.tensor_copy(nxt[:, 0:COLS - 1], cont[:, 1:COLS]))
                    c.link(nc.vector.memset(nxt[:, COLS - 1:COLS], 0.0))
                    c.join()
                    c.step(nc.vector.tensor_scalar(is_last[:, :], nxt[:, :], -1.0, 1.0, ALU.mult, ALU.add))
                    totals(0, neg_cont, ALU.add, ALU.max)
                    nc.vector.tensor_tensor(e[:, :, :], e[:, :, :], tot[:, :, :], ALU.subtract).then_inc(shifted, 1)
                    for n, row in enumerate(flag_rows):
                        c.link(nc.vector.tensor_copy(flags_t[:, n, :], row[0:n_heads, :]))
                    c.join()
                    dve.wait_ge(exped, 1)
                    totals(1, cont, ALU.mult, ALU.add)
                    c.step(nc.vector.tensor_scalar(tot[:, :, :], tot[:, :, :], floor, None, ALU.max))
                    c.step(nc.vector.reciprocal(run[:, :, :], tot[:, :, :]))
                    c.step(nc.vector.tensor_tensor(e[:, :, :], e[:, :, :], run[:, :, :], ALU.mult))
                    c.restart()
            K.recycle()

        def load(pairs_):
            loaded = K.sem("loaded")
            with nc.Block() as block:
                @block.sync
                def _(sp):
                    for target, source in pairs_:
                        sp.dma_start(target, source, allow_slow_non_contiguous=True).then_inc(loaded, 16)
                    sp.wait_ge(loaded, 16 * len(pairs_))
            K.recycle()

        def on_all(ap, n=NP):
            return ap.unsqueeze(0).to_broadcast([n, ap.shape[0]])

        def store_table(pairs_):
            stored = K.sem("stored0")
            with nc.Block() as block:
                @block.sync
                def _(sp):
                    for target, source in pairs_:
                        sp.dma_start(target, source, allow_slow_non_contiguous=True).then_inc(stored, 16)
                    sp.wait_ge(stored, 16 * len(pairs_))
            K.recycle()

        def masked_add(has, scale):
            chain_v = K.sem("chain_v")
            with nc.Block() as block:
                @block.vector
                def _(dve):
                    c = Chain(dve, chain_v)
                    wide = has[:, :].unsqueeze(2).to_broadcast([NP, NB, FEAT])
                    c.step(nc.vector.tensor_tensor(agg[:, :, :], agg[:, :, :], wide, ALU.mult))
                    c.step(nc.vector.scalar_tensor_tensor(x[:, :, :], agg[:, :, :], scale, x[:, :, :], ALU.mult, ALU.add))
                    c.restart()
            K.recycle()

        edge_masks(dst_i[:, :], edge_rows(A["dst"])[:, 0:1], edge_rows(A["dst"])[:, COLS - 1:COLS])
        normalize()
        e0 = ExitStack()
        alpha = sb(e0, "alpha", [EP, HEADS0, COLS])
        lo_s = sb(e0, "lo_s", [EP, COLS], BF16)
        hi_s = sb(e0, "hi_s", [EP, COLS], BF16)
        fd_stack = ExitStack()
        f_d = sb(fd_stack, "f_d", [NP, NB, 64])
        with ExitStack() as st:
            w = sb(st, "w_sd", [FEAT, 128])
            bias = sb(st, "b_sd", [NP, 128])
            f_s = sb(st, "f_s", [NP, NB, 64])
            load([(w[:, 0:64], A["L0_gnn_W2s"]), (w[:, 64:128], A["L0_gnn_W2d"]),
                  (bias[:, 0:64], on_all(A["L0_gnn_b2s"])), (bias[:, 64:128], on_all(A["L0_gnn_b2d"]))])

            def put(dve, views, g):
                for j, m, v in views:
                    at = bass.ds(g * NG + j, m)
                    for half, f in enumerate((f_s, f_d)):
                        side = slice(64 * half, 64 * half + 64)
                        last = nc.vector.tensor_tensor(f[:, at, :], v[:, :, side], bias[:, side].unsqueeze(1).to_broadcast([NP, m, 64]), ALU.add)
                return last
            node_product(h, FEAT, w[:, :], 128, put)
            store_table([(node_rows(tab_s0), f_s[:, :, :]), (node_rows(tab_d0), f_d[:, :, :])])

        FILL = 6400
        PIECES = COLS * 64 // FILL + COLS * HEADS3 // FILL
        EARLY = 11
        with ExitStack() as st:
            lo_d = sb(st, "lo_d", [EP, COLS], BF16)
            hi_d = sb(st, "hi_d", [EP, COLS], BF16)
            bits = sb(st, "bits", [EP, COLS], I32)
            attn = sb(st, "attn", [EP, 64])
            idx = [sb(st, f"idx{k}", [EP, CH], I32) for k in range(2)]
            en = [sb(st, f"en{k}", [EP, CH, 64]) for k in range(2)]
            en_back = [sb(st, f"en_back{k}", [EP, CH, 64]) for k in range(2)]
            zw = sb(st, "zw", [EP, CH, 64])
            hot_lo = [sb(st, f"hot_lo{k}", [EP, CH, 128], BF16) for k in range(2)]
            hot_hi = [sb(st, f"hot_hi{k}", [EP, CH, NB], BF16) for k in range(2)]
            counts = sb(st, "counts", [NP, NB])
            block_tot = sb(st, "block_tot", [NP, NB])
            start_of = sb(st, "start_of", [NP, NB])
            end_f = sb(st, "end_f", [NP, NB])
            lane = sb(st, "lane", [NP, 1])
            cnt_ps = [ps(st, f"cnt_ps{k}", [NP, NB]) for k in range(2)]
            tot_ps = ps(st, "tot_ps", [NP, NB])
            pre_ps = ps(st, "pre_ps", [NP, NB])
            ev = Spread(st, 64, ev_rows)
            idx_in = [K.sem(f"idx_in{k}") for k in range(2)]
            gathered = [K.own(f"gathered{k}") for k in range(2)]
            placed = K.own("placed")
            stored = [K.sem(f"stored{k}") for k in range(2)]
            back_in = [K.sem(f"back_in{k}") for k in range(2)]
            cleared, scored, hots, counted, copied, summed, starts, chain_v, loaded = (
                K.sem(n) for n in ("cleared", "scored", "hots", "counted", "copied", "summed", "starts", "chain_v", "loaded"))
            block = st.enter_context(nc.Block())
            src_rows = edge_rows(A["src"])

            @block.sync
            def _(sp):
                sp.dma_start(attn[:, :], on_all(A["L0_gnn_attn"].rearrange("a h f -> (a h f)"), EP)).then_inc(loaded, 16)
                for k in range(2):
                    sp.dma_start(idx[k][:, :], src_rows[:, cols(k)]).then_inc(idx_in[k], 16)

                def body(i):
                    for k in range(2):
                        t = 2 * i + k
                        K.wait(sp, "sp", gathered[k], (i + 1) * (16 * CH))
                        sp.dma_start(edge_rows(en_rows)[:, cols(t), :], en[k][:, :, :]).then_inc(stored[k], 16)
                        if not known_ge(t, 2 * PAIRS - 2):
                            sp.dma_start(idx[k][:, :], src_rows[:, cols(t + 2)]).then_inc(idx_in[k], 16)
                pairs(sp, body, ahead=True)
                for k in range(2):
                    sp.wait_ge(stored[k], 16 * PAIRS)

            @block.gpsimd
            def _(pool):
                def body(i):
                    for k in range(2):
                        K.wait(pool, "pool", idx_in[k], i * 16 + 16)
                        K.wait(pool, "pool", stored[k], i * 16)
                        for g in range(CH):
                            pool.indirect_dma_start(en[k][:, g, :], None, tab_s0,
                                                    bass.IndirectOffsetOnAxis(ap=idx[k][:, g:g + 1], axis=0)).then_inc(gathered[k], 16)
                pairs(pool, body, end=EARLY)
                pool.wait_ge(cleared, 16 * PIECES)
                pool.wait_ge(starts, 1)
                ev.place(pool, lambda b: f_d[:, b, :], first_dst, tab_d0, dst_i[:, 0:1], placed)
                pairs(pool, body, first=EARLY)

            @block.scalar
            def _(act):
                zeroed_pieces = 0

                def bring(t, k, i):
                    K.wait(act, "act", scored, t - 1)
                    K.wait(act, "act", stored[k], i * 16 + 16)
                    act.dma_start(en_back[k][:, :, :], edge_rows(en_rows)[:, cols(t), :]).then_inc(back_in[k], 16)
                    ev.load(act, t, k)
                for table, width in ((ev_rows, 64), (own_rows, HEADS3)):
                    filled = edge_rows(table[0:EDGES, :]).rearrange("p c f -> p (c f)")
                    for n in range(COLS * width // FILL):
                        act.dma_start(filled[:, n * FILL:(n + 1) * FILL].rearrange("p (n r) -> p n r", r=zeros.shape[1]),
                                      zeros[:, :].unsqueeze(1).to_broadcast([EP, FILL // zeros.shape[1], zeros.shape[1]])).then_inc(cleared, 16)
                        zeroed_pieces += 1
                        act.wait_ge(cleared, 16 * zeroed_pieces)
                act.wait_ge(placed, ev.PLACED)
                bring(0, 0, 0)
                bring(1, 1, 0)
                ev.lay(act, 0, 0, 0)

                def body(i):
                    for k in range(2):
                        t = 2 * i + k
                        if not known_ge(t, 2 * PAIRS - 1):
                            ev.lay(act, t + 1, 1 - k, i + k)
                        if not known_ge(t, 2 * PAIRS - 2):
                            bring(t + 2, k, i + 1)
                pairs(act, body, ahead=True)

            @block.tensor
            def _(pe):
                for q in range(2):
                    nc.tensor.matmul(cnt_ps[q][:, :], zbias[:, :], zbias[:, 0:NB], start=True, stop=False)

                    def body(i):
                        for k in range(2):
                            t = 2 * i + k
                            K.wait(pe, "pe", hots, t + 1 + q * (2 * PAIRS))
                            for g in range(CH):
                                last = nc.tensor.matmul(cnt_ps[q][:, :], hot_lo[k][:, g, :], hot_hi[k][:, g, :], start=False, stop=False)
                            last.then_inc(counted, 1)
                    pairs(pe, body)
                    nc.tensor.matmul(cnt_ps[q][:, :], zbias[:, :], zbias[:, 0:NB], start=False, stop=True).then_inc(counted, 1)
                    pe.wait_ge(copied, q + 1)
                    nc.tensor.matmul(tot_ps[:, :], ones[:, :], counts[:, :], start=True, stop=True)
                    nc.tensor.matmul(pre_ps[:, :], before[:, :], counts[:, :], start=True, stop=True).then_inc(summed, 1)

            @block.vector
            def _(dve):
                c = Chain(dve, chain_v)
                for key, lo, hi in ((src_i, lo_s, hi_s), (dst_i, lo_d, hi_d)):
                    c.step(nc.vector.tensor_scalar(bits[:, :], key[:, :], 127, None, ALU.bitwise_and))
                    c.step(nc.vector.tensor_copy(lo[:, :], bits[:, :]))
                    c.step(nc.vector.tensor_scalar(bits[:, :], key[:, :], 7, None, ALU.arith_shift_right))
                    c.step(nc.vector.tensor_copy(hi[:, :], bits[:, :]))
                c.step(nc.vector.tensor_scalar(lane[:, :], pbase[:, :], 1.0 / COLS, None, ALU.mult))
                dve.wait_ge(loaded, 16)
                c.restart()

                def hot(lo, hi, t, k):
                    nc.vector.tensor_tensor(hot_lo[k][:, :, :], iota_row[0:EP, :].unsqueeze(1).to_broadcast([EP, CH, 128]),
                                            lo[:, cols(t)].unsqueeze(2).to_broadcast([EP, CH, 128]), ALU.is_equal)
                    nc.vector.tensor_tensor(hot_hi[k][:, :, :], iota_row[0:EP, 0:NB].unsqueeze(1).to_broadcast([EP, CH, NB]),
                                            hi[:, cols(t)].unsqueeze(2).to_broadcast([EP, CH, NB]), ALU.is_equal).then_inc(hots, 1)

                def prefix(q, first, last, has, base):
                    dve.wait_ge(counted, (q + 1) * (2 * PAIRS + 1))
                    c.step(nc.vector.tensor_copy(counts[:, :], cnt_ps[q][:, :]))
                    dve.sem_inc(copied, 1)
                    dve.wait_ge(summed, q + 1)
                    c.step(nc.vector.tensor_copy(block_tot[:, :], tot_ps[:, :]))
                    c.link(nc.vector.memset(start_of[:, 0:1], 0.0))
                    c.step(nc.vector.tensor_tensor_scan(start_of[:, 1:NB], ones[:, 0:NB - 1], block_tot[:, 0:NB - 1], 0.0, ALU.mult, ALU.add))
                    c.step(nc.vector.tensor_tensor(start_of[:, :], start_of[:, :], pre_ps[:, :], ALU.add))
                    c.step(nc.vector.scalar_tensor_tensor(end_f[:, :], start_of[:, :], -1.0, counts[:, :], ALU.add, ALU.add))
                    c.step(nc.vector.tensor_scalar(end_f[:, :], end_f[:, :], 0.0, None, ALU.max))
                    c.link(nc.vector.tensor_copy(last[:, :], end_f[:, :]))
                    if base is not None:
                        c.link(nc.vector.tensor_copy(base[:, :], start_of[:, :]))
                    c.step(nc.vector.tensor_scalar(has[:, :], counts[:, :], 0.0, None, ALU.is_gt))
                    c.step(nc.vector.scalar_tensor_tensor(start_of[:, :], start_of[:, :], -float(EDGES), has[:, :], ALU.add, ALU.mult))
                    c.step(nc.vector.tensor_scalar(start_of[:, :], start_of[:, :], float(EDGES), None, ALU.add))
                    c.step(nc.vector.tensor_scalar(end_f[:, :], has[:, :], -1.0, 1.0, ALU.mult, ALU.add))
                    c.step(nc.vector.scalar_tensor_tensor(start_of[:, :], end_f[:, :], lane[:, 0:1], start_of[:, :], ALU.mult, ALU.add))
                    c.step(nc.vector.tensor_copy(first[:, :], start_of[:, :]))
                    dve.sem_inc(starts, 1)
                    c.restart()

                def count_dst(i):
                    for k in range(2):
                        t = 2 * i + k
                        K.wait(dve, "dve", counted, t - 1)
                        hot(lo_d, hi_d, t, k)
                pairs(dve, count_dst)
                prefix(0, first_dst, last_dst, has_dst, None)
                dve.wait_ge(placed, ev.PLACED)
                for ins in ev.start():
                    c.link(ins)
                c.restart()

                def body(i):
                    for k in range(2):
                        t = 2 * i + k
                        K.wait(dve, "dve", counted, t + 2 * PAIRS)
                        hot(lo_s, hi_s, t, k)
                        ev.scan(dve, c, t, k)
                        K.wait(dve, "dve", back_in[k], i * 16 + 16)
                        c.step(nc.vector.tensor_tensor(zw[:, :, :], en_back[k][:, :, :], ev.rows(k), ALU.add))
                        c.step(nc.vector.scalar_tensor_tensor(zw[:, :, :], zw[:, :, :], 0.2, zw[:, :, :], ALU.mult, ALU.max))
                        c.step(nc.vector.tensor_tensor(zw[:, :, :], zw[:, :, :], attn[:, :].unsqueeze(1).to_broadcast([EP, CH, 64]), ALU.mult))
                        nc.vector.tensor_reduce(alpha[:, :, cols(t)].rearrange("p h c -> p c h"),
                                                zw[:, :, :].rearrange("p c (h f) -> p c h f", h=HEADS0), AX.X, ALU.add).then_inc(scored, 1)
                        K.wait(dve, "dve", scored, t + 1)
                        c.restart()
                pairs(dve, body)
                prefix(1, first_src, last_src, has_src, base_src)
        fd_stack.close()
        K.recycle()

        segment_softmax(alpha, HEADS0, 1e-9)

        with ExitStack() as st:
            en = [sb(st, f"en{k}", [EP, CH, 64]) for k in range(2)]
            r = [sb(st, f"r{k}", [EP, CH, 64]) for k in range(2)]
            z = [sb(st, f"z{k}", [EP, CH, 64]) for k in range(2)]
            z_top = sb(st, "z_top", [EP, CH, HEADS0])
            total = sb(st, "total", [EP, CH, HEADS0])
            z_div = sb(st, "z_div", [EP, CH, HEADS0])
            hot_lo = [sb(st, f"hot_lo{k}", [EP, CH, 128], BF16) for k in range(2)]
            hot_hi = [sb(st, f"hot_hi{k}", [EP, CH, NB], BF16) for k in range(2)]
            hot_t = [sb(st, f"hot_t{q}", [NP, GR, EP]) for q in range(GROUPS)]
            hot_tb = [sb(st, f"hot_tb{q}", [NP, GR, EP], BF16) for q in range(GROUPS)]
            place_sb = [sb(st, f"place_sb{q}", [NP, NB]) for q in range(GROUPS)]
            own_same = [sb(st, f"own_same{k}", [EP, GR, EP], BF16) for k in range(2)]
            cross_same = [sb(st, f"cross_same{k}", [EP, 2, 3 * EP], BF16) for k in range(2)]
            not_before = sb(st, "not_before", [EP, GR, EP], BF16)
            picked = sb(st, "picked", [EP, GR, NB])
            pos = [sb(st, f"pos{k}", [EP, CH]) for k in range(2)]
            pos_i = [sb(st, f"pos_i{k}", [EP, CH], I32) for k in range(2)]
            ends = [sb(st, f"ends{k}", [EP, CH, 2], I32) for k in range(2)]
            place_ps = ps(st, "place_ps", [NP, NB])
            turn_ps = [ps(st, f"turn_ps{k}", [NP, GR, 128], BF16) for k in range(2)]
            own_ps = ps(st, "own_ps", [EP, GR, EP])
            cross_ps = ps(st, "cross_ps", [EP, 2, 512])
            rank_ps = [ps(st, f"rank_ps{k}", [EP, GR, NB]) for k in range(2)]
            S = SegmentSums(st, FEAT, sums)
            rows_in = [K.sem(f"rows_in{k}") for k in range(2)]
            sent = [K.own(f"sent{k}") for k in range(2)]
            (shifted, exped, multiplied, hots, turned, turned_sb, samed, copied_same, ranked, selected, placed, place_out, posed,
             chain_v, triangle) = (K.sem(n) for n in (
                 "shifted", "exped", "multiplied", "hots", "turned", "turned_sb", "samed", "copied_same", "ranked",
                 "selected", "placed", "place_out", "posed", "chain_v", "triangle"))
            block = st.enter_context(nc.Block())
            last_chunk = 2 * PAIRS - 1

            def cross(a, b):
                return (0, (b - 1) * EP) if a == 0 else (1, (b - 2 if a == 1 else 2) * EP)

            @block.sync
            def _(sp):
                def body(i):
                    for k in range(2):
                        t = 2 * i + k
                        K.wait(sp, "sp", multiplied, t - 1)
                        sp.dma_start(en[k][:, :, :], edge_rows(en_rows)[:, cols(t), :]).then_inc(rows_in[k], 16)
                        sp.dma_start(r[k][:, :, :], edge_rows(A["edge_attr3_2x32"])[:, cols(t), :, :].rearrange("p c h f -> p c (h f)")).then_inc(rows_in[k], 16)
                pairs(sp, body)

            @block.gpsimd
            def _(pool):
                def body(i):
                    for k in range(2):
                        t = 2 * i + k
                        K.wait(pool, "pool", posed, t + 1)
                        for g in range(CH):
                            pool.indirect_dma_start(by_src, bass.IndirectOffsetOnAxis(ap=pos_i[k][:, g:g + 1], axis=0),
                                                    ends[k][:, g, :], None).then_inc(sent[k], 16)
                pairs(pool, body)
                for k in range(2):
                    pool.wait_ge(sent[k], 16 * CH * PAIRS)

            @block.tensor
            def _(pe):
                def turn(n, k, q):
                    K.wait(pe, "pe", turned_sb, n - 1)
                    for g in range(GR):
                        last = nc.tensor.transpose(turn_ps[q % 2][:, g, 0:EP], hot_lo[k][:, q * GR + g, :], identb[0:EP, 0:EP])
                    last.then_inc(turned, 1)

                def rank(n, k, q):
                    s = q % 2
                    K.wait(pe, "pe", selected, n - 1)
                    K.wait(pe, "pe", copied_same, n + 1)
                    for b in range(GR):
                        o = rank_ps[s][:, b, :]
                        nc.tensor.matmul(o, hot_t[q][:, b, :], place_sb[q][:, :], start=True, stop=False)
                        for a in range(b):
                            bank, at = cross(a, b)
                            nc.tensor.matmul(o, cross_same[s][:, bank, at:at + EP], hot_hi[k][:, q * GR + a, :], start=False, stop=False)
                        last = nc.tensor.matmul(o, own_same[s][:, b, :], hot_hi[k][:, q * GR + b, :], start=False, stop=True)
                    last.then_inc(ranked, 1)

                def body(i):
                    for k in range(2):
                        for q in range(GROUPS):
                            t = 2 * i + k
                            n = t * GROUPS + q
                            if q < GROUPS - 1:
                                turn(n + 1, k, q + 1)
                            elif not known_ge(t, last_chunk):
                                K.wait(pe, "pe", hots, t + 2)
                                turn(n + 1, 1 - k, 0)
                            K.wait(pe, "pe", turned_sb, n + 1)
                            K.wait(pe, "pe", copied_same, n)
                            nc.tensor.matmul(own_ps[:, :, :].rearrange("p g e -> p (g e)"), identb[0:EP, 0:EP],
                                             not_before[:, :, :].rearrange("p g e -> p (g e)"), start=True, stop=False)
                            for a in range(GR):
                                nc.tensor.matmul(own_ps[:, a, :], hot_tb[q][:, a, :], hot_tb[q][:, a, :], start=False, stop=a == GR - 1)
                            for a in range(GR - 1):
                                bank, at = cross(a, a + 1)
                                later = hot_tb[q][:, a + 1:GR, :].rearrange("p c e -> p (c e)")
                                last = nc.tensor.matmul(cross_ps[:, bank, at:at + (GR - 1 - a) * EP], hot_tb[q][:, a, :], later, start=True, stop=True)
                            last.then_inc(samed, 1)
                            K.wait(pe, "pe", place_out, n + 1)
                            nc.tensor.matmul(place_ps[:, :], ident[:, :], place_sb[q][:, :], start=True, stop=False)
                            for g in range(GR):
                                last = nc.tensor.matmul(place_ps[:, :], hot_lo[k][:, q * GR + g, :], hot_hi[k][:, q * GR + g, :],
                                                        start=False, stop=g == GR - 1)
                            last.then_inc(placed, 1)
                            if q:
                                rank(n - 1, k, q - 1)
                            elif not first_chunk(t):
                                rank(n - 1, 1 - k, GROUPS - 1)
                pe.wait_ge(triangle, 1)
                K.wait(pe, "pe", hots, 1)
                turn(0, 0, 0)
                pairs(pe, body, ahead=True)
                rank(last_chunk * GROUPS + GROUPS - 1, 1, GROUPS - 1)

            @block.scalar
            def _(act):
                nc.scalar.copy(place_sb[0][:, :], base_src[:, :]).then_inc(place_out, 1)

                def take_turned(n, q):
                    K.wait(act, "act", turned, n + 1)
                    K.wait(act, "act", ranked, n - (GROUPS - 1))
                    nc.scalar.copy(hot_tb[q][:, :, :], turn_ps[q % 2][:, :, 0:EP])
                    nc.scalar.copy(hot_t[q][:, :, :], turn_ps[q % 2][:, :, 0:EP]).then_inc(turned_sb, 1)

                def body(i):
                    for k in range(2):
                        t = 2 * i + k
                        S.mask(act, t, k)
                        for q in range(GROUPS):
                            n, s = t * GROUPS + q, q % 2
                            if q < GROUPS - 1 or not known_ge(t, last_chunk):
                                take_turned(n + 1, (q + 1) % GROUPS)
                            K.wait(act, "act", samed, n + 1)
                            K.wait(act, "act", ranked, n - 1)
                            nc.scalar.activation(own_same[s][:, :, :], own_ps[:, :, :], ACT.Relu)
                            nc.scalar.copy(cross_same[s][:, :, :], cross_ps[:, :, 0:3 * EP]).then_inc(copied_same, 1)
                            K.wait(act, "act", placed, n + 1)
                            K.wait(act, "act", ranked, n - (GROUPS - 2))
                            nc.scalar.copy(place_sb[(q + 1) % GROUPS][:, :], place_ps[:, :]).then_inc(place_out, 1)
                            if q == 3 and not first_chunk(t):
                                S.store(act, t - 1, 1 - k, i - 1 + k)
                            if q == 2:
                                K.wait(act, "act", shifted, t + 1)
                                nc.scalar.activation(z[k][:, :, :], z[k][:, :, :], ACT.Exp).then_inc(exped, 1)
                take_turned(0, 0)
                pairs(act, body, ahead=True)
                S.store(act, last_chunk, 1, PAIRS - 1)
                S.finish(act)

            @block.vector
            def _(dve):
                c = Chain(dve, chain_v)
                for ins in S.start():
                    c.link(ins)
                nc.vector.tensor_scalar(not_before[:, :, :], before[0:EP, 0:EP].unsqueeze(1).to_broadcast([EP, GR, EP]),
                                        -1.0, None, ALU.add).then_inc(triangle, 1)
                c.restart()

                def per_head(ap):
                    return ap.unsqueeze(3).to_broadcast([EP, CH, HEADS0, FEAT])

                def heads(ap):
                    return ap.rearrange("p c (h f) -> p c h f", h=HEADS0)

                def hot(t, k):
                    K.wait(dve, "dve", ranked, (t - 1) * GROUPS)
                    nc.vector.tensor_tensor(hot_lo[k][:, :, :], iota_row[0:EP, :].unsqueeze(1).to_broadcast([EP, CH, 128]),
                                            lo_s[:, cols(t)].unsqueeze(2).to_broadcast([EP, CH, 128]), ALU.is_equal)
                    nc.vector.tensor_tensor(hot_hi[k][:, :, :], iota_row[0:EP, 0:NB].unsqueeze(1).to_broadcast([EP, CH, NB]),
                                            hi_s[:, cols(t)].unsqueeze(2).to_broadcast([EP, CH, NB]), ALU.is_equal).then_inc(hots, 1)

                def pick(n, k, q):
                    K.wait(dve, "dve", ranked, n + 1)
                    c.join()
                    for g in range(GR):
                        at = q * GR + g
                        c.link(nc.vector.scalar_tensor_tensor(picked[:, g, :], rank_ps[q % 2][:, g, :], 1.0, hot_hi[k][:, at, :], ALU.mult, ALU.mult,
                                                              accum_out=pos[k][:, at:at + 1]))
                    c.join()
                    dve.sem_inc(selected, 1)

                def send(t, k, i):
                    K.wait(dve, "dve", sent[k], i * (16 * CH))
                    c.link(nc.vector.tensor_copy(ends[k][:, :, 0], src_i[:, cols(t)]))
                    c.link(nc.vector.tensor_copy(ends[k][:, :, 1], dst_i[:, cols(t)]))
                    c.step(nc.vector.tensor_copy(pos_i[k][:, :], pos[k][:, :]))
                    dve.sem_inc(posed, 1)

                def divide(t, k):
                    K.wait(dve, "dve", exped, t + 1)
                    c.step(nc.vector.tensor_reduce(total[:, :, :], heads(z[k][:, :, :]), AX.X, ALU.add))
                    c.step(nc.vector.reciprocal(z_div[:, :, :], total[:, :, :]))
                    c.link(nc.vector.tensor_tensor(heads(z[k][:, :, :]), heads(z[k][:, :, :]), per_head(z_div[:, :, :]), ALU.mult))

                def add_up(t, k):
                    c.join()
                    c.link(nc.vector.tensor_tensor(S.message(k), z[k][:, :, 0:FEAT].rearrange("p c f -> p f c"),
                                                   z[k][:, :, FEAT:2 * FEAT].rearrange("p c f -> p f c"), ALU.add))
                    S.scan(dve, c, t, k)

                def body(i):
                    for k in range(2):
                        t = 2 * i + k
                        K.wait(dve, "dve", rows_in[k], i * 32 + 32)
                        nc.vector.tensor_tensor(z[k][:, :, :], en[k][:, :, :], r[k][:, :, :], ALU.mult).then_inc(multiplied, 1)
                        if not first_chunk(t):
                            pick(t * GROUPS - 1, 1 - k, GROUPS - 1)
                            send(t - 1, 1 - k, i - 1 + k)
                        K.wait(dve, "dve", multiplied, t + 1)
                        z4 = heads(z[k][:, :, :])
                        c.link(nc.vector.tensor_tensor(z4, z4, per_head(alpha[:, :, cols(t)].rearrange("p h c -> p c h")), ALU.mult))
                        if not known_ge(t, last_chunk):
                            hot(t + 1, 1 - k)
                        pick(t * GROUPS, k, 0)
                        c.step(nc.vector.tensor_reduce(z_top[:, :, :], z4, AX.X, ALU.max))
                        nc.vector.tensor_tensor(z4, z4, per_head(z_top[:, :, :]), ALU.subtract).then_inc(shifted, 1)
                        if not first_chunk(t):
                            divide(t - 1, 1 - k)
                        pick(t * GROUPS + 1, k, 1)
                        if not first_chunk(t):
                            add_up(t - 1, 1 - k)
                        pick(t * GROUPS + 2, k, 2)
                        c.restart()
                hot(0, 0)
                pairs(dve, body, ahead=True)
                pick(last_chunk * GROUPS + GROUPS - 1, 1, GROUPS - 1)
                send(last_chunk, 1, PAIRS - 1)
                divide(last_chunk, 1)
                add_up(last_chunk, 1)
                c.restart()
        K.recycle()
        e0.close()
        agg = sb(top, "agg", [NP, NB, FEAT])

        segment_ends(sums, FEAT, last_dst, agg)
        with ExitStack() as st:
            w = sb(st, "w1", [FEAT, FEAT])
            bias = sb(st, "b1", [NP, FEAT])
            load([(w[:, :], A["L0_gnn_W1"]), (bias[:, :], on_all(A["L0_gnn_b1"]))])
            chain_v = K.sem("chain_v")
            with nc.Block() as block:
                @block.vector
                def _(dve):
                    c = Chain(dve, chain_v)
                    c.step(nc.vector.tensor_tensor(agg[:, :, :], agg[:, :, :], has_dst[:, :].unsqueeze(2).to_broadcast([NP, NB, FEAT]), ALU.mult))
                    c.link(nc.vector.tensor_tensor(agg[:, :, :], agg[:, :, :], h[:, :, :], ALU.add))
                    c.link(nc.vector.tensor_tensor(x[:, :, :], x[:, :, :], bias[:, :].unsqueeze(1).to_broadcast([NP, NB, FEAT]), ALU.add))
                    c.restart()
            K.recycle()

            def put(dve, views, g):
                for j, m, v in views:
                    xs = x[:, bass.ds(g * NG + j, m), :]
                    last = nc.vector.tensor_tensor(xs, xs, v, ALU.add)
                return last
            node_product(agg, FEAT, w[:, :], FEAT, put)

        normalize()
        store_table([(node_rows(tab_h), h[:, :, :])])

        def gather_rows(st):
            idx = [sb(st, f"idx{k}", [EP, CH], I32) for k in range(2)]
            rows = [sb(st, f"hs{k}", [EP, CH, FEAT]) for k in range(2)]
            idx_in = [K.sem(f"idx_in{k}") for k in range(2)]
            gathered = [K.own(f"gathered{k}") for k in range(2)]

            def load_idx(sp, t, k, i):
                K.wait(sp, "sp", gathered[k], i * (16 * CH))
                sp.dma_start(idx[k][:, :], edge_rows(A["src"])[:, cols(t)]).then_inc(idx_in[k], 16)

            def gather(pool, t, k, i):
                K.wait(pool, "pool", idx_in[k], i * 16 + 16)
                for g in range(CH):
                    pool.indirect_dma_start(rows[k][:, g, :], None, tab_h,
                                            bass.IndirectOffsetOnAxis(ap=idx[k][:, g:g + 1], axis=0)).then_inc(gathered[k], 16)
            return rows, gathered, load_idx, gather

        with ExitStack() as st:
            rows, gathered, load_idx, gather = gather_rows(st)
            S = SegmentSums(st, FEAT, sums)
            laid, started, chain_v = K.sem("laid"), K.sem("started"), K.sem("chain_v")
            block = st.enter_context(nc.Block())

            @block.sync
            def _(sp):
                def body(i):
                    for k in range(2):
                        load_idx(sp, 2 * i + k, k, i)
                pairs(sp, body)

            @block.gpsimd
            def _(pool):
                def body(i):
                    for k in range(2):
                        t = 2 * i + k
                        K.wait(pool, "pool", laid, t - 1)
                        gather(pool, t, k, i)
                pairs(pool, body)

            @block.scalar
            def _(act):
                def body(i):
                    for k in range(2):
                        t = 2 * i + k
                        S.mask(act, t, k)
                        K.wait(act, "act", gathered[k], (i + 1) * (16 * CH))
                        nc.scalar.copy(S.message(k), rows[k][:, :, :].rearrange("p c f -> p f c")).then_inc(laid, 1)
                        S.store(act, t, k, i)
                pairs(act, body)
                S.finish(act)

            @block.vector
            def _(dve):
                c = Chain(dve, chain_v)
                for ins in S.start():
                    c.link(ins)
                c.restart()

                def body(i):
                    for k in range(2):
                        t = 2 * i + k
                        K.wait(dve, "dve", laid, t + 1)
                        S.scan(dve, c, t, k)
                        c.restart()
                pairs(dve, body)
        K.recycle()
        segment_ends(sums, FEAT, last_dst, agg)
        masked_add(has_dst, 1.0)

        normalize()
        store_table([(node_rows(tab_h), h[:, :, :])])
        MUL, HID, TPW = 8, 64, 256
        with ExitStack() as st:
            w1 = sb(st, "w1_pairs", [128, CH // 2, 128])
            w2 = sb(st, "w2_pair", [128, 128])
            w3 = sb(st, "w3_pair", [128, 2, TPW])
            b1 = sb(st, "b1_pair", [128, 1])
            b2 = sb(st, "b2_pair", [128, 1])
            b3 = sb(st, "b3", [1, TPW])
            b3_part = [sb(st, f"b3_part{n}", [1, TPW], BF16) for n in range(3)]
            b3_rest = sb(st, "b3_rest", [1, TPW])
            b3_rows = sb(st, "b3_rows", [3, 2, TPW], BF16)
            ones_b = sb(st, "ones_b", [3, EP], BF16)
            zero = [w1, w2, w3]
            loaded, zeroed, split, chain_v = K.sem("loaded"), K.sem("zeroed"), K.sem("split"), K.sem("chain_v")
            with nc.Block() as block:
                @block.vector
                def _(dve):
                    c = Chain(dve, chain_v)
                    nc.vector.memset(w1[:, :, :], 0.0).then_inc(zeroed, 1)
                    nc.vector.memset(w2[:, :], 0.0).then_inc(zeroed, 1)
                    nc.vector.memset(w3[:, :, :], 0.0).then_inc(zeroed, 1)
                    nc.vector.memset(ones_b[:, :], 1.0)
                    dve.wait_ge(loaded, 16)
                    c.step(nc.vector.tensor_scalar(b3[:, 64:128], b3[:, 64:128], 3.0 ** -0.5, None, ALU.mult))
                    c.step(nc.vector.tensor_copy(b3_part[0][:, :], b3[:, :]))
                    c.step(nc.vector.tensor_tensor(b3_rest[:, :], b3[:, :], b3_part[0][:, :], ALU.subtract))
                    c.step(nc.vector.tensor_copy(b3_part[1][:, :], b3_rest[:, :]))
                    c.step(nc.vector.tensor_tensor(b3_rest[:, :], b3_rest[:, :], b3_part[1][:, :], ALU.subtract))
                    c.step(nc.vector.tensor_copy(b3_part[2][:, :], b3_rest[:, :]))
                    dve.sem_inc(split, 1)
                    c.restart()

                @block.sync
                def _(sp):
                    sp.dma_start(b3[:, :], A["L2_gnn_b3"].unsqueeze(0)).then_inc(loaded, 16)
                    sp.wait_ge(zeroed, 3)
                    sp.wait_ge(loaded, 16)
                    n = 1
                    for c_ in range(CH):
                        o = (c_ % 2) * HID
                        sp.dma_start(w1[c_ * MUL:(c_ + 1) * MUL, c_ // 2, o:o + HID], A["L2_gnn_W1"]).then_inc(loaded, 16)
                        n += 1
                    for o in range(2):
                        at = slice(o * HID, (o + 1) * HID)
                        sp.dma_start(w2[at, at], A["L2_gnn_W2"]).then_inc(loaded, 16)
                        sp.dma_start(w3[at, o, :], A["L2_gnn_W3"]).then_inc(loaded, 16)
                        sp.dma_start(b1[at, :], A["L2_gnn_b1"].unsqueeze(1)).then_inc(loaded, 16)
                        sp.dma_start(b2[at, :], A["L2_gnn_b2"].unsqueeze(1)).then_inc(loaded, 16)
                        n += 4
                    sp.wait_ge(split, 1)
                    for m in range(3):
                        for o in range(2):
                            sp.dma_start(b3_rows[m:m + 1, o, :], b3_part[m][:, :]).then_inc(loaded, 16)
                            n += 1
                    sp.wait_ge(loaded, 16 * n)
            K.recycle()
            with nc.Block() as block:
                @block.vector
                def _(dve):
                    nc.vector.tensor_scalar(w3[:, :, 64:128], w3[:, :, 64:128], 3.0 ** -0.5, None, ALU.mult)

            rows, gathered, load_idx, gather = gather_rows(st)
            S = SegmentSums(st, FEAT, sums)
            radial = [sb(st, f"radial{k}", [EP, CH * MUL]) for k in range(2)]
            sh = sb(st, "sh", [EP, COLS, 4])
            radial_t = sb(st, "radial_t", [128, EP])
            x1 = sb(st, "x1", [128, 2, 4 * EP])
            x2 = [sb(st, f"x2_{k}", [128, 2, 4 * EP]) for k in range(2)]
            hv1 = sb(st, "hv1", [EP, CH, MUL, 3])
            zz = [sb(st, f"zz{k}", [EP, CH, 3, MUL]) for k in range(2)]
            zv = [sb(st, f"zv{k}", [EP, CH, 3, MUL]) for k in range(2)]
            zv_wide = [sb(st, f"zv_wide{k}", [EP, CH, 3, MUL, MUL]) for k in range(2)]
            prod_a = [sb(st, f"prod_a{k}", [EP, 4, MUL, 3, MUL]) for k in range(2)]
            prod_b = [sb(st, f"prod_b{k}", [EP, 4, 3, MUL, MUL]) for k in range(2)]
            res_a = sb(st, "res_a", [EP, CH, MUL, 3])
            res_b = sb(st, "res_b", [EP, CH, 3, MUL])
            cross = sb(st, "cross", [EP, CH, MUL, 3])
            radial_ps = ps(st, "radial_ps", [128, EP])
            hid_ps = ps(st, "hid_ps", [128, 2, 512])
            tp_ps = [ps(st, f"tp_ps{k}", [EP, 2, 512]) for k in range(2)]
            radial_in = [K.sem(f"radial_in{k}") for k in range(2)]
            (turned, turned_sb, hid1, act1, hid2, act2, tpw, taken, chain_v, used, scaled, widened, prepared, sh_in) = (
                K.sem(n) for n in ("turned", "turned_sb", "hid1", "act1", "hid2", "act2", "tpw", "taken", "chain_v", "used",
                                   "scaled", "widened", "prepared", "sh_in"))
            block = st.enter_context(nc.Block())

            @block.sync
            def _(sp):
                sp.dma_start(sh[:, :, :], edge_rows(A["edge_attr_4"])).then_inc(sh_in, 16)

                def body(i):
                    for k in range(2):
                        t = 2 * i + k
                        K.wait(sp, "sp", turned, t - 1)
                        sp.dma_start(radial[k][:, :], edge_rows(A["edge_attr_8"])[:, cols(t), :].rearrange("p c f -> p (c f)")).then_inc(radial_in[k], 16)
                        load_idx(sp, t, k, i)
                pairs(sp, body)

            @block.gpsimd
            def _(pool):
                def body(i):
                    for k in range(2):
                        t = 2 * i + k
                        K.wait(pool, "pool", prepared, t - 1)
                        K.wait(pool, "pool", widened, t - 1)
                        gather(pool, t, k, i)
                pairs(pool, body)

            @block.tensor
            def _(pe):
                def turn(t, k, i):
                    K.wait(pe, "pe", radial_in[k], i * 16 + 16)
                    K.wait(pe, "pe", turned_sb, t)
                    nc.tensor.transpose(radial_ps[:, :], radial[k][:, :], ident[0:EP, 0:EP]).then_inc(turned, 1)

                def hidden1(t):
                    K.wait(pe, "pe", turned_sb, t + 1)
                    K.wait(pe, "pe", act2, 2 * t)
                    for a in range(2):
                        for b in range(4):
                            last = nc.tensor.matmul(hid_ps[:, a, b * EP:(b + 1) * EP], w1[:, a * 4 + b, :], radial_t[:, :], start=True, stop=True)
                        last.then_inc(hid1, 1)

                def hidden2(t, a):
                    K.wait(pe, "pe", act1, 2 * t + a + 1)
                    nc.tensor.matmul(hid_ps[:, a, 0:4 * EP], w2[:, :], x1[:, a, :], start=True, stop=True).then_inc(hid2, 1)

                def products(t, k, q):
                    a = q // 2
                    if q % 2 == 0:
                        K.wait(pe, "pe", act2, 2 * t + a + 1)
                    K.wait(pe, "pe", taken, 4 * t + q - 1)
                    for j in range(2):
                        b = (q % 2) * 2 + j
                        o = tp_ps[q % 2][:, j, :]
                        nc.tensor.matmul(o, x2[k][:, a, b * EP:(b + 1) * EP], w3[:, :, :].rearrange("p o n -> p (o n)"), start=True, stop=False)
                        last = nc.tensor.matmul(o, ones_b[:, :], b3_rows[:, :, :].rearrange("p o n -> p (o n)"), start=False, stop=True)
                    last.then_inc(tpw, 1)

                turn(0, 0, 0)
                hidden1(0)
                hidden2(0, 0)
                hidden2(0, 1)

                def body(i):
                    for k in range(2):
                        t = 2 * i + k
                        more = not known_ge(t, 2 * PAIRS - 1)
                        products(t, k, 0)
                        products(t, k, 1)
                        if more:
                            turn(t + 1, 1 - k, i + k)
                            hidden1(t + 1)
                            hidden2(t + 1, 0)
                            hidden2(t + 1, 1)
                        products(t, k, 2)
                        products(t, k, 3)
                pairs(pe, body, ahead=True)

            @block.scalar
            def _(act):
                def take_turned(t):
                    K.wait(act, "act", turned, t + 1)
                    K.wait(act, "act", hid1, 2 * t)
                    nc.scalar.copy(radial_t[:, :], radial_ps[:, :]).then_inc(turned_sb, 1)

                def layer1(t):
                    for a in range(2):
                        K.wait(act, "act", hid1, 2 * t + a + 1)
                        K.wait(act, "act", hid2, 2 * t + a - 1)
                        nc.scalar.activation(x1[:, a, :], hid_ps[:, a, 0:4 * EP], ACT.Silu, bias=b1[:, 0:1]).then_inc(act1, 1)

                def layer2(t, k):
                    for a in range(2):
                        K.wait(act, "act", hid2, 2 * t + a + 1)
                        K.wait(act, "act", tpw, 4 * (t - 1))
                        nc.scalar.activation(x2[k][:, a, :], hid_ps[:, a, 0:4 * EP], ACT.Silu, bias=b2[:, 0:1]).then_inc(act2, 1)
                def widen(t, k, i):
                    K.wait(act, "act", gathered[k], (i + 1) * (16 * CH))
                    K.wait(act, "act", used, t - 1)
                    nc.scalar.copy(zz[k][:, :, 2, :], rows[k][:, :, 0:MUL])
                    K.wait(act, "act", scaled, t + 1)
                    nc.scalar.copy(zv_wide[k][:, :, :, :, :].rearrange("p c i u w -> p (c i u) w"),
                                   zv[k][:, :, :, :].rearrange("p c i u -> p (c i u)").unsqueeze(2).to_broadcast([EP, CH * 3 * MUL, MUL])).then_inc(widened, 1)

                take_turned(0)
                layer1(0)
                layer2(0, 0)
                widen(0, 0, 0)

                def body(i):
                    for k in range(2):
                        t = 2 * i + k
                        more = not known_ge(t, 2 * PAIRS - 1)
                        S.mask(act, t, k)
                        if more:
                            take_turned(t + 1)
                            layer1(t + 1)
                            layer2(t + 1, 1 - k)
                        if not first_chunk(t):
                            S.store(act, t - 1, 1 - k, i - 1 + k)
                        if more:
                            widen(t + 1, 1 - k, i + k)
                pairs(act, body, ahead=True)
                S.store(act, 2 * PAIRS - 1, 1, PAIRS - 1)
                S.finish(act)

            @block.vector
            def _(dve):
                c = Chain(dve, chain_v)
                for ins in S.start():
                    c.link(ins)
                c.restart()

                def sh1(t):
                    return sh[:, cols(t), 1:4].unsqueeze(2).to_broadcast([EP, CH, MUL, 3])

                def prepare(t, k, i):
                    K.wait(dve, "dve", gathered[k], (i + 1) * (16 * CH))
                    hs = rows[k][:, :, 0:MUL]
                    hv = rows[k][:, :, MUL:FEAT].rearrange("p c (u i) -> p c u i", i=3)
                    sh0 = sh[:, cols(t), 0:1]
                    K.wait(dve, "dve", widened, t - 1)
                    nc.vector.tensor_tensor(zv[k][:, :, :, :], hv.rearrange("p c u i -> p c i u"),
                                            sh0.unsqueeze(3).to_broadcast([EP, CH, 3, MUL]), ALU.mult).then_inc(scaled, 1)
                    c.link(nc.vector.tensor_tensor(hv1[:, :, :, :], hv, sh1(t), ALU.mult))
                    c.step(nc.vector.tensor_tensor(zz[k][:, :, 0, :], hs, sh0.to_broadcast([EP, CH, MUL]), ALU.mult))
                    c.step(nc.vector.tensor_reduce(zz[k][:, :, 1, :], hv1[:, :, :, :], AX.X, ALU.add))
                    K.wait(dve, "dve", scaled, t + 1)
                    dve.sem_inc(prepared, 1)

                dve.wait_ge(sh_in, 16)
                prepare(0, 0, 0)
                c.restart()

                def body(i):
                    for k in range(2):
                        t = 2 * i + k
                        if not known_ge(t, 2 * PAIRS - 1):
                            prepare(t + 1, 1 - k, i + k)
                        K.wait(dve, "dve", widened, t + 1)

                        def total(q, done):
                            dve.wait_ge(chain_v, done)
                            K.wait(dve, "dve", taken, 4 * t + q + 1)
                            four = slice(4 * q, 4 * q + 4)
                            c.link(nc.vector.tensor_reduce(res_a[:, four, :, :].rearrange("p c w b -> p (c w b)"),
                                                           prod_a[q % 2][:, :, :, :, :].rearrange("p c w b u -> p (c w b) u"), AX.X, ALU.add))
                            c.link(nc.vector.tensor_reduce(res_b[:, four, :, :].rearrange("p c i w -> p (c i) w"),
                                                           prod_b[q % 2][:, :, :, :, :].rearrange("p c i u w -> p (c i) w u"), AX.X, ALU.add))
                        done = 0
                        for q in range(4):
                            K.wait(dve, "dve", tpw, 4 * t + q + 1)
                            four = slice(4 * q, 4 * q + 4)
                            wts = tp_ps[q % 2][:, :, :].rearrange("p j (o n) -> p (j o) n", o=2)
                            shape = [EP, 4, MUL, 3 * MUL]
                            if q >= 2:
                                dve.wait_ge(chain_v, summed)
                            c.link(nc.vector.tensor_tensor(prod_a[q % 2][:, :, :, :, :].rearrange("p c w b u -> p c w (b u)"),
                                                           wts[:, :, 0:192].rearrange("p c (n w) -> p c w n", w=MUL),
                                                           zz[k][:, four, :, :].rearrange("p c b u -> p c (b u)").unsqueeze(2).to_broadcast(shape), ALU.mult))
                            nc.vector.tensor_tensor(prod_b[q % 2][:, :, :, :, :].rearrange("p c i u w -> p c i (u w)"),
                                                    wts[:, :, 192:256].unsqueeze(2).to_broadcast([EP, 4, 3, MUL * MUL]),
                                                    zv_wide[k][:, four, :, :, :].rearrange("p c i u w -> p c i (u w)"), ALU.mult).then_inc(taken, 1)
                            made = c.n
                            if q:
                                total(q - 1, done)
                                summed = c.n
                            done = made
                        total(3, done)
                        c.join()
                        msg = S.message(k)
                        c.link(nc.vector.tensor_tensor(msg[:, 0:MUL, :], res_a[:, :, :, 0].rearrange("p c w -> p w c"),
                                                       res_a[:, :, :, 1].rearrange("p c w -> p w c"), ALU.add))
                        c.step(nc.vector.tensor_tensor(cross[:, :, :, :], sh1(t), res_a[:, :, :, 2].unsqueeze(3).to_broadcast([EP, CH, MUL, 3]), ALU.mult))
                        dve.sem_inc(used, 1)
                        c.link(nc.vector.tensor_tensor(msg[:, MUL:FEAT, :].rearrange("p (w i) c -> p w i c", i=3),
                                                       cross[:, :, :, :].rearrange("p c w i -> p w i c"),
                                                       res_b[:, :, :, :].rearrange("p c i w -> p w i c"), ALU.add))
                        S.scan(dve, c, t, k)
                        c.restart()
                pairs(dve, body, ahead=True)
        K.recycle()
        segment_ends(sums, FEAT, last_dst, agg)
        masked_add(has_dst, 1.0 / 16)
        with ExitStack() as st:
            w = sb(st, "w_self", [FEAT, FEAT])
            zeroed, loaded = K.sem("zeroed"), K.sem("loaded")
            with nc.Block() as block:
                @block.vector
                def _(dve):
                    nc.vector.memset(w[:, :], 0.0).then_inc(zeroed, 1)

                @block.sync
                def _(sp):
                    sp.wait_ge(zeroed, 1)
                    sp.dma_start(w[0:MUL, 0:MUL], A["L2_gnn_Ws"]).then_inc(loaded, 16)
                    for u in range(MUL):
                        for m in range(3):
                            at = MUL + 3 * u + m
                            sp.dma_start(w[at:at + 1, MUL + m:FEAT:3], A["L2_gnn_Wv"][u:u + 1, :], allow_slow_non_contiguous=True).then_inc(loaded, 16)
                    sp.wait_ge(loaded, 16 * (1 + 3 * MUL))
            K.recycle()

            def put(dve, views, g):
                for j, m, v in views:
                    xs = x[:, bass.ds(g * NG + j, m), :]
                    last = nc.vector.scalar_tensor_tensor(xs, v, MUL ** -0.5, xs, ALU.mult, ALU.add)
                return last
            node_product(h, FEAT, w[:, :], FEAT, put)

        normalize()
        a_src = sb(top, "a_src", [NP, NB, HEADS3])
        first_key = sb(top, "first_key", [EP, 1], I32)
        with ExitStack() as st:
            w = sb(st, "w3h", [FEAT, HEADS3, FEAT])
            fc = sb(st, "fc", [FEAT, 2, FEAT])
            part = sb(st, "part", [FEAT, 2, HEADS3, FEAT])
            w_sd = sb(st, "w_sd3", [FEAT, 2, HEADS3])
            fcb = sb(st, "fcb3", [NP, 1])
            h3 = sb(st, "h3", [NP, NB, FEAT + HEADS3])
            load([(w[:, :, :], A["L3_gnn_w"].rearrange("h f o -> f h o")),
                  (fc[:, :, :].rearrange("p s o -> p (s o)"), on_all(A["L3_gnn_fc_w"][0, :], FEAT)),
                  (fcb[:, :], on_all(A["L3_gnn_fc_b"]))])
            chain_v = K.sem("chain_v")
            with nc.Block() as block:
                @block.vector
                def _(dve):
                    c = Chain(dve, chain_v)
                    for s in range(2):
                        c.link(nc.vector.tensor_tensor(part[:, s, :, :], w[:, :, :], fc[:, s, :].unsqueeze(1).to_broadcast([FEAT, HEADS3, FEAT]), ALU.mult))
                    c.join()
                    c.step(nc.vector.tensor_reduce(w_sd[:, :, :], part[:, :, :, :], AX.X, ALU.add))
                    c.restart()
            K.recycle()

            def put(dve, views, g):
                for j, m, v in views:
                    at = bass.ds(g * NG + j, m)
                    nc.vector.tensor_scalar(a_src[:, at, :], v[:, :, 0:HEADS3], fcb[:, 0:1], None, ALU.add)
                    last = nc.vector.tensor_copy(h3[:, at, FEAT:], v[:, :, HEADS3:])
                return last
            node_product(h, FEAT, w_sd[:, :, :].rearrange("p s h -> p (s h)"), 2 * HEADS3, put)
            with nc.Block() as block:
                @block.vector
                def _(dve):
                    nc.vector.tensor_copy(h3[:, :, 0:FEAT], h[:, :, :])
            store_table([(node_rows(tab_h3), h3[:, :, :]), (node_rows(tab_a3), a_src[:, :, :])])

        with ExitStack() as st:
            key = sb(st, "key_src", [EP, COLS, 2], I32)
            load([(key[:, :, :], edge_rows(by_src)), (first_key[:, :], edge_rows(by_src)[:, 0, 0:1])])
            edge_masks(key[:, :, 0], edge_rows(by_src)[:, 0, 0:1], edge_rows(by_src)[:, COLS - 1, 0:1])

        def attention_ends(target):
            wide = FEAT + 1
            heads = [wide, HEADS3, EP]
            with ExitStack() as st:
                tails = sb(st, "tails", [EP, ATT_ROW])
                ends = sb(st, "ends", [EP, ATT_ROW])
                fixed = sb(st, "fixed", [EP, ATT_ROW])
                both = sb(st, "both", [EP, 2, HEADS3, wide])
                no_carry = sb(st, "no_carry", [wide, EP])
                no_pass = sb(st, "no_pass", [wide, EP])
                tail_top = sb(st, "tail_top", heads)
                carry_top = sb(st, "carry_top", [wide, HEADS3, EP + 1])
                carry = sb(st, "carry", [wide, HEADS3, EP + 1])
                factor = sb(st, "factor", [wide, 2, HEADS3, EP])
                part = sb(st, "part", heads)
                end_rows = sb(st, "end_rows", [EP, HEADS3, wide])
                mix = sb(st, "mix", [EP, 2, HEADS3])
                top_end = sb(st, "top_end", [EP, HEADS3])
                turn = ps(st, "turn", [wide, 2, HEADS3, 128])
                back = ps(st, "back", [EP, 2, 512])
                loaded, arranged, turned, shifted, exped, scanned, backed, mended, chain_v = (K.sem(n) for n in (
                    "loaded", "arranged", "turned", "shifted", "exped", "scanned", "backed", "mended", "chain_v"))
                got, put_back, gathered = (K.own(n) for n in ("got", "put_back", "gathered"))
                block = st.enter_context(nc.Block())

                @block.sync
                def _(sp):
                    sp.dma_start(tails[:, :], edge_rows(sums3)[:, COLS - 1, :]).then_inc(loaded, 16)

                @block.tensor
                def _(pe):
                    pe.wait_ge(arranged, 1)
                    for n in range(2):
                        for j in range(HEADS3):
                            last = nc.tensor.transpose(turn[:, n, j, 0:EP], both[:, n, j, :], ident[0:EP, 0:EP])
                    last.then_inc(turned, 1)
                    pe.wait_ge(scanned, 1)
                    for n, row in enumerate((carry, carry_top)):
                        for j in range(HEADS3):
                            last = nc.tensor.transpose(back[:, n, j * 64:j * 64 + wide], row[:, j, 0:EP], ident[0:wide, 0:wide])
                    last.then_inc(backed, 1)

                @block.scalar
                def _(act):
                    act.wait_ge(shifted, 1)
                    nc.scalar.activation(factor[:, :, :, :], factor[:, :, :, :], ACT.Exp).then_inc(exped, 1)
                    act.wait_ge(shifted, 2)
                    nc.scalar.activation(mix[:, :, :], mix[:, :, :], ACT.Exp).then_inc(exped, 1)

                @block.vector
                def _(dve):
                    c = Chain(dve, chain_v)
                    c.link(nc.vector.tensor_scalar(no_carry[:, :], fwd_row[0:wide, :], BIG, -BIG, ALU.mult, ALU.add))
                    c.link(nc.vector.tensor_scalar(no_pass[:, :], fwd_all[0:wide, :], BIG, -BIG, ALU.mult, ALU.add))
                    c.link(nc.vector.memset(carry_top[:, :, 0], -BIG))
                    c.link(nc.vector.memset(carry[:, :, 0], 0.0))

                    def arrange(target_, rows):
                        c.link(nc.vector.tensor_copy(target_[:, :, 0:FEAT], rows[:, 0:ATT].rearrange("p (h f) -> p h f", h=HEADS3)))
                        c.link(nc.vector.tensor_copy(target_[:, :, FEAT], rows[:, ATT:ATT_SUMS]))
                    dve.wait_ge(loaded, 16)
                    arrange(both[:, 0, :, :], tails)
                    c.link(nc.vector.tensor_copy(both[:, 1, :, :], tails[:, ATT_SUMS:].unsqueeze(2).to_broadcast([EP, HEADS3, wide])))
                    c.join()
                    dve.sem_inc(arranged, 1)
                    dve.wait_ge(turned, 1)
                    c.step(nc.vector.tensor_tensor(tail_top[:, :, :], turn[:, 1, :, 0:EP], no_carry[:, :].unsqueeze(1).to_broadcast(heads), ALU.add))
                    for j in range(HEADS3):
                        c.link(nc.vector.tensor_tensor_scan(carry_top[:, j, 1:EP + 1], no_pass[:, :], tail_top[:, j, :], -BIG, ALU.add, ALU.max))
                    c.join()
                    c.link(nc.vector.tensor_tensor(factor[:, 1, :, :], tail_top[:, :, :], carry_top[:, :, 1:EP + 1], ALU.subtract))
                    c.step(nc.vector.tensor_tensor(factor[:, 0, :, :], carry_top[:, :, 0:EP], no_pass[:, :].unsqueeze(1).to_broadcast(heads), ALU.add))
                    c.step(nc.vector.tensor_tensor(factor[:, 0, :, :], factor[:, 0, :, :], carry_top[:, :, 1:EP + 1], ALU.subtract))
                    dve.sem_inc(shifted, 1)
                    dve.wait_ge(exped, 1)
                    c.step(nc.vector.tensor_tensor(part[:, :, :], factor[:, 1, :, :], turn[:, 0, :, 0:EP], ALU.mult))
                    for j in range(HEADS3):
                        c.link(nc.vector.tensor_tensor_scan(carry[:, j, 1:EP + 1], factor[:, 0, j, :], part[:, j, :], 0.0, ALU.mult, ALU.add))
                    c.join()
                    dve.sem_inc(scanned, 1)
                    dve.wait_ge(backed, 1)
                    dve.wait_ge(got, 16)
                    carried = back[:, 0, 0:HEADS3 * 64].rearrange("p (h f) -> p h f", h=HEADS3)[:, :, 0:wide]
                    carried_top = back[:, 1, 0:HEADS3 * 64].rearrange("p (h f) -> p h f", h=HEADS3)[:, :, 0]
                    end_top = ends[:, ATT_SUMS:]
                    arrange(end_rows, ends)
                    c.step(nc.vector.tensor_tensor(top_end[:, :], carried_top, end_top, ALU.max))
                    c.link(nc.vector.tensor_tensor(mix[:, 0, :], end_top, top_end[:, :], ALU.subtract))
                    c.step(nc.vector.tensor_tensor(mix[:, 1, :], carried_top, top_end[:, :], ALU.subtract))
                    dve.sem_inc(shifted, 1)
                    dve.wait_ge(exped, 2)
                    shape = [EP, HEADS3, wide]
                    c.link(nc.vector.tensor_tensor(end_rows[:, :, :], end_rows[:, :, :], mix[:, 0, :].unsqueeze(2).to_broadcast(shape), ALU.mult))
                    c.step(nc.vector.tensor_tensor(both[:, 0, :, :], carried, mix[:, 1, :].unsqueeze(2).to_broadcast(shape), ALU.mult))
                    c.step(nc.vector.tensor_tensor(end_rows[:, :, :], end_rows[:, :, :], both[:, 0, :, :], ALU.add))
                    c.link(nc.vector.tensor_copy(fixed[:, 0:ATT].rearrange("p (h f) -> p h f", h=HEADS3), end_rows[:, :, 0:FEAT]))
                    c.link(nc.vector.tensor_copy(fixed[:, ATT:ATT_SUMS], end_rows[:, :, FEAT]))
                    c.link(nc.vector.tensor_copy(fixed[:, ATT_SUMS:], top_end[:, :]))
                    c.join()
                    dve.sem_inc(mended, 1)
                    c.restart()

                @block.gpsimd
                def _(pool):
                    pool.indirect_dma_start(ends[:, :], None, sums3, bass.IndirectOffsetOnAxis(ap=endrow[:, 0:1], axis=0)).then_inc(got, 16)
                    pool.wait_ge(mended, 1)
                    pool.wait_ge(loaded, 16)
                    pool.indirect_dma_start(sums3, bass.IndirectOffsetOnAxis(ap=endrow[:, 0:1], axis=0), fixed[:, :], None).then_inc(put_back, 16)
                    pool.wait_ge(put_back, 16)
                    for b in range(NB):
                        pool.indirect_dma_start(target[:, b, :], None, sums3,
                                                bass.IndirectOffsetOnAxis(ap=last_src[:, b:b + 1], axis=0)).then_inc(gathered, 16)
                    pool.wait_ge(gathered, 16 * NB)
            K.recycle()

        with ExitStack() as st:
            idx = [sb(st, f"idx{k}", [EP, CH, 2], I32) for k in range(2)]
            rows = [sb(st, f"hs{k}", [EP, CH, FEAT + HEADS3]) for k in range(2)]
            own = Spread(st, HEADS3, own_rows)
            no_cont = sb(st, "no_cont", [EP, COLS])
            no_cont_h = [sb(st, f"no_cont_h{k}", [EP, HEADS3, CH + 1]) for k in range(2)]
            score = sb(st, "score", [EP, HEADS3, CH + 1])
            score_in = sb(st, "score_in", [EP, HEADS3, CH])
            most = [sb(st, f"most{k}", [EP, HEADS3, CH + 1]) for k in range(2)]
            shift = [sb(st, f"shift{k}", [EP, 2, HEADS3, CH]) for k in range(2)]
            S = SegmentSums(st, ATT_SUMS, sums3, [most[k][:, :, 1:CH + 1].rearrange("p h c -> p c h") for k in range(2)])
            placed = K.own("placed")
            idx_in = [K.sem(f"idx_in{k}") for k in range(2)]
            gathered = [K.own(f"gathered{k}") for k in range(2)]
            masked, shifted, exped, used, started, chain_v = (K.sem(n) for n in ("masked", "shifted", "exped", "used", "started", "chain_v"))
            block = st.enter_context(nc.Block())
            last_chunk = 2 * PAIRS - 1

            @block.sync
            def _(sp):
                def body(i):
                    for k in range(2):
                        t = 2 * i + k
                        K.wait(sp, "sp", gathered[k], i * (16 * CH))
                        sp.dma_start(idx[k][:, :, :], edge_rows(by_src)[:, cols(t), :]).then_inc(idx_in[k], 16)
                pairs(sp, body)

            @block.gpsimd
            def _(pool):
                own.place(pool, lambda b: a_src[:, b, :], first_src, tab_a3, first_key[:, 0:1], placed)

                def body(i):
                    for k in range(2):
                        t = 2 * i + k
                        K.wait(pool, "pool", idx_in[k], i * 16 + 16)
                        K.wait(pool, "pool", used, t - 1)
                        for g in range(CH):
                            pool.indirect_dma_start(rows[k][:, g, :], None, tab_h3,
                                                    bass.IndirectOffsetOnAxis(ap=idx[k][:, g, 1:2], axis=0)).then_inc(gathered[k], 16)
                pairs(pool, body)

            @block.scalar
            def _(act):
                act.wait_ge(placed, own.PLACED)
                act.wait_ge(started, 1)
                own.load(act, 0, 0)
                own.load(act, 1, 1)
                own.lay(act, 0, 0, 0)

                def body(i):
                    for k in range(2):
                        t = 2 * i + k
                        K.wait(act, "act", shifted, t - 1)
                        nc.scalar.copy(no_cont_h[k][:, :, 1:CH + 1],
                                       no_cont[:, cols(t)].unsqueeze(1).to_broadcast([EP, HEADS3, CH])).then_inc(masked, 1)
                        if not known_ge(t, last_chunk):
                            own.lay(act, t + 1, 1 - k, i + k)
                        if not known_ge(t, last_chunk - 1):
                            K.wait(act, "act", own.laid, t + 1)
                            own.load(act, t + 2, k)
                        if not first_chunk(t):
                            S.store(act, t - 1, 1 - k, i - 1 + k)
                        K.wait(act, "act", shifted, t + 1)
                        K.wait(act, "act", S.scanned, t - 1)
                        weight = S.message(k)[:, ATT:ATT_SUMS, :]
                        rescale = S.keep[k][:, ATT:ATT_SUMS, 1:CH + 1]
                        nc.scalar.activation(weight, shift[k][:, 1, :, :], ACT.Exp).then_inc(exped, 1)
                        nc.scalar.activation(rescale, shift[k][:, 0, :, :], ACT.Exp).then_inc(exped, 1)
                        K.wait(act, "act", exped, 2 * t + 2)
                        nc.scalar.copy(S.keep[k][:, 0:ATT, 1:CH + 1].rearrange("p (h f) c -> p h f c", h=HEADS3),
                                       rescale.unsqueeze(2).to_broadcast([EP, HEADS3, FEAT, CH])).then_inc(S.kept, 1)
                pairs(act, body, ahead=True)
                S.store(act, last_chunk, 1, PAIRS - 1)
                S.finish(act)

            @block.vector
            def _(dve):
                c = Chain(dve, chain_v)
                for ins in S.start():
                    c.link(ins)
                c.link(nc.vector.tensor_scalar(no_cont[:, :], cont[:, :], BIG, -BIG, ALU.mult, ALU.add))
                for k in range(2):
                    c.link(nc.vector.memset(no_cont_h[k][:, :, 0], -BIG))
                c.link(nc.vector.memset(most[1][:, :, CH], -BIG))
                dve.wait_ge(placed, own.PLACED)
                for ins in own.start():
                    c.link(ins)
                c.join()
                dve.sem_inc(started, 1)
                c.restart()

                def body(i):
                    for k in range(2):
                        t = 2 * i + k
                        own.scan(dve, c, t, k)
                        K.wait(dve, "dve", gathered[k], (i + 1) * (16 * CH))
                        now, before_ = most[k][:, :, 1:CH + 1], most[k][:, :, 0:CH]
                        c.link(nc.vector.tensor_copy(score[:, :, 0], most[1 - k][:, :, CH]))
                        c.step(nc.vector.tensor_tensor(score_in[:, :, :], own.rows(k).rearrange("p c h -> p h c"),
                                                       rows[k][:, :, FEAT:].rearrange("p c h -> p h c"), ALU.add))
                        c.step(nc.vector.scalar_tensor_tensor(score[:, :, 1:CH + 1], score_in[:, :, :], 0.2, score_in[:, :, :], ALU.mult, ALU.max))
                        K.wait(dve, "dve", masked, t + 1)
                        K.wait(dve, "dve", S.copied, t - 1)
                        flat = lambda ap: ap[:, :, :].rearrange("p h c -> p (h c)")
                        c.step(nc.vector.tensor_tensor_scan(flat(most[k]), flat(no_cont_h[k]), flat(score), -BIG, ALU.add, ALU.max))
                        c.link(nc.vector.tensor_tensor(shift[k][:, 1, :, :], score[:, :, 1:CH + 1], now, ALU.subtract))
                        c.step(nc.vector.tensor_tensor(shift[k][:, 0, :, :], before_, no_cont_h[k][:, :, 1:CH + 1], ALU.add))
                        c.step(nc.vector.tensor_tensor(shift[k][:, 0, :, :], shift[k][:, 0, :, :], now, ALU.subtract))
                        dve.sem_inc(shifted, 1)
                        K.wait(dve, "dve", exped, 2 * t + 1)
                        shape = [EP, HEADS3, FEAT, CH]
                        c.step(nc.vector.tensor_tensor(S.message(k)[:, 0:ATT, :].rearrange("p (h f) c -> p h f c", h=HEADS3),
                                                       rows[k][:, :, 0:FEAT].rearrange("p c f -> p f c").unsqueeze(1).to_broadcast(shape),
                                                       S.message(k)[:, ATT:ATT_SUMS, :].unsqueeze(2).to_broadcast(shape), ALU.mult))
                        dve.sem_inc(used, 1)
                        S.scan(dve, c, t, k)
                        c.restart()
                pairs(dve, body)
        K.recycle()

        with ExitStack() as st:
            agg3 = sb(st, "agg3", [NP, NB, ATT_ROW])
            share = sb(st, "share", [NP, NB, HEADS3])
            attention_ends(agg3)
            w = sb(st, "w_out", [HEADS3 * FEAT, FEAT])
            bias = sb(st, "b_out", [NP, FEAT])
            load([(w[:, :], A["L3_gnn_w"].rearrange("h f o -> (h f) o")), (bias[:, :], on_all(A["L3_gnn_bias"]))])
            chain_v = K.sem("chain_v")
            with nc.Block() as block:
                @block.vector
                def _(dve):
                    c = Chain(dve, chain_v)
                    weighted = agg3[:, :, 0:ATT].rearrange("p b (h f) -> p b h f", h=HEADS3)
                    c.step(nc.vector.reciprocal(share[:, :, :], agg3[:, :, ATT:ATT_SUMS]))
                    c.step(nc.vector.tensor_tensor(share[:, :, :], share[:, :, :], has_src[:, :].unsqueeze(2).to_broadcast([NP, NB, HEADS3]), ALU.mult))
                    c.link(nc.vector.tensor_tensor(weighted, weighted, share[:, :, :].unsqueeze(3).to_broadcast([NP, NB, HEADS3, FEAT]), ALU.mult))
                    c.link(nc.vector.tensor_tensor(x[:, :, :], x[:, :, :], bias[:, :].unsqueeze(1).to_broadcast([NP, NB, FEAT]), ALU.add))
                    c.restart()
            K.recycle()

            def put(dve, views, g):
                for j, m, v in views:
                    xs = x[:, bass.ds(g * NG + j, m), :]
                    last = nc.vector.scalar_tensor_tensor(xs, v, 1.0 / HEADS3, xs, ALU.mult, ALU.add)
                return last
            node_product(agg3[:, :, 0:ATT], ATT, w[:, :], FEAT, put)
        full = (NB - 1) * NP
        store_table([(out[0:full, :].rearrange("(b l) f -> l b f", l=NP), x[:, 0:NB - 1, :]),
                     (out[full:NODES, :], x[0:TAIL, NB - 1, :])])


_INS = ['x', 'src', 'dst', 'edge_attr3_2x32', 'edge_attr_4', 'edge_attr_8', 'L0_gnn_W1', 'L0_gnn_b1', 'L0_gnn_W2s', 'L0_gnn_b2s',
        'L0_gnn_W2d', 'L0_gnn_b2d', 'L0_gnn_attn', 'L2_gnn_W1', 'L2_gnn_b1', 'L2_gnn_W2', 'L2_gnn_b2', 'L2_gnn_W3', 'L2_gnn_b3',
        'L2_gnn_Ws', 'L2_gnn_Wv', 'L3_gnn_w', 'L3_gnn_fc_w', 'L3_gnn_fc_b', 'L3_gnn_bias']


def kernel(**inputs):
    import numpy as _np
    import concourse.bacc as _bacc
    from concourse import mybir as _mybir
    from concourse.bass_utils import run_bass_kernel_spmd as _run

    nc = _bacc.Bacc("TRN2", target_bir_lowering=False, num_devices=1)
    arrays, args = {}, {}
    for name in _INS:
        a = _np.ascontiguousarray(inputs[name])
        arrays[f"in_{name}"] = a
        args[name] = nc.dram_tensor(f"in_{name}", a.shape, _mybir.dt.from_np(a.dtype), kind="ExternalInput").ap()
    out = nc.dram_tensor("out_x", (NODES, FEAT), F32, kind="ExternalOutput").ap()
    build(nc, args, out)
    r = _run(nc, [arrays], core_ids=[0])
    return r.results[0]["out_x"]
```

```python
import concourse.bass as bass
from concourse import mybir
from contextlib import ExitStack

F32 = mybir.dt.float32
I32 = mybir.dt.int32
BF16 = mybir.dt.bfloat16
ALU = mybir.AluOpType
ACT = mybir.ActivationFunctionType
AX = mybir.AxisListType

NODES, EDGES, FEAT = 12500, 200000, 32
EP = 125
COLS = EDGES // EP
CH = 16
PAIRS = COLS // (2 * CH)
NP = 128
NB = -(-NODES // NP)
TAIL = NODES - (NB - 1) * NP
NPAD = NB * NP
GR = 4
GROUPS = CH // GR
BIG = 1.0e30
HEADS0, HEADS3 = 2, 4
ATT = HEADS3 * FEAT
ATT_SUMS = ATT + HEADS3
ATT_ROW = ATT_SUMS + HEADS3


class Chain:

    def __init__(self, eng, sem):
        self.eng, self.sem, self.n = eng, sem, 0

    def link(self, ins):
        self.n += 1
        return ins.then_inc(self.sem, 1)

    def mark(self, ins):
        self.link(ins)
        return self.n

    def until(self, n):
        self.eng.wait_ge(self.sem, n)

    def join(self):
        self.eng.wait_ge(self.sem, self.n)

    def step(self, ins):
        self.link(ins)
        self.join()

    def restart(self):
        if self.n:
            self.join()
            self.eng.sem_clear(self.sem)
            self.n = 0


class Kernel:

    def __init__(self, nc, stack):
        self.nc, self.stack, self.sems, self.used, self.owned = nc, stack, {}, [], 0

    def sem(self, name):
        if name not in self.sems:
            self.sems[name] = self.stack.enter_context(self.nc.semaphore(name))
        if name not in self.used:
            self.used.append(name)
        return self.sems[name]

    def own(self, name):
        self.owned += 1
        return self.stack.enter_context(self.nc.semaphore(f"{name}_{self.owned}"))

    def recycle(self):
        names, self.used = self.used, []
        with self.nc.Block() as block:
            @block.sync
            def _(sp):
                for name in names:
                    sp.sem_clear(self.sems[name])

    def wait(self, eng, who, sem, value):
        if isinstance(value, int):
            if value > 0:
                eng.wait_ge(sem, value)
            return
        eng.wait_ge(sem, value)
        eng.sem_inc(self.sem("tick_" + who), 1)


def pairs(eng, body, first=0, end=PAIRS, ahead=False):
    if first == 0:
        body(0)
        first = 1
    with eng.Fori(first, end - ahead) as i:
        body(i)
    if ahead:
        body(end - 1)


def known_ge(t, n):
    return isinstance(t, int) and t >= n


def first_chunk(t):
    return isinstance(t, int) and t == 0


def first_pair(t):
    return isinstance(t, int) and t < 2


def cols(t):
    return bass.ds(t * CH, CH)


def build(nc, A, out):
    top = ExitStack()
    with top:
        K = Kernel(nc, top)

        names = {}

        def once(name):
            names[name] = names.get(name, 0) + 1
            return name if names[name] == 1 else f"{name}_{names[name]}"

        def sb(stack, name, shape, dt=F32):
            return stack.enter_context(nc.sbuf_tensor(once(name), shape, dt))

        def ps(stack, name, shape, dt=F32):
            return stack.enter_context(nc.psum_tensor(once(name), shape, dt))

        def dram(name, shape, dt=F32):
            return nc.dram_tensor(name, shape, dt, kind="Internal").ap()

        x = sb(top, "x", [NP, NB, FEAT])
        h = sb(top, "h", [NP, NB, FEAT])
        ident = sb(top, "ident", [128, 128])
        identb = sb(top, "identb", [128, 128], BF16)
        ones = sb(top, "ones", [128, 128])
        before = sb(top, "before", [128, 128])
        iota_row = sb(top, "iota_row", [128, 128], BF16)
        pbase = sb(top, "pbase", [128, 1])
        node_of = sb(top, "node_of", [NP, NB])
        zbias = sb(top, "zbias", [NP, 128])
        zeros = sb(top, "zeros", [EP, 640])
        src_i = sb(top, "src_i", [EP, COLS], I32)
        dst_i = sb(top, "dst_i", [EP, COLS], I32)
        last_dst = sb(top, "last_dst", [NP, NB], I32)
        has_dst = sb(top, "has_dst", [NP, NB])
        first_dst = sb(top, "first_dst", [NP, NB], I32)
        first_src = sb(top, "first_src", [NP, NB], I32)
        last_src = sb(top, "last_src", [NP, NB], I32)
        has_src = sb(top, "has_src", [NP, NB])
        base_src = sb(top, "base_src", [NP, NB])

        tab_s0 = dram("tab_s0", (NPAD, 64))
        tab_d0 = dram("tab_d0", (NPAD, 64))
        tab_h = dram("tab_h", (NPAD, FEAT))
        tab_h3 = dram("tab_h3", (NPAD, FEAT + HEADS3))
        tab_a3 = dram("tab_a3", (NPAD, HEADS3))
        en_rows = dram("en_rows", (EDGES, 64))
        ev_rows = dram("ev_rows", (EDGES + NPAD, 64))
        own_rows = dram("own_rows", (EDGES + NPAD, HEADS3))
        sums = dram("sums", (EDGES, FEAT))
        sums3 = dram("sums3", (EDGES, ATT_ROW))
        by_src = dram("by_src", (EDGES, 2), I32)

        def edge_rows(ap):
            if len(ap.shape) == 1:
                return ap.rearrange("(p c) -> p c", p=EP)
            if len(ap.shape) == 2:
                return ap.rearrange("(p c) f -> p c f", p=EP)
            return ap.rearrange("(p c) h f -> p c h f", p=EP)

        def node_rows(ap):
            return ap.rearrange("(b l) f -> l b f", l=NP)

        with ExitStack() as st:
            iota_i = sb(st, "iota_i", [128, 128], I32)
            pbase_i = sb(st, "pbase_i", [128, 1], I32)
            node_i = sb(st, "node_i", [NP, NB], I32)
            loaded, made, iotas = K.sem("loaded"), K.sem("made"), K.sem("iotas")
            chain_v, chain_p = K.sem("chain_v"), K.sem("chain_p")
            zeroed = K.sem("zeroed")
            block = st.enter_context(nc.Block())

            @block.sync
            def _(sp):
                sp.dma_start(src_i[:, :], edge_rows(A["src"])).then_inc(loaded, 16)
                sp.dma_start(dst_i[:, :], edge_rows(A["dst"])).then_inc(loaded, 16)
                full = (NB - 1) * NP
                sp.dma_start(x[:, 0:NB - 1, :], A["x"][0:full, :].rearrange("(b l) f -> l b f", l=NP)).then_inc(loaded, 16)
                sp.wait_ge(zeroed, 1)
                sp.dma_start(x[0:TAIL, NB - 1, :], A["x"][full:NODES, :]).then_inc(loaded, 16)
                sp.wait_ge(loaded, 64)

            @block.gpsimd
            def _(pool):
                c = Chain(pool, chain_p)
                nc.gpsimd.iota(iota_i[:, :], [[1, 128]], base=0, channel_multiplier=0).then_inc(iotas, 1)
                nc.gpsimd.iota(pbase_i[:, :], [[0, 1]], base=0, channel_multiplier=COLS).then_inc(iotas, 1)
                nc.gpsimd.iota(node_i[:, :], [[NP, NB]], base=0, channel_multiplier=1).then_inc(iotas, 1)
                c.link(nc.gpsimd.memset(ident[:, :], 0.0))
                c.step(nc.gpsimd.memset(before[:, :], 0.0))
                nc.gpsimd.affine_select(out=ident[:, :], in_=ident[:, :], compare_op=ALU.not_equal, fill=1.0,
                                        base=0, pattern=[[-1, 128]], channel_multiplier=1).then_inc(made, 1)
                nc.gpsimd.affine_select(out=before[:, :], in_=before[:, :], compare_op=ALU.is_ge, fill=1.0,
                                        base=0, pattern=[[-1, 128]], channel_multiplier=1).then_inc(made, 1)
                c.restart()

            @block.vector
            def _(dve):
                nc.vector.memset(zeros[:, :], 0.0)
                nc.vector.memset(x[:, NB - 1, :], 0.0).then_inc(zeroed, 1)
                nc.vector.memset(zbias[:, :], 0.0)
                nc.vector.memset(ones[:, :], 1.0)
                dve.wait_ge(iotas, 3)
                nc.vector.tensor_copy(node_of[:, :], node_i[:, :])
                nc.vector.tensor_copy(iota_row[:, :], iota_i[:, :])
                nc.vector.tensor_copy(pbase[:, :], pbase_i[:, :])
                dve.wait_ge(made, 2)
                nc.vector.tensor_copy(identb[:, :], ident[:, :])
        K.recycle()

        class EdgeMasks:

            def __init__(self, name, first_keys, last_keys):
                self.first_keys, self.last_keys = first_keys, last_keys
                self.cont = sb(top, "cont_" + name, [EP, COLS])
                self.endrow = sb(top, "endrow_" + name, [EP, 1], I32)
                self.fwd_row = sb(top, "fwd_row_" + name, [128, EP])
                self.fwd_all = sb(top, "fwd_all_" + name, [128, EP])

            def scratch(self, st, ends=None):
                self.ends = ends
                self.first_seg = ends.first_seg if ends else sb(st, "first_seg", [EP, COLS])
                self.key = sb(st, "key", [EP, COLS])
                self.nxt_i = sb(st, "nxt_i", [EP, 1], I32)
                self.nxt = sb(st, "nxt", [EP, 1])
                self.prv_i = sb(st, "prv_i", [EP, 1], I32)
                self.prv = sb(st, "prv", [EP, 1])
                self.goes_on = sb(st, "goes_on", [EP, 4])
                self.length = sb(st, "length", [EP, 1])
                self.diag = sb(st, "diag", [EP, 2, EP])
                self.rows = ps(st, "rows", [128, 2, 512])
                self.edge_in, self.filled, self.diags, self.rowed = (K.sem(n) for n in ("edge_in", "edge_filled", "edge_diags", "edge_rowed"))

            def load(self, sp):
                sp.wait_ge(self.filled, 1)
                sp.dma_start(self.nxt_i[0:EP - 1, :], self.first_keys[1:EP, :], allow_slow_non_contiguous=True).then_inc(self.edge_in, 16)
                sp.dma_start(self.prv_i[1:EP, :], self.last_keys[0:EP - 1, :], allow_slow_non_contiguous=True).then_inc(self.edge_in, 16)

            def turn(self, pe):
                pe.wait_ge(self.diags, 2)
                for k in range(2):
                    nc.tensor.matmul(self.rows[:, k, 0:EP], ones[0:EP, :], self.diag[:, k, :], start=True, stop=True).then_inc(self.rowed, 1)

            def make(self, dve, c, key_i):
                cont, key, first_seg, length, rows, ends = self.cont, self.key, self.first_seg, self.length, self.rows, self.ends
                c.step(nc.vector.memset(self.prv_i[:, :], -1))
                nc.vector.memset(self.nxt_i[:, :], -1).then_inc(self.filled, 1)
                c.step(nc.vector.tensor_copy(key[:, :], key_i))
                c.step(nc.vector.tensor_tensor(cont[:, 1:COLS], key[:, 1:COLS], key[:, 0:COLS - 1], ALU.is_equal))
                c.link(nc.vector.memset(first_seg[:, 0:1], 1.0))
                c.link(nc.vector.tensor_tensor_scan(first_seg[:, 1:COLS], cont[:, 1:COLS], cont[:, 1:COLS], 1.0, ALU.mult, ALU.min))
                if ends:
                    c.link(nc.vector.memset(ends.last_seg[:, COLS - 1:COLS], 1.0))
                    c.link(nc.vector.tensor_tensor_scan(ends.last_seg[:, 0:COLS - 1][:, ::-1], cont[:, 1:COLS][:, ::-1], cont[:, 1:COLS][:, ::-1],
                                                        1.0, ALU.mult, ALU.min))
                c.join()
                c.step(nc.vector.reduce_sum(length[:, :], first_seg[:, :], axis=AX.X))
                c.step(nc.vector.scalar_tensor_tensor(length[:, :], length[:, :], -1.0, pbase[0:EP, :], ALU.add, ALU.add))
                c.link(nc.vector.tensor_copy(self.endrow[:, :], length[:, :]))
                dve.wait_ge(self.edge_in, 32)
                c.link(nc.vector.tensor_copy(self.prv[:, :], self.prv_i[:, :]))
                c.step(nc.vector.tensor_copy(self.nxt[:, :], self.nxt_i[:, :]))
                c.link(nc.vector.tensor_tensor(cont[:, 0:1], key[:, 0:1], self.prv[:, :], ALU.is_equal))
                c.step(nc.vector.tensor_tensor(self.goes_on[:, 0:1], key[:, COLS - 1:COLS], self.nxt[:, :], ALU.is_equal))
                nc.vector.tensor_scalar(self.diag[:, 0, :], ident[0:EP, 0:EP], self.goes_on[:, 0:1], None, ALU.mult).then_inc(self.diags, 1)
                nc.vector.tensor_scalar(self.diag[:, 1, :], ident[0:EP, 0:EP], first_seg[:, COLS - 1:COLS], None, ALU.mult).then_inc(self.diags, 1)
                dve.wait_ge(self.rowed, 2)
                c.step(nc.vector.tensor_copy(self.fwd_row[:, :], rows[:, 0, 0:EP]))
                c.step(nc.vector.tensor_tensor(self.fwd_all[:, :], self.fwd_row[:, :], rows[:, 1, 0:EP], ALU.mult))
                if ends:
                    c.link(nc.vector.memset(ends.bwd_row[:, 0:1], 0.0))
                    c.step(nc.vector.tensor_copy(ends.bwd_row[:, 1:EP], rows[:, 0, 0:EP - 1]))
                    c.step(nc.vector.tensor_tensor(ends.bwd_all[:, :], ends.bwd_row[:, :], rows[:, 1, 0:EP], ALU.mult))

        class SegmentEnds:

            def __init__(self, st):
                self.first_seg = sb(st, "first_seg", [EP, COLS])
                self.last_seg = sb(st, "last_seg", [EP, COLS])
                self.bwd_row = sb(st, "bwd_row", [128, EP])
                self.bwd_all = sb(st, "bwd_all", [128, EP])

        by_dst = EdgeMasks("dst", edge_rows(A["dst"])[:, 0:1], edge_rows(A["dst"])[:, COLS - 1:COLS])
        by_key = edge_rows(by_src)
        by_src_masks = EdgeMasks("src", by_key[:, 0, 0:1], by_key[:, COLS - 1, 0:1])

        SET = 14
        SETS = NB // SET
        sums_in = [K.own(f"sums_in{g}") for g in range(SETS)]
        sum_rounds = []

        def node_stage(begin, finish, n_out=FEAT, operand=None, weights=None, gather=None, normal=None, then=None, stores=None):
            wide = operand is not None and operand.shape[2] == 128
            if gather:
                sum_rounds.append(1)
            with ExitStack() as st:
                products = [(operand, weights, n_out)] if weights is not None else []
                if then:
                    products.append((h, then[0], then[1]))
                pieces = [(b, 1) for b in range(SET)] if wide else [(b, min(4, SET - b)) for b in range(0, SET, 4)]
                spread_w, turned_ps, turned, prod = [], [], [], []
                for n, (_, _, outs) in enumerate(products):
                    spread_w.append(None if wide else sb(st, f"spread_w{n}", [128, 4 * outs]))
                    turned_ps.append(ps(st, f"turned_ps{n}", [128, len(pieces), 128]))
                    turned.append(sb(st, f"turned{n}", [128, len(pieces), 128]))
                    prod.append(ps(st, f"prod{n}", [NP, -(-SET * outs // 512) * 512]))
                if normal:
                    d = sb(st, "d", [NP, SET, FEAT])
                    sq = sb(st, "sq", [NP, SET, FEAT])
                    mean = sb(st, "mean", [NP, SET])
                    var = sb(st, "var", [NP, SET])
                    std = sb(st, "std", [NP, SET])
                spread_in, zeroed, begun, varied, rooted, renewed, done, stored, chain_v = (K.sem(n) for n in (
                    "spread_in", "zeroed", "begun", "varied", "rooted", "renewed", "done", "stored0", "chain_v"))
                n_turned, n_copied, n_prod, n_taken = ([K.sem(f"{n}{k}") for k in range(2)] for n in ("n_turned", "n_copied", "n_prod", "n_taken"))
                block = st.enter_context(nc.Block())
                sets = [slice(g * SET, (g + 1) * SET) for g in range(SETS)]

                def small(ap):
                    return ap[:, :].unsqueeze(2).to_broadcast([NP, SET, FEAT])

                @block.sync
                def _(sp):
                    if products and not wide:
                        sp.wait_ge(zeroed, 1)
                        for n, (_, w, outs) in enumerate(products):
                            for q in range(4):
                                sp.dma_start(spread_w[n][q * FEAT:(q + 1) * FEAT, q * outs:(q + 1) * outs], w).then_inc(spread_in, 16)
                    sent = 0
                    for g, at in enumerate(sets):
                        if stores:
                            sp.wait_ge(done, g + 1)
                            for target, source in stores(at):
                                sp.dma_start(target, source).then_inc(stored, 16)
                                sent += 1
                    if sent:
                        sp.wait_ge(stored, 16 * sent)

                @block.gpsimd
                def _(pool):
                    if gather:
                        table, rows, target = gather
                        for g in range(SETS):
                            for b in range(g * SET, (g + 1) * SET):
                                pool.indirect_dma_start(target[:, b, :], None, table,
                                                        bass.IndirectOffsetOnAxis(ap=rows[:, b:b + 1], axis=0)).then_inc(sums_in[g], 16)
                        for g in range(SETS):
                            pool.wait_ge(sums_in[g], 16 * SET * len(sum_rounds))

                @block.tensor
                def _(pe):
                    if products and not wide:
                        pe.wait_ge(spread_in, 64 * len(products))
                    for g, at in enumerate(sets):
                        for n, (source, w, outs) in enumerate(products):
                            pe.wait_ge(renewed if n else begun, g + 1)
                            if g:
                                pe.wait_ge(n_copied[n], g)
                            for q, (b, m) in enumerate(pieces):
                                piece = source[:, at.start + b, :] if wide else source[:, at.start + b:at.start + b + m, :].rearrange("p b f -> p (b f)")
                                last = nc.tensor.transpose(turned_ps[n][0:128 if wide else m * FEAT, q, :], piece, ident[:, :])
                            last.then_inc(n_turned[n], 1)
                            pe.wait_ge(n_copied[n], g + 1)
                            if g:
                                pe.wait_ge(n_taken[n], g)
                            for q, (b, m) in enumerate(pieces):
                                k = 128 if wide else m * FEAT
                                last = nc.tensor.matmul(prod[n][:, b * outs:(b + m) * outs], turned[n][0:k, q, :],
                                                        w if wide else spread_w[n][0:k, 0:m * outs], start=True, stop=True)
                            last.then_inc(n_prod[n], 1)

                @block.scalar
                def _(act):
                    def root(g):
                        act.wait_ge(varied, g + 1)
                        nc.scalar.activation(std[:, :], var[:, :], ACT.Sqrt).then_inc(rooted, 1)

                    def copy(n, g):
                        act.wait_ge(n_turned[n], g + 1)
                        if g:
                            act.wait_ge(n_prod[n], g)
                        full = [q for q, (b, m) in enumerate(pieces) if wide or m == 4]
                        if len(full) < len(pieces):
                            part = pieces[-1][1] * FEAT
                            nc.scalar.copy(turned[n][0:part, len(full), :], turned_ps[n][0:part, len(full), :])
                        nc.scalar.copy(turned[n][:, 0:len(full), :], turned_ps[n][:, 0:len(full), :]).then_inc(n_copied[n], 1)

                    for g in range(SETS):
                        if normal == "before":
                            root(g)
                        if weights is not None:
                            copy(0, g)
                        if normal == "after":
                            root(g)
                        if then:
                            copy(1, g)

                @block.vector
                def _(dve):
                    c = Chain(dve, chain_v)
                    if products and not wide:
                        for w in spread_w:
                            c.link(nc.vector.memset(w[:, :], 0.0))
                        c.join()
                        dve.sem_inc(zeroed, 1)

                    def normalize(g, at):
                        c.step(nc.vector.reduce_sum(mean[:, :], x[:, at, :], axis=AX.X))
                        c.step(nc.vector.tensor_scalar(mean[:, :], mean[:, :], 1.0 / FEAT, None, ALU.mult))
                        c.step(nc.vector.tensor_tensor(d[:, :, :], x[:, at, :], small(mean), ALU.subtract))
                        c.step(nc.vector.tensor_tensor(sq[:, :, :], d[:, :, :], d[:, :, :], ALU.mult))
                        c.step(nc.vector.reduce_sum(var[:, :], sq[:, :, :], axis=AX.X))
                        nc.vector.tensor_scalar(var[:, :], var[:, :], 1.0 / FEAT, 1e-5, ALU.mult, ALU.add).then_inc(varied, 1)
                        dve.wait_ge(rooted, g + 1)
                        c.step(nc.vector.reciprocal(mean[:, :], std[:, :]))
                        c.step(nc.vector.scalar_tensor_tensor(h[:, at, :], d[:, :, :], 0.0, small(mean), ALU.max, ALU.mult))

                    def before_product(g):
                        if gather:
                            dve.wait_ge(sums_in[g], 16 * SET * len(sum_rounds))
                        if normal == "before":
                            normalize(g, sets[g])
                        begin(c, sets[g])
                        c.join()
                        dve.sem_inc(begun, 1)

                    def product_of(n, g, outs):
                        dve.wait_ge(n_prod[n], g + 1)
                        return prod[n][:, 0:SET * outs].rearrange("p (b o) -> p b o", o=outs)

                    before_product(0)
                    for g, at in enumerate(sets):
                        if g + 1 < SETS:
                            before_product(g + 1)
                        if weights is not None:
                            finish(c, at, product_of(0, g, n_out))
                            c.join()
                            dve.sem_inc(n_taken[0], 1)
                        if normal == "after":
                            normalize(g, at)
                        if then:
                            dve.sem_inc(renewed, 1)
                            then[2](c, at, product_of(1, g, then[1]))
                            c.join()
                            dve.sem_inc(n_taken[1], 1)
                        dve.sem_inc(done, 1)
                    c.restart()
            K.recycle()

        def mend_sums(table, width):
            final = edge_rows(table)[:, COLS - 1, :]
            with ExitStack() as st:
                tails = sb(st, "tails", [EP, width])
                tails_t = sb(st, "tails_t", [width, EP])
                carry_t = sb(st, "carry_t", [width, EP + 1])
                ends = sb(st, "ends", [EP, width])
                fixed = sb(st, "fixed", [EP, width])
                turn = ps(st, "turn", [width, EP])
                back = ps(st, "back", [EP, width])
                loaded, turned, scanned, backed, mended, chain_v = (K.sem(n) for n in (
                    "loaded", "turned", "scanned", "backed", "mended", "chain_v"))
                got, put_back = (K.own(n) for n in ("got", "put_back"))
                block = st.enter_context(nc.Block())

                @block.sync
                def _(sp):
                    sp.dma_start(tails[:, :], final).then_inc(loaded, 16)

                @block.tensor
                def _(pe):
                    pe.wait_ge(loaded, 16)
                    nc.tensor.transpose(turn[:, :], tails[:, :], ident[0:EP, 0:EP]).then_inc(turned, 1)
                    pe.wait_ge(scanned, 1)
                    nc.tensor.transpose(back[:, :], carry_t[:, 0:EP], ident[0:width, 0:width]).then_inc(backed, 1)

                @block.vector
                def _(dve):
                    c = Chain(dve, chain_v)
                    dve.wait_ge(turned, 1)
                    c.link(nc.vector.memset(carry_t[:, 0:1], 0.0))
                    c.step(nc.vector.tensor_tensor(tails_t[:, :], turn[:, :], by_dst.fwd_row[0:width, :], ALU.mult))
                    nc.vector.tensor_tensor_scan(carry_t[:, 1:EP + 1], by_dst.fwd_all[0:width, :], tails_t[:, :], 0.0,
                                                 ALU.mult, ALU.add).then_inc(scanned, 1)
                    dve.wait_ge(backed, 1)
                    dve.wait_ge(got, 16)
                    nc.vector.tensor_tensor(fixed[:, :], back[:, :], ends[:, :], ALU.add).then_inc(mended, 1)
                    c.restart()

                @block.gpsimd
                def _(pool):
                    pool.indirect_dma_start(ends[:, :], None, table, bass.IndirectOffsetOnAxis(ap=by_dst.endrow[:, 0:1], axis=0)).then_inc(got, 16)
                    pool.wait_ge(mended, 1)
                    pool.wait_ge(loaded, 16)
                    pool.indirect_dma_start(table, bass.IndirectOffsetOnAxis(ap=by_dst.endrow[:, 0:1], axis=0), fixed[:, :], None).then_inc(put_back, 16)
                    pool.wait_ge(put_back, 16)
            K.recycle()

        class SegmentSums:

            def __init__(self, st, width, table, beside=None):
                self.width, self.table, self.beside = width, edge_rows(table), beside
                self.fresh = [sb(st, f"fresh{k}", [EP, width, CH + 1]) for k in range(2)]
                self.keep = [sb(st, f"keep{k}", [EP, width, CH + 1]) for k in range(2)]
                self.run = [sb(st, f"run{k}", [EP, width, CH + 1]) for k in range(2)]
                self.rows = [sb(st, f"rows{k}", [EP, CH, table.shape[1]]) for k in range(2)]
                self.kept, self.scanned, self.copied = K.sem("kept"), K.sem("scanned"), K.sem("copied")
                self.stored = [K.sem(f"stored{k}") for k in range(2)]

            def message(self, k):
                return self.fresh[k][:, :, 1:CH + 1]

            def start(self):
                for k in range(2):
                    last = nc.vector.memset(self.keep[k][:, :, 0], 0.0)
                return [last, nc.vector.memset(self.run[1][:, :, CH], 0.0)]

            def mask(self, act, t, k):
                K.wait(act, "act", self.scanned, t - 1)
                flags = by_dst.cont[:, cols(t)].unsqueeze(1).to_broadcast([EP, self.width, CH])
                nc.scalar.copy(self.keep[k][:, :, 1:CH + 1], flags).then_inc(self.kept, 1)

            def carry(self, c, k):
                return c.mark(nc.vector.tensor_copy(self.fresh[k][:, :, 0], self.run[1 - k][:, :, CH]))

            def scan(self, dve, c, t, k, carried=False, settle=True):
                if not carried:
                    self.carry(c, k)
                if settle:
                    c.join()
                K.wait(dve, "dve", self.kept, t + 1)
                K.wait(dve, "dve", self.copied, t - 1)
                flat = lambda ap: ap[:, :, :].rearrange("p f c -> p (f c)")
                nc.vector.tensor_tensor_scan(flat(self.run[k]), flat(self.keep[k]), flat(self.fresh[k]), 0.0,
                                             ALU.mult, ALU.add).then_inc(self.scanned, 1)
                if settle:
                    K.wait(dve, "dve", self.scanned, t + 1)

            def store(self, act, t, k, i):
                K.wait(act, "act", self.scanned, t + 1)
                K.wait(act, "act", self.stored[k], i * 16)
                if self.beside:
                    nc.scalar.copy(self.rows[k][:, :, self.width:], self.beside[k])
                nc.scalar.copy(self.rows[k][:, :, 0:self.width], self.run[k][:, :, 1:CH + 1].rearrange("p f c -> p c f")).then_inc(self.copied, 1)
                K.wait(act, "act", self.copied, t + 1)
                act.dma_start(self.table[:, cols(t), :], self.rows[k][:, :, :]).then_inc(self.stored[k], 16)

            def finish(self, act):
                for k in range(2):
                    act.wait_ge(self.stored[k], 16 * PAIRS)

        class Spread:

            def __init__(self, st, width, table, masks):
                self.masks = masks
                self.width, self.whole, self.table = width, table, edge_rows(table[0:EDGES, :])
                self.raw = [sb(st, f"raw{k}", [EP, CH, width]) for k in range(2)]
                self.fresh = [sb(st, f"sfresh{k}", [EP, width, CH + 1]) for k in range(2)]
                self.keep = [sb(st, f"skeep{k}", [EP, width, CH + 1]) for k in range(2)]
                self.run = [sb(st, f"srun{k}", [EP, width, CH + 1]) for k in range(2)]
                self.init = sb(st, "sinit", [EP, width])
                self.raw_in = [K.sem(f"raw_in{k}") for k in range(2)]
                self.laid, self.spread = K.sem("spread_laid"), K.sem("spread_done")

            def rows(self, k):
                return self.run[k][:, :, 1:CH + 1].rearrange("p f c -> p c f")

            def place(self, pool, nodes, first_rows, table_of_nodes, first_key, scattered):
                for b in range(NB):
                    pool.indirect_dma_start(self.whole, bass.IndirectOffsetOnAxis(ap=first_rows[:, b:b + 1], axis=0),
                                            nodes(b), None).then_inc(scattered, 16)
                pool.indirect_dma_start(self.init[:, :], None, table_of_nodes,
                                        bass.IndirectOffsetOnAxis(ap=first_key, axis=0)).then_inc(scattered, 16)

            PLACED = 16 * (NB + 1)

            def start(self):
                for k in range(2):
                    last = nc.vector.memset(self.keep[k][:, :, 0], 0.0)
                return [last, nc.vector.tensor_copy(self.run[1][:, :, CH], self.init[:, :])]

            def load(self, eng, t, k):
                eng.dma_start(self.raw[k][:, :, :], self.table[:, cols(t), :]).then_inc(self.raw_in[k], 16)

            def lay(self, act, t, k, i):
                K.wait(act, "act", self.spread, t - 1)
                flags = self.masks.cont[:, cols(t)].unsqueeze(1).to_broadcast([EP, self.width, CH])
                nc.scalar.copy(self.keep[k][:, :, 1:CH + 1], flags)
                K.wait(act, "act", self.raw_in[k], i * 16 + 16)
                nc.scalar.copy(self.fresh[k][:, :, 1:CH + 1], self.raw[k][:, :, :].rearrange("p c f -> p f c")).then_inc(self.laid, 1)

            def scan(self, dve, c, t, k):
                c.step(nc.vector.tensor_copy(self.fresh[k][:, :, 0], self.run[1 - k][:, :, CH]))
                K.wait(dve, "dve", self.laid, t + 1)
                flat = lambda ap: ap[:, :, :].rearrange("p f c -> p (f c)")
                nc.vector.tensor_tensor_scan(flat(self.run[k]), flat(self.keep[k]), flat(self.fresh[k]), 0.0,
                                             ALU.mult, ALU.add).then_inc(self.spread, 1)
                K.wait(dve, "dve", self.spread, t + 1)

        def segment_softmax(e, n_heads, floor):
            with ExitStack() as st:
                neg_cont = sb(st, "neg_cont", [EP, COLS + 1])
                neg_first = sb(st, "neg_first", [EP, COLS])
                neg_last = sb(st, "neg_last", [EP, COLS])
                same = sb(st, "same", [EP, COLS + 1])
                run = sb(st, "run", [EP, n_heads, COLS])
                tot = sb(st, "tot", [EP, n_heads, COLS])
                edge_t = sb(st, "edge_t", [n_heads, 2, EP])
                flags_t = sb(st, "flags_t", [n_heads, 4, EP])
                carry_t = sb(st, "carry_t", [n_heads, 2, EP + 1])
                carry = sb(st, "carry", [EP, 2, n_heads])
                turn = ps(st, "turn", [n_heads, 2, 512])
                back = ps(st, "back", [EP, 2, 512])
                tot_done, turned, scanned, backed, shifted, exped, chain_v = (K.sem(n) for n in (
                    "tot_done", "turned", "scanned", "backed", "shifted", "exped", "chain_v"))
                block = st.enter_context(nc.Block())

                @block.tensor
                def _(pe):
                    for r in range(2):
                        pe.wait_ge(tot_done, r + 1)
                        nc.tensor.transpose(turn[:, 0, 0:EP], tot[:, :, COLS - 1], ident[0:EP, 0:EP])
                        nc.tensor.transpose(turn[:, 1, 0:EP], tot[:, :, 0], ident[0:EP, 0:EP]).then_inc(turned, 1)
                        pe.wait_ge(scanned, r + 1)
                        nc.tensor.transpose(back[:, 0, 0:n_heads], carry_t[:, 0, 0:EP], ident[0:n_heads, 0:n_heads])
                        nc.tensor.transpose(back[:, 1, 0:n_heads], carry_t[:, 1, 1:EP + 1], ident[0:n_heads, 0:n_heads]).then_inc(backed, 1)

                @block.scalar
                def _(act):
                    act.wait_ge(shifted, 1)
                    nc.scalar.activation(e[:, :, :], e[:, :, :], ACT.Exp).then_inc(exped, 1)

                @block.vector
                def _(dve):
                    c = Chain(dve, chain_v)

                    def totals(r, flags, op0, op1):
                        for j in range(n_heads):
                            c.link(nc.vector.tensor_tensor_scan(run[:, j, :], flags[:, 0:COLS], e[:, j, :], -BIG if op1 == ALU.max else 0.0, op0, op1))
                        c.join()
                        for j in range(n_heads):
                            c.link(nc.vector.tensor_tensor_scan(tot[:, j, ::-1], flags[:, 1:COLS + 1][:, ::-1], run[:, j, ::-1], -BIG if op1 == ALU.max else 0.0, op0, ALU.max))
                        c.join()
                        dve.sem_inc(tot_done, 1)
                        dve.wait_ge(turned, r + 1)
                        comb = ALU.add if op1 == ALU.max else ALU.mult
                        c.link(nc.vector.tensor_tensor(edge_t[:, 0, :], turn[:, 0, 0:EP], flags_t[:, 0, :], comb))
                        c.link(nc.vector.tensor_tensor(edge_t[:, 1, :], turn[:, 1, 0:EP], flags_t[:, 1, :], comb))
                        none = -BIG if op1 == ALU.max else 0.0
                        c.link(nc.vector.memset(carry_t[:, 0, 0:1], none))
                        c.step(nc.vector.memset(carry_t[:, 1, EP:EP + 1], none))
                        c.link(nc.vector.tensor_tensor_scan(carry_t[:, 0, 1:EP + 1], flags_t[:, 2, :], edge_t[:, 0, :], none, comb, op1))
                        c.step(nc.vector.tensor_tensor_scan(carry_t[:, 1, 0:EP][:, ::-1], flags_t[:, 3, ::-1], edge_t[:, 1, ::-1], none, comb, op1))
                        dve.sem_inc(scanned, 1)
                        dve.wait_ge(backed, r + 1)
                        c.step(nc.vector.tensor_copy(carry[:, :, :], back[:, :, 0:n_heads]))
                        for side, member in enumerate((neg_first, neg_last) if op1 == ALU.max else (dst_ends.first_seg, dst_ends.last_seg)):
                            for j in range(n_heads):
                                c.link(nc.vector.scalar_tensor_tensor(tot[:, j, :], member[:, :], carry[:, side, j:j + 1], tot[:, j, :], comb, op1))
                            c.join()

                    flag_rows = (by_dst.fwd_row, dst_ends.bwd_row, by_dst.fwd_all, dst_ends.bwd_all)
                    for src_mask, dst_mask in ((by_dst.cont, neg_cont), (dst_ends.first_seg, neg_first), (dst_ends.last_seg, neg_last)):
                        c.link(nc.vector.tensor_scalar(dst_mask[:, 0:COLS], src_mask[:, :], BIG, -BIG, ALU.mult, ALU.add))
                    c.link(nc.vector.tensor_copy(same[:, 0:COLS], by_dst.cont[:, :]))
                    c.link(nc.vector.memset(neg_cont[:, COLS:], -BIG))
                    c.link(nc.vector.memset(same[:, COLS:], 0.0))
                    for n, row in enumerate(flag_rows):
                        c.link(nc.vector.tensor_scalar(flags_t[:, n, :], row[0:n_heads, :], BIG, -BIG, ALU.mult, ALU.add))
                    c.join()
                    totals(0, neg_cont, ALU.add, ALU.max)
                    nc.vector.tensor_tensor(e[:, :, :], e[:, :, :], tot[:, :, :], ALU.subtract).then_inc(shifted, 1)
                    for n, row in enumerate(flag_rows):
                        c.link(nc.vector.tensor_copy(flags_t[:, n, :], row[0:n_heads, :]))
                    c.join()
                    dve.wait_ge(exped, 1)
                    totals(1, same, ALU.mult, ALU.add)
                    c.step(nc.vector.tensor_scalar(tot[:, :, :], tot[:, :, :], floor, None, ALU.max))
                    c.step(nc.vector.reciprocal(run[:, :, :], tot[:, :, :]))
                    c.step(nc.vector.tensor_tensor(e[:, :, :], e[:, :, :], run[:, :, :], ALU.mult))
                    c.restart()
            K.recycle()

        def load(pairs_):
            loaded = K.sem("loaded")
            with nc.Block() as block:
                @block.sync
                def _(sp):
                    for target, source in pairs_:
                        sp.dma_start(target, source, allow_slow_non_contiguous=True).then_inc(loaded, 16)
                    sp.wait_ge(loaded, 16 * len(pairs_))
            K.recycle()

        def on_all(ap, n=NP):
            return ap.unsqueeze(0).to_broadcast([n, ap.shape[0]])

        ends_stack = ExitStack()
        dst_ends = SegmentEnds(ends_stack)
        e0 = ExitStack()
        alpha = sb(e0, "alpha", [EP, HEADS0, COLS])
        lo_s = sb(e0, "lo_s", [EP, COLS], BF16)
        hi_s = sb(e0, "hi_s", [EP, COLS], BF16)
        fd_stack = ExitStack()
        f_d = sb(fd_stack, "f_d", [NP, NB, 64])
        with ExitStack() as st:
            w = sb(st, "w_sd", [FEAT, 128])
            bias = sb(st, "b_sd", [NP, 128])
            f_s = sb(st, "f_s", [NP, NB, 64])
            load([(w[:, 0:64], A["L0_gnn_W2s"]), (w[:, 64:128], A["L0_gnn_W2d"]),
                  (bias[:, 0:64], on_all(A["L0_gnn_b2s"])), (bias[:, 64:128], on_all(A["L0_gnn_b2d"]))])

            def project(c, at, product):
                for half, f in enumerate((f_s, f_d)):
                    side = slice(64 * half, 64 * half + 64)
                    c.link(nc.vector.tensor_tensor(f[:, at, :], product[:, :, side], bias[:, side].unsqueeze(1).to_broadcast([NP, SET, 64]), ALU.add))
            node_stage(lambda c, at: None, project, 128, h, w[:, :], normal="before",
                       stores=lambda at: [(node_rows(tab_s0)[:, at, :], f_s[:, at, :]), (node_rows(tab_d0)[:, at, :], f_d[:, at, :])])

        FILL = 6400
        PIECES = COLS * 64 // FILL + COLS * HEADS3 // FILL
        EARLY = 12
        with ExitStack() as st:
            lo_d = sb(st, "lo_d", [EP, COLS], BF16)
            hi_d = sb(st, "hi_d", [EP, COLS], BF16)
            bits = sb(st, "bits", [EP, COLS], I32)
            attn = sb(st, "attn", [EP, 64])
            idx = [sb(st, f"idx{k}", [EP, CH], I32) for k in range(2)]
            en = [sb(st, f"en{k}", [EP, CH, 64]) for k in range(2)]
            en_back = [sb(st, f"en_back{k}", [EP, CH, 64]) for k in range(2)]
            zw = sb(st, "zw", [EP, CH, 64])
            hot_lo = [sb(st, f"hot_lo{k}", [EP, CH, 128], BF16) for k in range(2)]
            hot_hi = [sb(st, f"hot_hi{k}", [EP, CH, NB], BF16) for k in range(2)]
            counts = sb(st, "counts", [NP, NB])
            block_tot = sb(st, "block_tot", [NP, NB])
            start_of = sb(st, "start_of", [NP, NB])
            end_f = sb(st, "end_f", [NP, NB])
            cnt_ps = [ps(st, f"cnt_ps{k}", [NP, NB]) for k in range(2)]
            tot_ps = ps(st, "tot_ps", [NP, NB])
            pre_ps = ps(st, "pre_ps", [NP, NB])
            ev = Spread(st, 64, ev_rows, by_dst)
            by_dst.scratch(st, dst_ends)
            idx_in = [K.sem(f"idx_in{k}") for k in range(2)]
            gathered = [K.own(f"gathered{k}") for k in range(2)]
            placed = K.own("placed")
            stored = [K.sem(f"stored{k}") for k in range(2)]
            back_in = [K.sem(f"back_in{k}") for k in range(2)]
            cleared, scored, hots, counted, copied, summed, starts, chain_v, loaded = (
                K.sem(n) for n in ("cleared", "scored", "hots", "counted", "copied", "summed", "starts", "chain_v", "loaded"))
            block = st.enter_context(nc.Block())
            src_rows = edge_rows(A["src"])

            @block.sync
            def _(sp):
                sp.dma_start(attn[:, :], on_all(A["L0_gnn_attn"].rearrange("a h f -> (a h f)"), EP)).then_inc(loaded, 16)
                for k in range(2):
                    sp.dma_start(idx[k][:, :], src_rows[:, cols(k)]).then_inc(idx_in[k], 16)
                by_dst.load(sp)

                def body(i):
                    for k in range(2):
                        t = 2 * i + k
                        K.wait(sp, "sp", gathered[k], (i + 1) * (16 * CH))
                        sp.dma_start(edge_rows(en_rows)[:, cols(t), :], en[k][:, :, :]).then_inc(stored[k], 16)
                        if not known_ge(t, 2 * PAIRS - 2):
                            sp.dma_start(idx[k][:, :], src_rows[:, cols(t + 2)]).then_inc(idx_in[k], 16)
                pairs(sp, body, ahead=True)
                for k in range(2):
                    sp.wait_ge(stored[k], 16 * PAIRS)

            @block.gpsimd
            def _(pool):
                def body(i):
                    for k in range(2):
                        K.wait(pool, "pool", idx_in[k], i * 16 + 16)
                        K.wait(pool, "pool", stored[k], i * 16)
                        for g in range(CH):
                            pool.indirect_dma_start(en[k][:, g, :], None, tab_s0,
                                                    bass.IndirectOffsetOnAxis(ap=idx[k][:, g:g + 1], axis=0)).then_inc(gathered[k], 16)
                pairs(pool, body, end=EARLY)
                pool.wait_ge(cleared, 16 * PIECES)
                pool.wait_ge(starts, 1)
                ev.place(pool, lambda b: f_d[:, b, :], first_dst, tab_d0, dst_i[:, 0:1], placed)
                pairs(pool, body, first=EARLY)

            @block.scalar
            def _(act):
                zeroed_pieces = 0

                def bring(t, k, i):
                    K.wait(act, "act", scored, t - 1)
                    K.wait(act, "act", stored[k], i * 16 + 16)
                    act.dma_start(en_back[k][:, :, :], edge_rows(en_rows)[:, cols(t), :]).then_inc(back_in[k], 16)
                    ev.load(act, t, k)
                for k in range(2):
                    act.wait_ge(idx_in[k], 16)
                for table, width in ((ev_rows, 64), (own_rows, HEADS3)):
                    filled = edge_rows(table[0:EDGES, :]).rearrange("p c f -> p (c f)")
                    for n in range(COLS * width // FILL):
                        act.dma_start(filled[:, n * FILL:(n + 1) * FILL].rearrange("p (n r) -> p n r", r=zeros.shape[1]),
                                      zeros[:, :].unsqueeze(1).to_broadcast([EP, FILL // zeros.shape[1], zeros.shape[1]])).then_inc(cleared, 16)
                        zeroed_pieces += 1
                        act.wait_ge(cleared, 16 * zeroed_pieces)
                act.wait_ge(placed, ev.PLACED)
                bring(0, 0, 0)
                bring(1, 1, 0)
                ev.lay(act, 0, 0, 0)

                def body(i):
                    for k in range(2):
                        t = 2 * i + k
                        if not known_ge(t, 2 * PAIRS - 1):
                            ev.lay(act, t + 1, 1 - k, i + k)
                        if not known_ge(t, 2 * PAIRS - 2):
                            bring(t + 2, k, i + 1)
                pairs(act, body, ahead=True)

            @block.tensor
            def _(pe):
                by_dst.turn(pe)
                for q in range(2):
                    nc.tensor.matmul(cnt_ps[q][:, :], zbias[:, :], zbias[:, 0:NB], start=True, stop=False)

                    def body(i):
                        for k in range(2):
                            t = 2 * i + k
                            K.wait(pe, "pe", hots, t + 1 + q * (2 * PAIRS))
                            for g in range(CH):
                                last = nc.tensor.matmul(cnt_ps[q][:, :], hot_lo[k][:, g, :], hot_hi[k][:, g, :], start=False, stop=False)
                            last.then_inc(counted, 1)
                    pairs(pe, body)
                    nc.tensor.matmul(cnt_ps[q][:, :], zbias[:, :], zbias[:, 0:NB], start=False, stop=True).then_inc(counted, 1)
                    pe.wait_ge(copied, q + 1)
                    nc.tensor.matmul(tot_ps[:, :], ones[:, :], counts[:, :], start=True, stop=True)
                    nc.tensor.matmul(pre_ps[:, :], before[:, :], counts[:, :], start=True, stop=True).then_inc(summed, 1)

            @block.vector
            def _(dve):
                c = Chain(dve, chain_v)
                by_dst.make(dve, c, dst_i[:, :])
                for key, lo, hi in ((src_i, lo_s, hi_s), (dst_i, lo_d, hi_d)):
                    c.step(nc.vector.tensor_scalar(bits[:, :], key[:, :], 127, None, ALU.bitwise_and))
                    c.step(nc.vector.tensor_copy(lo[:, :], bits[:, :]))
                    c.step(nc.vector.tensor_scalar(bits[:, :], key[:, :], 7, None, ALU.arith_shift_right))
                    c.step(nc.vector.tensor_copy(hi[:, :], bits[:, :]))
                dve.wait_ge(loaded, 16)
                c.restart()

                def hot(lo, hi, t, k):
                    nc.vector.tensor_tensor(hot_lo[k][:, :, :], iota_row[0:EP, :].unsqueeze(1).to_broadcast([EP, CH, 128]),
                                            lo[:, cols(t)].unsqueeze(2).to_broadcast([EP, CH, 128]), ALU.is_equal)
                    nc.vector.tensor_tensor(hot_hi[k][:, :, :], iota_row[0:EP, 0:NB].unsqueeze(1).to_broadcast([EP, CH, NB]),
                                            hi[:, cols(t)].unsqueeze(2).to_broadcast([EP, CH, NB]), ALU.is_equal).then_inc(hots, 1)

                def prefix(q, first, last, has, base):
                    dve.wait_ge(counted, (q + 1) * (2 * PAIRS + 1))
                    c.step(nc.vector.tensor_copy(counts[:, :], cnt_ps[q][:, :]))
                    dve.sem_inc(copied, 1)
                    dve.wait_ge(summed, q + 1)
                    c.step(nc.vector.tensor_copy(block_tot[:, :], tot_ps[:, :]))
                    c.link(nc.vector.memset(start_of[:, 0:1], 0.0))
                    c.step(nc.vector.tensor_tensor_scan(start_of[:, 1:NB], ones[:, 0:NB - 1], block_tot[:, 0:NB - 1], 0.0, ALU.mult, ALU.add))
                    c.step(nc.vector.tensor_tensor(start_of[:, :], start_of[:, :], pre_ps[:, :], ALU.add))
                    c.step(nc.vector.scalar_tensor_tensor(end_f[:, :], start_of[:, :], -1.0, counts[:, :], ALU.add, ALU.add))
                    c.step(nc.vector.tensor_scalar(end_f[:, :], end_f[:, :], 0.0, None, ALU.max))
                    c.link(nc.vector.tensor_copy(last[:, :], end_f[:, :]))
                    if base is not None:
                        c.link(nc.vector.tensor_copy(base[:, :], start_of[:, :]))
                    c.step(nc.vector.tensor_scalar(has[:, :], counts[:, :], 0.0, None, ALU.is_gt))
                    c.step(nc.vector.scalar_tensor_tensor(start_of[:, :], start_of[:, :], -float(EDGES), has[:, :], ALU.add, ALU.mult))
                    c.step(nc.vector.tensor_scalar(start_of[:, :], start_of[:, :], float(EDGES), None, ALU.add))
                    c.step(nc.vector.tensor_scalar(end_f[:, :], has[:, :], -1.0, 1.0, ALU.mult, ALU.add))
                    c.step(nc.vector.tensor_tensor(end_f[:, :], end_f[:, :], node_of[:, :], ALU.mult))
                    c.step(nc.vector.tensor_tensor(start_of[:, :], start_of[:, :], end_f[:, :], ALU.add))
                    c.step(nc.vector.tensor_copy(first[:, :], start_of[:, :]))
                    dve.sem_inc(starts, 1)
                    c.restart()

                def count_dst(i):
                    for k in range(2):
                        t = 2 * i + k
                        K.wait(dve, "dve", counted, t - 1)
                        hot(lo_d, hi_d, t, k)
                pairs(dve, count_dst)
                prefix(0, first_dst, last_dst, has_dst, None)
                dve.wait_ge(placed, ev.PLACED)
                for ins in ev.start():
                    c.link(ins)
                c.restart()

                def body(i):
                    for k in range(2):
                        t = 2 * i + k
                        K.wait(dve, "dve", counted, t + 2 * PAIRS)
                        hot(lo_s, hi_s, t, k)
                        ev.scan(dve, c, t, k)
                        K.wait(dve, "dve", back_in[k], i * 16 + 16)
                        c.step(nc.vector.tensor_tensor(zw[:, :, :], en_back[k][:, :, :], ev.rows(k), ALU.add))
                        c.step(nc.vector.scalar_tensor_tensor(zw[:, :, :], zw[:, :, :], 0.2, zw[:, :, :], ALU.mult, ALU.max))
                        c.step(nc.vector.tensor_tensor(zw[:, :, :], zw[:, :, :], attn[:, :].unsqueeze(1).to_broadcast([EP, CH, 64]), ALU.mult))
                        nc.vector.tensor_reduce(alpha[:, :, cols(t)].rearrange("p h c -> p c h"),
                                                zw[:, :, :].rearrange("p c (h f) -> p c h f", h=HEADS0), AX.X, ALU.add).then_inc(scored, 1)
                        K.wait(dve, "dve", scored, t + 1)
                        c.restart()
                pairs(dve, body)
                prefix(1, first_src, last_src, has_src, base_src)
        fd_stack.close()
        K.recycle()

        segment_softmax(alpha, HEADS0, 1e-9)

        with ExitStack() as st:
            en = [sb(st, f"en{k}", [EP, CH, 64]) for k in range(2)]
            r = [sb(st, f"r{k}", [EP, CH, 64]) for k in range(2)]
            z = [sb(st, f"z{k}", [EP, CH, 64]) for k in range(2)]
            z_top = sb(st, "z_top", [EP, CH, HEADS0])
            total = sb(st, "total", [EP, CH, HEADS0])
            z_div = sb(st, "z_div", [EP, CH, HEADS0])
            hot_lo = [sb(st, f"hot_lo{k}", [EP, CH, 128], BF16) for k in range(2)]
            hot_hi = [sb(st, f"hot_hi{k}", [EP, CH, NB], BF16) for k in range(2)]
            hot_t = [sb(st, f"hot_t{q}", [NP, GR, EP]) for q in range(GROUPS)]
            hot_tb = [sb(st, f"hot_tb{q}", [NP, GR, EP], BF16) for q in range(GROUPS)]
            place_sb = [sb(st, f"place_sb{q}", [NP, NB]) for q in range(GROUPS)]
            own_same = [sb(st, f"own_same{k}", [EP, GR, EP], BF16) for k in range(2)]
            cross_same = [sb(st, f"cross_same{k}", [EP, 2, 3 * EP], BF16) for k in range(2)]
            not_before = sb(st, "not_before", [EP, GR, EP], BF16)
            picked = sb(st, "picked", [EP, GR, NB])
            pos = [sb(st, f"pos{k}", [EP, CH]) for k in range(2)]
            pos_i = [sb(st, f"pos_i{k}", [EP, CH], I32) for k in range(2)]
            ends = [sb(st, f"ends{k}", [EP, CH, 2], I32) for k in range(2)]
            place_ps = ps(st, "place_ps", [NP, NB])
            turn_ps = [ps(st, f"turn_ps{k}", [NP, GR, 128], BF16) for k in range(2)]
            own_ps = ps(st, "own_ps", [EP, GR, EP])
            cross_ps = ps(st, "cross_ps", [EP, 2, 512])
            rank_ps = [ps(st, f"rank_ps{k}", [EP, GR, NB]) for k in range(2)]
            S = SegmentSums(st, FEAT, sums)
            rows_in = [K.sem(f"rows_in{k}") for k in range(2)]
            sent = [K.own(f"sent{k}") for k in range(2)]
            (shifted, exped, multiplied, hots, turned, turned_sb, samed, copied_same, ranked, selected, placed, place_out, posed,
             chain_v, triangle) = (K.sem(n) for n in (
                 "shifted", "exped", "multiplied", "hots", "turned", "turned_sb", "samed", "copied_same", "ranked",
                 "selected", "placed", "place_out", "posed", "chain_v", "triangle"))
            block = st.enter_context(nc.Block())
            last_chunk = 2 * PAIRS - 1

            def cross(a, b):
                return (0, (b - 1) * EP) if a == 0 else (1, (b - 2 if a == 1 else 2) * EP)

            @block.sync
            def _(sp):
                def body(i):
                    for k in range(2):
                        t = 2 * i + k
                        K.wait(sp, "sp", multiplied, t - 1)
                        sp.dma_start(en[k][:, :, :], edge_rows(en_rows)[:, cols(t), :]).then_inc(rows_in[k], 16)
                        sp.dma_start(r[k][:, :, :], edge_rows(A["edge_attr3_2x32"])[:, cols(t), :, :].rearrange("p c h f -> p c (h f)")).then_inc(rows_in[k], 16)
                pairs(sp, body)

            @block.gpsimd
            def _(pool):
                def body(i):
                    for k in range(2):
                        t = 2 * i + k
                        K.wait(pool, "pool", posed, t + 1)
                        for g in range(CH):
                            pool.indirect_dma_start(by_src, bass.IndirectOffsetOnAxis(ap=pos_i[k][:, g:g + 1], axis=0),
                                                    ends[k][:, g, :], None).then_inc(sent[k], 16)
                pairs(pool, body)
                for k in range(2):
                    pool.wait_ge(sent[k], 16 * CH * PAIRS)

            @block.tensor
            def _(pe):
                def turn(n, k, q):
                    K.wait(pe, "pe", turned_sb, n - 1)
                    for g in range(GR):
                        last = nc.tensor.transpose(turn_ps[q % 2][:, g, 0:EP], hot_lo[k][:, q * GR + g, :], identb[0:EP, 0:EP])
                    last.then_inc(turned, 1)

                def rank(n, k, q):
                    s = q % 2
                    K.wait(pe, "pe", selected, GR * (n - 1))
                    K.wait(pe, "pe", copied_same, n + 1)
                    for b in range(GR):
                        o = rank_ps[s][:, b, :]
                        nc.tensor.matmul(o, hot_t[q][:, b, :], place_sb[q][:, :], start=True, stop=False)
                        for a in range(b):
                            bank, at = cross(a, b)
                            nc.tensor.matmul(o, cross_same[s][:, bank, at:at + EP], hot_hi[k][:, q * GR + a, :], start=False, stop=False)
                        last = nc.tensor.matmul(o, own_same[s][:, b, :], hot_hi[k][:, q * GR + b, :], start=False, stop=True)
                    last.then_inc(ranked, 1)

                def body(i):
                    for k in range(2):
                        for q in range(GROUPS):
                            t = 2 * i + k
                            n = t * GROUPS + q
                            if q < GROUPS - 1:
                                turn(n + 1, k, q + 1)
                            elif not known_ge(t, last_chunk):
                                K.wait(pe, "pe", hots, t + 2)
                                turn(n + 1, 1 - k, 0)
                            K.wait(pe, "pe", turned_sb, n + 1)
                            K.wait(pe, "pe", copied_same, n)
                            nc.tensor.matmul(own_ps[:, :, :].rearrange("p g e -> p (g e)"), identb[0:EP, 0:EP],
                                             not_before[:, :, :].rearrange("p g e -> p (g e)"), start=True, stop=False)
                            for a in range(GR):
                                nc.tensor.matmul(own_ps[:, a, :], hot_tb[q][:, a, :], hot_tb[q][:, a, :], start=False, stop=a == GR - 1)
                            for a in range(GR - 1):
                                bank, at = cross(a, a + 1)
                                later = hot_tb[q][:, a + 1:GR, :].rearrange("p c e -> p (c e)")
                                last = nc.tensor.matmul(cross_ps[:, bank, at:at + (GR - 1 - a) * EP], hot_tb[q][:, a, :], later, start=True, stop=True)
                            last.then_inc(samed, 1)
                            K.wait(pe, "pe", place_out, n + 1)
                            nc.tensor.matmul(place_ps[:, :], ident[:, :], place_sb[q][:, :], start=True, stop=False)
                            for g in range(GR):
                                last = nc.tensor.matmul(place_ps[:, :], hot_lo[k][:, q * GR + g, :], hot_hi[k][:, q * GR + g, :],
                                                        start=False, stop=g == GR - 1)
                            last.then_inc(placed, 1)
                            if q:
                                rank(n - 1, k, q - 1)
                            elif not first_chunk(t):
                                rank(n - 1, 1 - k, GROUPS - 1)
                pe.wait_ge(triangle, 1)
                K.wait(pe, "pe", hots, 1)
                turn(0, 0, 0)
                pairs(pe, body, ahead=True)
                rank(last_chunk * GROUPS + GROUPS - 1, 1, GROUPS - 1)

            @block.scalar
            def _(act):
                nc.scalar.copy(place_sb[0][:, :], base_src[:, :]).then_inc(place_out, 1)

                def take_turned(n, q):
                    K.wait(act, "act", turned, n + 1)
                    K.wait(act, "act", ranked, n - (GROUPS - 1))
                    nc.scalar.copy(hot_tb[q][:, :, :], turn_ps[q % 2][:, :, 0:EP])
                    nc.scalar.copy(hot_t[q][:, :, :], turn_ps[q % 2][:, :, 0:EP]).then_inc(turned_sb, 1)

                def exps(t, k):
                    K.wait(act, "act", shifted, t + 1)
                    nc.scalar.activation(z[k][:, :, :], z[k][:, :, :], ACT.Exp).then_inc(exped, 1)

                def body(i):
                    for k in range(2):
                        t = 2 * i + k
                        for q in range(GROUPS):
                            n, s = t * GROUPS + q, q % 2
                            if q < GROUPS - 1 or not known_ge(t, last_chunk):
                                take_turned(n + 1, (q + 1) % GROUPS)
                            K.wait(act, "act", samed, n + 1)
                            K.wait(act, "act", ranked, n - 1)
                            nc.scalar.activation(own_same[s][:, :, :], own_ps[:, :, :], ACT.Relu)
                            nc.scalar.copy(cross_same[s][:, :, :], cross_ps[:, :, 0:3 * EP]).then_inc(copied_same, 1)
                            K.wait(act, "act", placed, n + 1)
                            K.wait(act, "act", ranked, n - (GROUPS - 2))
                            nc.scalar.copy(place_sb[(q + 1) % GROUPS][:, :], place_ps[:, :]).then_inc(place_out, 1)
                            if q == 0 and not first_chunk(t):
                                exps(t - 1, 1 - k)
                            if q == 1 and not first_pair(t):
                                S.store(act, t - 2, k, i - 1)
                            if q == 2:
                                S.mask(act, t, k)
                take_turned(0, 0)
                pairs(act, body, ahead=True)
                exps(last_chunk, 1)
                for k in range(2):
                    S.store(act, last_chunk - 1 + k, k, PAIRS - 1)
                S.finish(act)

            @block.vector
            def _(dve):
                c = Chain(dve, chain_v)
                for ins in S.start():
                    c.link(ins)
                nc.vector.tensor_scalar(not_before[:, :, :], before[0:EP, 0:EP].unsqueeze(1).to_broadcast([EP, GR, EP]),
                                        -1.0, None, ALU.add).then_inc(triangle, 1)
                c.restart()

                def per_head(ap):
                    return ap.unsqueeze(3).to_broadcast([EP, CH, HEADS0, FEAT])

                def heads(ap):
                    return ap.rearrange("p c (h f) -> p c h f", h=HEADS0)

                def hot(t, k):
                    K.wait(dve, "dve", ranked, (t - 1) * GROUPS)
                    nc.vector.tensor_tensor(hot_lo[k][:, :, :], iota_row[0:EP, :].unsqueeze(1).to_broadcast([EP, CH, 128]),
                                            lo_s[:, cols(t)].unsqueeze(2).to_broadcast([EP, CH, 128]), ALU.is_equal)
                    nc.vector.tensor_tensor(hot_hi[k][:, :, :], iota_row[0:EP, 0:NB].unsqueeze(1).to_broadcast([EP, CH, NB]),
                                            hi_s[:, cols(t)].unsqueeze(2).to_broadcast([EP, CH, NB]), ALU.is_equal).then_inc(hots, 1)

                def add_exps(t, k):
                    K.wait(dve, "dve", exped, t + 1)
                    return c.mark(nc.vector.tensor_reduce(total[:, :, :], heads(z[k][:, :, :]), AX.X, ALU.add))

                def divide(k):
                    return c.mark(nc.vector.tensor_tensor(heads(z[k][:, :, :]), heads(z[k][:, :, :]), per_head(z_div[:, :, :]), ALU.mult))

                def add_up(t, k):
                    c.link(nc.vector.tensor_tensor(S.message(k), z[k][:, :, 0:FEAT].rearrange("p c f -> p f c"),
                                                   z[k][:, :, FEAT:2 * FEAT].rearrange("p c f -> p f c"), ALU.add))
                    S.scan(dve, c, t, k, carried=True)

                def pick(n, k, q):
                    K.wait(dve, "dve", ranked, n + 1)
                    K.wait(dve, "dve", selected, GR * n)
                    for g in range(GR):
                        at = q * GR + g
                        nc.vector.scalar_tensor_tensor(picked[:, g, :], rank_ps[q % 2][:, g, :], 1.0, hot_hi[k][:, at, :], ALU.mult, ALU.mult,
                                                       accum_out=pos[k][:, at:at + 1]).then_inc(selected, 1)

                def send(t, k, i):
                    K.wait(dve, "dve", sent[k], i * (16 * CH))
                    c.link(nc.vector.tensor_copy(ends[k][:, :, 0], src_i[:, cols(t)]))
                    c.link(nc.vector.tensor_copy(ends[k][:, :, 1], dst_i[:, cols(t)]))
                    K.wait(dve, "dve", selected, (t + 1) * CH)
                    c.step(nc.vector.tensor_copy(pos_i[k][:, :], pos[k][:, :]))
                    dve.sem_inc(posed, 1)

                def body(i):
                    for k in range(2):
                        t = 2 * i + k
                        K.wait(dve, "dve", rows_in[k], i * 32 + 32)
                        nc.vector.tensor_tensor(z[k][:, :, :], en[k][:, :, :], r[k][:, :, :], ALU.mult).then_inc(multiplied, 1)
                        if not first_chunk(t):
                            pick(t * GROUPS - 1, 1 - k, GROUPS - 1)
                            send(t - 1, 1 - k, i - 1 + k)
                        K.wait(dve, "dve", multiplied, t + 1)
                        z4 = heads(z[k][:, :, :])
                        weighted = c.mark(nc.vector.tensor_tensor(z4, z4, per_head(alpha[:, :, cols(t)].rearrange("p h c -> p c h")), ALU.mult))
                        if not known_ge(t, last_chunk):
                            hot(t + 1, 1 - k)
                        pick(t * GROUPS, k, 0)
                        c.until(weighted)
                        topped = c.mark(nc.vector.tensor_reduce(z_top[:, :, :], z4, AX.X, ALU.max))
                        if not first_chunk(t):
                            summed = add_exps(t - 1, 1 - k)
                        c.until(topped)
                        nc.vector.tensor_tensor(z4, z4, per_head(z_top[:, :, :]), ALU.subtract).then_inc(shifted, 1)
                        if not first_chunk(t):
                            c.until(summed)
                            inverse = c.mark(nc.vector.reciprocal(z_div[:, :, :], total[:, :, :]))
                        pick(t * GROUPS + 1, k, 1)
                        if not first_chunk(t):
                            c.until(inverse)
                            divided = divide(1 - k)
                            S.carry(c, 1 - k)
                        pick(t * GROUPS + 2, k, 2)
                        if not first_chunk(t):
                            c.until(divided)
                            add_up(t - 1, 1 - k)
                    c.restart()
                hot(0, 0)
                pairs(dve, body, ahead=True)
                pick(last_chunk * GROUPS + GROUPS - 1, 1, GROUPS - 1)
                send(last_chunk, 1, PAIRS - 1)
                c.until(add_exps(last_chunk, 1))
                c.step(nc.vector.reciprocal(z_div[:, :, :], total[:, :, :]))
                c.until(divide(1))
                S.carry(c, 1)
                add_up(last_chunk, 1)
                c.restart()
        K.recycle()
        e0.close()
        ends_stack.close()
        agg = sb(top, "agg", [NP, NB, FEAT])

        def of_set(flags):
            return flags.unsqueeze(2).to_broadcast([NP, SET, FEAT])

        def table_of_h(at):
            return [(node_rows(tab_h)[:, at, :], h[:, at, :])]

        mend_sums(sums, FEAT)
        with ExitStack() as st:
            w = sb(st, "w1", [FEAT, FEAT])
            bias = sb(st, "b1", [NP, FEAT])
            load([(w[:, :], A["L0_gnn_W1"]), (bias[:, :], on_all(A["L0_gnn_b1"]))])

            def begin(c, at):
                c.link(nc.vector.tensor_tensor(x[:, at, :], x[:, at, :], bias[:, :].unsqueeze(1).to_broadcast([NP, SET, FEAT]), ALU.add))
                c.step(nc.vector.tensor_tensor(agg[:, at, :], agg[:, at, :], of_set(has_dst[:, at]), ALU.mult))
                c.link(nc.vector.tensor_tensor(agg[:, at, :], agg[:, at, :], h[:, at, :], ALU.add))

            def finish(c, at, product):
                c.step(nc.vector.tensor_tensor(x[:, at, :], x[:, at, :], product, ALU.add))
            node_stage(begin, finish, FEAT, agg, w[:, :], gather=(sums, last_dst, agg), normal="after", stores=table_of_h)

        def gather_rows(st):
            idx = [sb(st, f"idx{k}", [EP, CH], I32) for k in range(2)]
            rows = [sb(st, f"hs{k}", [EP, CH, FEAT]) for k in range(2)]
            idx_in = [K.sem(f"idx_in{k}") for k in range(2)]
            gathered = [K.own(f"gathered{k}") for k in range(2)]

            def load_idx(sp, t, k, i):
                K.wait(sp, "sp", gathered[k], i * (16 * CH))
                sp.dma_start(idx[k][:, :], edge_rows(A["src"])[:, cols(t)]).then_inc(idx_in[k], 16)

            def gather(pool, t, k, i):
                K.wait(pool, "pool", idx_in[k], i * 16 + 16)
                for g in range(CH):
                    pool.indirect_dma_start(rows[k][:, g, :], None, tab_h,
                                            bass.IndirectOffsetOnAxis(ap=idx[k][:, g:g + 1], axis=0)).then_inc(gathered[k], 16)
            return rows, gathered, load_idx, gather

        MUL, HID, TPW = 8, 64, 256
        a_src = sb(top, "a_src", [NP, NB, HEADS3])
        first_key = sb(top, "first_key", [EP, 1], I32)
        weights = ExitStack()
        w1 = sb(weights, "w1_pairs", [128, CH // 2, 128])
        w2 = sb(weights, "w2_pair", [128, 128])
        w3 = sb(weights, "w3_pair", [128, 2, TPW])
        b1 = sb(weights, "b1_pair", [128, 1])
        b2 = sb(weights, "b2_pair", [128, 1])
        b3_rows = sb(weights, "b3_rows", [3, 2, TPW], BF16)
        ones_b = sb(weights, "ones_b", [3, EP], BF16)
        own_w = sb(weights, "own_w", [FEAT, FEAT])
        w_sd = sb(weights, "w_sd3", [FEAT, 2, HEADS3])
        fcb = sb(weights, "fcb3", [NP, 1])
        with ExitStack() as st:
            rows, gathered, load_idx, gather = gather_rows(st)
            S = SegmentSums(st, FEAT, sums)
            key = sb(st, "key_src", [EP, COLS, 2], I32)
            by_src_masks.scratch(st)
            b3 = sb(st, "b3", [1, TPW])
            b3_part = [sb(st, f"b3_part{n}", [1, TPW], BF16) for n in range(3)]
            b3_rest = sb(st, "b3_rest", [1, TPW])
            w3h = sb(st, "w3h", [FEAT, HEADS3, FEAT])
            fc = sb(st, "fc", [FEAT, 2, FEAT])
            part = sb(st, "part", [FEAT, 2, HEADS3, FEAT])
            key_in, b3_in, weights_in, parts_in, blank, split = (K.sem(n) for n in ("key_in", "b3_in", "weights_in", "parts_in", "blank", "split"))
            laid, chain_v = K.sem("laid"), K.sem("chain_v")
            block = st.enter_context(nc.Block())
            small = [(w1[n * MUL:(n + 1) * MUL, n // 2, (n % 2) * HID:(n % 2 + 1) * HID], A["L2_gnn_W1"]) for n in range(CH)]
            for o in range(2):
                at = slice(o * HID, (o + 1) * HID)
                small += [(w2[at, at], A["L2_gnn_W2"]), (w3[at, o, :], A["L2_gnn_W3"]),
                          (b1[at, :], A["L2_gnn_b1"].unsqueeze(1)), (b2[at, :], A["L2_gnn_b2"].unsqueeze(1))]
            small += [(w3h[:, :, :], A["L3_gnn_w"].rearrange("h f o -> f h o")),
                      (fc[:, :, :].rearrange("p s o -> p (s o)"), on_all(A["L3_gnn_fc_w"][0, :], FEAT)),
                      (fcb[:, :], on_all(A["L3_gnn_fc_b"])), (own_w[0:MUL, 0:MUL], A["L2_gnn_Ws"])]
            for u in range(MUL):
                for m in range(3):
                    at = MUL + 3 * u + m
                    small.append((own_w[at:at + 1, MUL + m:FEAT:3], A["L2_gnn_Wv"][u:u + 1, :]))

            @block.sync
            def _(sp):
                def body(i):
                    for k in range(2):
                        load_idx(sp, 2 * i + k, k, i)
                body(0)
                sp.dma_start(b3[:, :], A["L2_gnn_b3"].unsqueeze(0)).then_inc(b3_in, 16)
                sp.dma_start(key[:, :, :], by_key).then_inc(key_in, 16)
                sp.dma_start(first_key[:, :], by_key[:, 0, 0:1], allow_slow_non_contiguous=True).then_inc(key_in, 16)
                sp.wait_ge(blank, 4)
                for target, source in small:
                    sp.dma_start(target, source, allow_slow_non_contiguous=True).then_inc(weights_in, 16)
                sp.wait_ge(split, 1)
                for m in range(3):
                    for o in range(2):
                        sp.dma_start(b3_rows[m:m + 1, o, :], b3_part[m][:, :]).then_inc(parts_in, 16)
                by_src_masks.load(sp)
                pairs(sp, body, first=1)
                sp.wait_ge(key_in, 32)
                sp.wait_ge(parts_in, 16 * 6)

            @block.tensor
            def _(pe):
                by_src_masks.turn(pe)

            @block.gpsimd
            def _(pool):
                def body(i):
                    for k in range(2):
                        t = 2 * i + k
                        K.wait(pool, "pool", laid, t - 1)
                        gather(pool, t, k, i)
                pairs(pool, body)

            @block.scalar
            def _(act):
                def body(i):
                    for k in range(2):
                        t = 2 * i + k
                        S.mask(act, t, k)
                        K.wait(act, "act", gathered[k], (i + 1) * (16 * CH))
                        nc.scalar.copy(S.message(k), rows[k][:, :, :].rearrange("p c f -> p f c")).then_inc(laid, 1)
                        S.store(act, t, k, i)
                pairs(act, body)
                S.finish(act)

            @block.vector
            def _(dve):
                c = Chain(dve, chain_v)
                for ins in S.start():
                    c.link(ins)
                for w in (w1[:, :, :], w2[:, :], w3[:, :, :], own_w[:, :]):
                    nc.vector.memset(w, 0.0).then_inc(blank, 1)
                nc.vector.memset(ones_b[:, :], 1.0)
                dve.wait_ge(b3_in, 16)
                c.step(nc.vector.tensor_scalar(b3[:, 64:128], b3[:, 64:128], 3.0 ** -0.5, None, ALU.mult))
                c.step(nc.vector.tensor_copy(b3_part[0][:, :], b3[:, :]))
                c.step(nc.vector.tensor_tensor(b3_rest[:, :], b3[:, :], b3_part[0][:, :], ALU.subtract))
                c.step(nc.vector.tensor_copy(b3_part[1][:, :], b3_rest[:, :]))
                c.step(nc.vector.tensor_tensor(b3_rest[:, :], b3_rest[:, :], b3_part[1][:, :], ALU.subtract))
                c.step(nc.vector.tensor_copy(b3_part[2][:, :], b3_rest[:, :]))
                dve.sem_inc(split, 1)
                dve.wait_ge(key_in, 32)
                by_src_masks.make(dve, c, key[:, :, 0])
                dve.wait_ge(weights_in, 16 * len(small))
                c.link(nc.vector.tensor_scalar(w3[:, :, 64:128], w3[:, :, 64:128], 3.0 ** -0.5, None, ALU.mult))
                for n in range(2):
                    c.link(nc.vector.tensor_tensor(part[:, n, :, :], w3h[:, :, :], fc[:, n, :].unsqueeze(1).to_broadcast([FEAT, HEADS3, FEAT]), ALU.mult))
                c.join()
                c.link(nc.vector.tensor_reduce(w_sd[:, :, :], part[:, :, :, :], AX.X, ALU.add))
                c.restart()

                def body(i):
                    for k in range(2):
                        t = 2 * i + k
                        K.wait(dve, "dve", laid, t + 1)
                        S.scan(dve, c, t, k)
                        c.restart()
                pairs(dve, body)
        K.recycle()
        mend_sums(sums, FEAT)

        def begin(c, at):
            c.step(nc.vector.tensor_tensor(agg[:, at, :], agg[:, at, :], of_set(has_dst[:, at]), ALU.mult))
            c.link(nc.vector.tensor_tensor(x[:, at, :], x[:, at, :], agg[:, at, :], ALU.add))
        node_stage(begin, None, gather=(sums, last_dst, agg), normal="after", stores=table_of_h)

        with ExitStack() as st:
            rows, gathered, load_idx, gather = gather_rows(st)
            S = SegmentSums(st, FEAT, sums)
            radial = [sb(st, f"radial{k}", [EP, CH * MUL]) for k in range(2)]
            sh = sb(st, "sh", [EP, COLS, 4])
            radial_t = sb(st, "radial_t", [128, EP])
            x1 = sb(st, "x1", [128, 2, 4 * EP])
            x2 = [sb(st, f"x2_{k}", [128, 2, 4 * EP]) for k in range(2)]
            hv1 = sb(st, "hv1", [EP, CH, MUL, 3])
            zz = [sb(st, f"zz{k}", [EP, CH, 3, MUL]) for k in range(2)]
            zv = [sb(st, f"zv{k}", [EP, CH, 3, MUL]) for k in range(2)]
            zv_wide = [sb(st, f"zv_wide{k}", [EP, CH, 3, MUL, MUL]) for k in range(2)]
            prod_a = [sb(st, f"prod_a{k}", [EP, 4, MUL, 3, MUL]) for k in range(2)]
            prod_b = [sb(st, f"prod_b{k}", [EP, 4, 3, MUL, MUL]) for k in range(2)]
            res_a = sb(st, "res_a", [EP, CH, MUL, 3])
            res_b = sb(st, "res_b", [EP, CH, 3, MUL])
            cross = sb(st, "cross", [EP, CH, MUL, 3])
            radial_ps = ps(st, "radial_ps", [128, EP])
            hid_ps = ps(st, "hid_ps", [128, 2, 512])
            tp_ps = [ps(st, f"tp_ps{k}", [EP, 2, 512]) for k in range(2)]
            radial_in = [K.sem(f"radial_in{k}") for k in range(2)]
            (turned, turned_sb, hid1, act1, hid2, act2, tpw, taken, chain_v, chain_odd, used, scaled, widened, prepared, sh_in) = (
                K.sem(n) for n in ("turned", "turned_sb", "hid1", "act1", "hid2", "act2", "tpw", "taken", "chain_v", "chain_odd", "used",
                                   "scaled", "widened", "prepared", "sh_in"))
            block = st.enter_context(nc.Block())

            @block.sync
            def _(sp):
                sp.dma_start(sh[:, :, :], edge_rows(A["edge_attr_4"])).then_inc(sh_in, 16)

                def body(i):
                    for k in range(2):
                        t = 2 * i + k
                        K.wait(sp, "sp", turned, t - 1)
                        sp.dma_start(radial[k][:, :], edge_rows(A["edge_attr_8"])[:, cols(t), :].rearrange("p c f -> p (c f)")).then_inc(radial_in[k], 16)
                        load_idx(sp, t, k, i)
                pairs(sp, body)

            @block.gpsimd
            def _(pool):
                def body(i):
                    for k in range(2):
                        t = 2 * i + k
                        K.wait(pool, "pool", prepared, t - 1)
                        K.wait(pool, "pool", widened, t - 1)
                        gather(pool, t, k, i)
                pairs(pool, body)

            @block.tensor
            def _(pe):
                def turn(t, k, i):
                    K.wait(pe, "pe", radial_in[k], i * 16 + 16)
                    K.wait(pe, "pe", turned_sb, t)
                    nc.tensor.transpose(radial_ps[:, :], radial[k][:, :], ident[0:EP, 0:EP]).then_inc(turned, 1)

                def hidden1(t):
                    K.wait(pe, "pe", turned_sb, t + 1)
                    K.wait(pe, "pe", act2, 2 * t)
                    for a in range(2):
                        for b in range(4):
                            last = nc.tensor.matmul(hid_ps[:, a, b * EP:(b + 1) * EP], w1[:, a * 4 + b, :], radial_t[:, :], start=True, stop=True)
                        last.then_inc(hid1, 1)

                def hidden2(t, a):
                    K.wait(pe, "pe", act1, 2 * t + a + 1)
                    nc.tensor.matmul(hid_ps[:, a, 0:4 * EP], w2[:, :], x1[:, a, :], start=True, stop=True).then_inc(hid2, 1)

                def products(t, k, q):
                    a = q // 2
                    if q % 2 == 0:
                        K.wait(pe, "pe", act2, 2 * t + a + 1)
                    K.wait(pe, "pe", taken, 4 * t + q - 1)
                    for j in range(2):
                        b = (q % 2) * 2 + j
                        o = tp_ps[q % 2][:, j, :]
                        nc.tensor.matmul(o, x2[k][:, a, b * EP:(b + 1) * EP], w3[:, :, :].rearrange("p o n -> p (o n)"), start=True, stop=False)
                        last = nc.tensor.matmul(o, ones_b[:, :], b3_rows[:, :, :].rearrange("p o n -> p (o n)"), start=False, stop=True)
                    last.then_inc(tpw, 1)

                turn(0, 0, 0)
                hidden1(0)
                hidden2(0, 0)
                hidden2(0, 1)

                def body(i):
                    for k in range(2):
                        t = 2 * i + k
                        more = not known_ge(t, 2 * PAIRS - 1)
                        products(t, k, 0)
                        products(t, k, 1)
                        if more:
                            turn(t + 1, 1 - k, i + k)
                            hidden1(t + 1)
                            hidden2(t + 1, 0)
                            hidden2(t + 1, 1)
                        products(t, k, 2)
                        products(t, k, 3)
                pairs(pe, body, ahead=True)

            @block.scalar
            def _(act):
                def take_turned(t):
                    K.wait(act, "act", turned, t + 1)
                    K.wait(act, "act", hid1, 2 * t)
                    nc.scalar.copy(radial_t[:, :], radial_ps[:, :]).then_inc(turned_sb, 1)

                def layer1(t):
                    for a in range(2):
                        K.wait(act, "act", hid1, 2 * t + a + 1)
                        K.wait(act, "act", hid2, 2 * t + a - 1)
                        nc.scalar.activation(x1[:, a, :], hid_ps[:, a, 0:4 * EP], ACT.Silu, bias=b1[:, 0:1]).then_inc(act1, 1)

                def layer2(t, k):
                    for a in range(2):
                        K.wait(act, "act", hid2, 2 * t + a + 1)
                        K.wait(act, "act", tpw, 4 * (t - 1))
                        nc.scalar.activation(x2[k][:, a, :], hid_ps[:, a, 0:4 * EP], ACT.Silu, bias=b2[:, 0:1]).then_inc(act2, 1)
                def widen(t, k, i):
                    K.wait(act, "act", gathered[k], (i + 1) * (16 * CH))
                    K.wait(act, "act", used, t - 1)
                    nc.scalar.copy(zz[k][:, :, 2, :], rows[k][:, :, 0:MUL])
                    if not known_ge(t, 2 * PAIRS - 1):
                        take_turned(t + 1)
                    K.wait(act, "act", scaled, t + 1)
                    nc.scalar.copy(zv_wide[k][:, :, :, :, :].rearrange("p c i u w -> p (c i u) w"),
                                   zv[k][:, :, :, :].rearrange("p c i u -> p (c i u)").unsqueeze(2).to_broadcast([EP, CH * 3 * MUL, MUL])).then_inc(widened, 1)

                take_turned(0)
                layer1(0)
                layer2(0, 0)
                widen(0, 0, 0)

                def body(i):
                    for k in range(2):
                        t = 2 * i + k
                        more = not known_ge(t, 2 * PAIRS - 1)
                        if more:
                            layer1(t + 1)
                        S.mask(act, t, k)
                        if more:
                            layer2(t + 1, 1 - k)
                        if not first_chunk(t):
                            S.store(act, t - 1, 1 - k, i - 1 + k)
                        if more:
                            widen(t + 1, 1 - k, i + k)
                pairs(act, body, ahead=True)
                S.store(act, 2 * PAIRS - 1, 1, PAIRS - 1)
                S.finish(act)

            @block.vector
            def _(dve):
                chains = [Chain(dve, chain_v), Chain(dve, chain_odd)]
                for ins in S.start():
                    chains[1].link(ins)
                chains[1].restart()

                def sh1(t):
                    return sh[:, cols(t), 1:4].unsqueeze(2).to_broadcast([EP, CH, MUL, 3])

                def prepare(c, t, k, i):
                    K.wait(dve, "dve", gathered[k], (i + 1) * (16 * CH))
                    hs = rows[k][:, :, 0:MUL]
                    hv = rows[k][:, :, MUL:FEAT].rearrange("p c (u i) -> p c u i", i=3)
                    sh0 = sh[:, cols(t), 0:1]
                    K.wait(dve, "dve", widened, t - 1)
                    nc.vector.tensor_tensor(zv[k][:, :, :, :], hv.rearrange("p c u i -> p c i u"),
                                            sh0.unsqueeze(3).to_broadcast([EP, CH, 3, MUL]), ALU.mult).then_inc(scaled, 1)
                    c.link(nc.vector.tensor_tensor(zz[k][:, :, 0, :], hs, sh0.to_broadcast([EP, CH, MUL]), ALU.mult))
                    return c.mark(nc.vector.tensor_tensor(hv1[:, :, :, :], hv, sh1(t), ALU.mult))

                def dot(c, t, k, multiplied):
                    c.until(multiplied)
                    K.wait(dve, "dve", scaled, t + 1)
                    dve.sem_inc(prepared, 1)
                    return c.mark(nc.vector.tensor_reduce(zz[k][:, :, 1, :], hv1[:, :, :, :], AX.X, ALU.add))

                dve.wait_ge(sh_in, 16)
                ready = [dot(chains[1], 0, 0, prepare(chains[1], 0, 0, 0)), 0]

                def body(i):
                    for k in range(2):
                        t = 2 * i + k
                        c, last_c = chains[k], chains[1 - k]
                        K.wait(dve, "dve", widened, t + 1)

                        def total(q, done):
                            c.until(done)
                            K.wait(dve, "dve", taken, 4 * t + q + 1)
                            four = slice(4 * q, 4 * q + 4)
                            c.link(nc.vector.tensor_reduce(res_a[:, four, :, :].rearrange("p c w b -> p (c w b)"),
                                                           prod_a[q % 2][:, :, :, :, :].rearrange("p c w b u -> p (c w b) u"), AX.X, ALU.add))
                            c.link(nc.vector.tensor_reduce(res_b[:, four, :, :].rearrange("p c i w -> p (c i) w"),
                                                           prod_b[q % 2][:, :, :, :, :].rearrange("p c i u w -> p (c i) w u"), AX.X, ALU.add))
                        done = 0
                        more = not known_ge(t, 2 * PAIRS - 1)
                        last_c.until(ready[k])
                        for q in range(4):
                            K.wait(dve, "dve", tpw, 4 * t + q + 1)
                            four = slice(4 * q, 4 * q + 4)
                            wts = tp_ps[q % 2][:, :, :].rearrange("p j (o n) -> p (j o) n", o=2)
                            shape = [EP, 4, MUL, 3 * MUL]
                            if q >= 2:
                                c.until(summed)
                            c.link(nc.vector.tensor_tensor(prod_a[q % 2][:, :, :, :, :].rearrange("p c w b u -> p c w (b u)"),
                                                           wts[:, :, 0:192].rearrange("p c (n w) -> p c w n", w=MUL),
                                                           zz[k][:, four, :, :].rearrange("p c b u -> p c (b u)").unsqueeze(2).to_broadcast(shape), ALU.mult))
                            nc.vector.tensor_tensor(prod_b[q % 2][:, :, :, :, :].rearrange("p c i u w -> p c i (u w)"),
                                                    wts[:, :, 192:256].unsqueeze(2).to_broadcast([EP, 4, 3, MUL * MUL]),
                                                    zv_wide[k][:, four, :, :, :].rearrange("p c i u w -> p c i (u w)"), ALU.mult).then_inc(taken, 1)
                            made = c.n
                            if q == 1:
                                last_c.restart()
                            if q == 1 and not first_chunk(t):
                                S.scan(dve, c, t - 1, 1 - k, carried=True, settle=False)
                            if q == 3 and more:
                                multiplied = prepare(c, t + 1, 1 - k, i + k)
                            if q:
                                total(q - 1, done)
                                summed = c.n
                            done = made
                        total(3, done)
                        made = c.n
                        if more:
                            ready[1 - k] = dot(c, t + 1, 1 - k, multiplied)
                        c.until(made)
                        crossed = c.mark(nc.vector.tensor_tensor(cross[:, :, :, :], sh1(t), res_a[:, :, :, 2].unsqueeze(3).to_broadcast([EP, CH, MUL, 3]), ALU.mult))
                        msg = S.message(k)
                        K.wait(dve, "dve", S.scanned, t)
                        S.carry(c, k)
                        c.link(nc.vector.tensor_tensor(msg[:, 0:MUL, :], res_a[:, :, :, 0].rearrange("p c w -> p w c"),
                                                       res_a[:, :, :, 1].rearrange("p c w -> p w c"), ALU.add))
                        c.until(crossed)
                        dve.sem_inc(used, 1)
                        c.link(nc.vector.tensor_tensor(msg[:, MUL:FEAT, :].rearrange("p (w i) c -> p w i c", i=3),
                                                       cross[:, :, :, :].rearrange("p c w i -> p w i c"),
                                                       res_b[:, :, :, :].rearrange("p c i w -> p w i c"), ALU.add))
                pairs(dve, body, ahead=True)
                S.scan(dve, chains[1], 2 * PAIRS - 1, 1, carried=True)
        K.recycle()
        mend_sums(sums, FEAT)
        with ExitStack() as st:
            h3 = sb(st, "h3", [NP, NB, FEAT + HEADS3])

            def begin(c, at):
                c.step(nc.vector.tensor_tensor(agg[:, at, :], agg[:, at, :], of_set(has_dst[:, at]), ALU.mult))
                c.link(nc.vector.scalar_tensor_tensor(x[:, at, :], agg[:, at, :], 1.0 / 16, x[:, at, :], ALU.mult, ALU.add))

            def finish(c, at, product):
                c.step(nc.vector.scalar_tensor_tensor(x[:, at, :], product, MUL ** -0.5, x[:, at, :], ALU.mult, ALU.add))

            def scores(c, at, product):
                c.link(nc.vector.tensor_scalar(a_src[:, at, :], product[:, :, 0:HEADS3], fcb[:, 0:1], None, ALU.add))
                c.link(nc.vector.tensor_copy(h3[:, at, FEAT:], product[:, :, HEADS3:]))
                c.link(nc.vector.tensor_copy(h3[:, at, 0:FEAT], h[:, at, :]))
            node_stage(begin, finish, FEAT, h, own_w[:, :], gather=(sums, last_dst, agg), normal="after",
                       then=(w_sd[:, :, :].rearrange("p s h -> p (s h)"), 2 * HEADS3, scores),
                       stores=lambda at: [(node_rows(tab_h3)[:, at, :], h3[:, at, :]), (node_rows(tab_a3)[:, at, :], a_src[:, at, :])])

        weights.close()

        def mend_attention():
            wide = FEAT + 1
            heads = [wide, HEADS3, EP]
            with ExitStack() as st:
                tails = sb(st, "tails", [EP, ATT_ROW])
                ends = sb(st, "ends", [EP, ATT_ROW])
                fixed = sb(st, "fixed", [EP, ATT_ROW])
                both = sb(st, "both", [EP, 2, HEADS3, wide])
                no_carry = sb(st, "no_carry", [wide, EP])
                no_pass = sb(st, "no_pass", [wide, EP])
                tail_top = sb(st, "tail_top", heads)
                carry_top = sb(st, "carry_top", [wide, HEADS3, EP + 1])
                carry = sb(st, "carry", [wide, HEADS3, EP + 1])
                factor = sb(st, "factor", [wide, 2, HEADS3, EP])
                part = sb(st, "part", heads)
                end_rows = sb(st, "end_rows", [EP, HEADS3, wide])
                mix = sb(st, "mix", [EP, 2, HEADS3])
                top_end = sb(st, "top_end", [EP, HEADS3])
                turn = ps(st, "turn", [wide, 2, HEADS3, 128])
                back = ps(st, "back", [EP, 2, 512])
                loaded, arranged, turned, shifted, exped, scanned, backed, mended, chain_v = (K.sem(n) for n in (
                    "loaded", "arranged", "turned", "shifted", "exped", "scanned", "backed", "mended", "chain_v"))
                got, put_back = (K.own(n) for n in ("got", "put_back"))
                block = st.enter_context(nc.Block())

                @block.sync
                def _(sp):
                    sp.dma_start(tails[:, :], edge_rows(sums3)[:, COLS - 1, :]).then_inc(loaded, 16)

                @block.tensor
                def _(pe):
                    pe.wait_ge(arranged, 1)
                    for n in range(2):
                        for j in range(HEADS3):
                            last = nc.tensor.transpose(turn[:, n, j, 0:EP], both[:, n, j, :], ident[0:EP, 0:EP])
                    last.then_inc(turned, 1)
                    pe.wait_ge(scanned, 1)
                    for n, row in enumerate((carry, carry_top)):
                        for j in range(HEADS3):
                            last = nc.tensor.transpose(back[:, n, j * 64:j * 64 + wide], row[:, j, 0:EP], ident[0:wide, 0:wide])
                    last.then_inc(backed, 1)

                @block.scalar
                def _(act):
                    act.wait_ge(shifted, 1)
                    nc.scalar.activation(factor[:, :, :, :], factor[:, :, :, :], ACT.Exp).then_inc(exped, 1)
                    act.wait_ge(shifted, 2)
                    nc.scalar.activation(mix[:, :, :], mix[:, :, :], ACT.Exp).then_inc(exped, 1)

                @block.vector
                def _(dve):
                    c = Chain(dve, chain_v)
                    c.link(nc.vector.tensor_scalar(no_carry[:, :], by_src_masks.fwd_row[0:wide, :], BIG, -BIG, ALU.mult, ALU.add))
                    c.link(nc.vector.tensor_scalar(no_pass[:, :], by_src_masks.fwd_all[0:wide, :], BIG, -BIG, ALU.mult, ALU.add))
                    c.link(nc.vector.memset(carry_top[:, :, 0], -BIG))
                    c.link(nc.vector.memset(carry[:, :, 0], 0.0))

                    def arrange(target_, rows):
                        c.link(nc.vector.tensor_copy(target_[:, :, 0:FEAT], rows[:, 0:ATT].rearrange("p (h f) -> p h f", h=HEADS3)))
                        c.link(nc.vector.tensor_copy(target_[:, :, FEAT], rows[:, ATT:ATT_SUMS]))
                    dve.wait_ge(loaded, 16)
                    arrange(both[:, 0, :, :], tails)
                    c.link(nc.vector.tensor_copy(both[:, 1, :, :], tails[:, ATT_SUMS:].unsqueeze(2).to_broadcast([EP, HEADS3, wide])))
                    c.join()
                    dve.sem_inc(arranged, 1)
                    dve.wait_ge(turned, 1)
                    c.step(nc.vector.tensor_tensor(tail_top[:, :, :], turn[:, 1, :, 0:EP], no_carry[:, :].unsqueeze(1).to_broadcast(heads), ALU.add))
                    for j in range(HEADS3):
                        c.link(nc.vector.tensor_tensor_scan(carry_top[:, j, 1:EP + 1], no_pass[:, :], tail_top[:, j, :], -BIG, ALU.add, ALU.max))
                    c.join()
                    c.link(nc.vector.tensor_tensor(factor[:, 1, :, :], tail_top[:, :, :], carry_top[:, :, 1:EP + 1], ALU.subtract))
                    c.step(nc.vector.tensor_tensor(factor[:, 0, :, :], carry_top[:, :, 0:EP], no_pass[:, :].unsqueeze(1).to_broadcast(heads), ALU.add))
                    c.step(nc.vector.tensor_tensor(factor[:, 0, :, :], factor[:, 0, :, :], carry_top[:, :, 1:EP + 1], ALU.subtract))
                    dve.sem_inc(shifted, 1)
                    dve.wait_ge(exped, 1)
                    c.step(nc.vector.tensor_tensor(part[:, :, :], factor[:, 1, :, :], turn[:, 0, :, 0:EP], ALU.mult))
                    for j in range(HEADS3):
                        c.link(nc.vector.tensor_tensor_scan(carry[:, j, 1:EP + 1], factor[:, 0, j, :], part[:, j, :], 0.0, ALU.mult, ALU.add))
                    c.join()
                    dve.sem_inc(scanned, 1)
                    dve.wait_ge(backed, 1)
                    dve.wait_ge(got, 16)
                    carried = back[:, 0, 0:HEADS3 * 64].rearrange("p (h f) -> p h f", h=HEADS3)[:, :, 0:wide]
                    carried_top = back[:, 1, 0:HEADS3 * 64].rearrange("p (h f) -> p h f", h=HEADS3)[:, :, 0]
                    end_top = ends[:, ATT_SUMS:]
                    arrange(end_rows, ends)
                    c.step(nc.vector.tensor_tensor(top_end[:, :], carried_top, end_top, ALU.max))
                    c.link(nc.vector.tensor_tensor(mix[:, 0, :], end_top, top_end[:, :], ALU.subtract))
                    c.step(nc.vector.tensor_tensor(mix[:, 1, :], carried_top, top_end[:, :], ALU.subtract))
                    dve.sem_inc(shifted, 1)
                    dve.wait_ge(exped, 2)
                    shape = [EP, HEADS3, wide]
                    c.link(nc.vector.tensor_tensor(end_rows[:, :, :], end_rows[:, :, :], mix[:, 0, :].unsqueeze(2).to_broadcast(shape), ALU.mult))
                    c.step(nc.vector.tensor_tensor(both[:, 0, :, :], carried, mix[:, 1, :].unsqueeze(2).to_broadcast(shape), ALU.mult))
                    c.step(nc.vector.tensor_tensor(end_rows[:, :, :], end_rows[:, :, :], both[:, 0, :, :], ALU.add))
                    c.link(nc.vector.tensor_copy(fixed[:, 0:ATT].rearrange("p (h f) -> p h f", h=HEADS3), end_rows[:, :, 0:FEAT]))
                    c.link(nc.vector.tensor_copy(fixed[:, ATT:ATT_SUMS], end_rows[:, :, FEAT]))
                    c.link(nc.vector.tensor_copy(fixed[:, ATT_SUMS:], top_end[:, :]))
                    c.join()
                    dve.sem_inc(mended, 1)
                    c.restart()

                @block.gpsimd
                def _(pool):
                    pool.indirect_dma_start(ends[:, :], None, sums3, bass.IndirectOffsetOnAxis(ap=by_src_masks.endrow[:, 0:1], axis=0)).then_inc(got, 16)
                    pool.wait_ge(mended, 1)
                    pool.wait_ge(loaded, 16)
                    pool.indirect_dma_start(sums3, bass.IndirectOffsetOnAxis(ap=by_src_masks.endrow[:, 0:1], axis=0), fixed[:, :], None).then_inc(put_back, 16)
                    pool.wait_ge(put_back, 16)
            K.recycle()

        with ExitStack() as st:
            idx = [sb(st, f"idx{k}", [EP, CH, 2], I32) for k in range(2)]
            rows = [sb(st, f"hs{k}", [EP, CH, FEAT + HEADS3]) for k in range(2)]
            own = Spread(st, HEADS3, own_rows, by_src_masks)
            no_cont = sb(st, "no_cont", [EP, COLS])
            no_cont_h = [sb(st, f"no_cont_h{k}", [EP, HEADS3, CH + 1]) for k in range(2)]
            score = sb(st, "score", [EP, HEADS3, CH + 1])
            score_in = sb(st, "score_in", [EP, HEADS3, CH])
            most = [sb(st, f"most{k}", [EP, HEADS3, CH + 1]) for k in range(2)]
            shift = [sb(st, f"shift{k}", [EP, 2, HEADS3, CH]) for k in range(2)]
            S = SegmentSums(st, ATT_SUMS, sums3, [most[k][:, :, 1:CH + 1].rearrange("p h c -> p c h") for k in range(2)])
            placed = K.own("placed")
            idx_in = [K.sem(f"idx_in{k}") for k in range(2)]
            gathered = [K.own(f"gathered{k}") for k in range(2)]
            masked, shifted, exped, used, started, chain_v = (K.sem(n) for n in ("masked", "shifted", "exped", "used", "started", "chain_v"))
            block = st.enter_context(nc.Block())
            last_chunk = 2 * PAIRS - 1

            @block.sync
            def _(sp):
                def body(i):
                    for k in range(2):
                        t = 2 * i + k
                        K.wait(sp, "sp", gathered[k], i * (16 * CH))
                        sp.dma_start(idx[k][:, :, :], edge_rows(by_src)[:, cols(t), :]).then_inc(idx_in[k], 16)
                pairs(sp, body)

            @block.gpsimd
            def _(pool):
                own.place(pool, lambda b: a_src[:, b, :], first_src, tab_a3, first_key[:, 0:1], placed)

                def body(i):
                    for k in range(2):
                        t = 2 * i + k
                        K.wait(pool, "pool", idx_in[k], i * 16 + 16)
                        K.wait(pool, "pool", used, t - 1)
                        for g in range(CH):
                            pool.indirect_dma_start(rows[k][:, g, :], None, tab_h3,
                                                    bass.IndirectOffsetOnAxis(ap=idx[k][:, g, 1:2], axis=0)).then_inc(gathered[k], 16)
                pairs(pool, body)

            @block.scalar
            def _(act):
                act.wait_ge(placed, own.PLACED)
                act.wait_ge(started, 1)
                own.load(act, 0, 0)
                own.load(act, 1, 1)
                own.lay(act, 0, 0, 0)

                def body(i):
                    for k in range(2):
                        t = 2 * i + k
                        K.wait(act, "act", shifted, t - 1)
                        nc.scalar.copy(no_cont_h[k][:, :, 1:CH + 1],
                                       no_cont[:, cols(t)].unsqueeze(1).to_broadcast([EP, HEADS3, CH])).then_inc(masked, 1)
                        if not known_ge(t, last_chunk):
                            own.lay(act, t + 1, 1 - k, i + k)
                        if not known_ge(t, last_chunk - 1):
                            K.wait(act, "act", own.laid, t + 1)
                            own.load(act, t + 2, k)
                        if not first_chunk(t):
                            S.store(act, t - 1, 1 - k, i - 1 + k)
                        K.wait(act, "act", shifted, t + 1)
                        K.wait(act, "act", S.scanned, t - 1)
                        weight = S.message(k)[:, ATT:ATT_SUMS, :]
                        rescale = S.keep[k][:, ATT:ATT_SUMS, 1:CH + 1]
                        nc.scalar.activation(weight, shift[k][:, 1, :, :], ACT.Exp).then_inc(exped, 1)
                        nc.scalar.activation(rescale, shift[k][:, 0, :, :], ACT.Exp).then_inc(exped, 1)
                        K.wait(act, "act", exped, 2 * t + 2)
                        nc.scalar.copy(S.keep[k][:, 0:ATT, 1:CH + 1].rearrange("p (h f) c -> p h f c", h=HEADS3),
                                       rescale.unsqueeze(2).to_broadcast([EP, HEADS3, FEAT, CH])).then_inc(S.kept, 1)
                pairs(act, body, ahead=True)
                S.store(act, last_chunk, 1, PAIRS - 1)
                S.finish(act)

            @block.vector
            def _(dve):
                c = Chain(dve, chain_v)
                for ins in S.start():
                    c.link(ins)
                c.link(nc.vector.tensor_scalar(no_cont[:, :], by_src_masks.cont[:, :], BIG, -BIG, ALU.mult, ALU.add))
                for k in range(2):
                    c.link(nc.vector.memset(no_cont_h[k][:, :, 0], -BIG))
                c.link(nc.vector.memset(most[1][:, :, CH], -BIG))
                dve.wait_ge(placed, own.PLACED)
                for ins in own.start():
                    c.link(ins)
                c.join()
                dve.sem_inc(started, 1)
                c.restart()

                def body(i):
                    for k in range(2):
                        t = 2 * i + k
                        own.scan(dve, c, t, k)
                        K.wait(dve, "dve", gathered[k], (i + 1) * (16 * CH))
                        now, before_ = most[k][:, :, 1:CH + 1], most[k][:, :, 0:CH]
                        c.link(nc.vector.tensor_copy(score[:, :, 0], most[1 - k][:, :, CH]))
                        c.step(nc.vector.tensor_tensor(score_in[:, :, :], own.rows(k).rearrange("p c h -> p h c"),
                                                       rows[k][:, :, FEAT:].rearrange("p c h -> p h c"), ALU.add))
                        c.step(nc.vector.scalar_tensor_tensor(score[:, :, 1:CH + 1], score_in[:, :, :], 0.2, score_in[:, :, :], ALU.mult, ALU.max))
                        K.wait(dve, "dve", masked, t + 1)
                        K.wait(dve, "dve", S.copied, t - 1)
                        flat = lambda ap: ap[:, :, :].rearrange("p h c -> p (h c)")
                        c.step(nc.vector.tensor_tensor_scan(flat(most[k]), flat(no_cont_h[k]), flat(score), -BIG, ALU.add, ALU.max))
                        c.link(nc.vector.tensor_tensor(shift[k][:, 1, :, :], score[:, :, 1:CH + 1], now, ALU.subtract))
                        c.step(nc.vector.tensor_tensor(shift[k][:, 0, :, :], before_, no_cont_h[k][:, :, 1:CH + 1], ALU.add))
                        c.step(nc.vector.tensor_tensor(shift[k][:, 0, :, :], shift[k][:, 0, :, :], now, ALU.subtract))
                        dve.sem_inc(shifted, 1)
                        K.wait(dve, "dve", exped, 2 * t + 1)
                        shape = [EP, HEADS3, FEAT, CH]
                        c.step(nc.vector.tensor_tensor(S.message(k)[:, 0:ATT, :].rearrange("p (h f) c -> p h f c", h=HEADS3),
                                                       rows[k][:, :, 0:FEAT].rearrange("p c f -> p f c").unsqueeze(1).to_broadcast(shape),
                                                       S.message(k)[:, ATT:ATT_SUMS, :].unsqueeze(2).to_broadcast(shape), ALU.mult))
                        dve.sem_inc(used, 1)
                        S.scan(dve, c, t, k)
                        c.restart()
                pairs(dve, body)
        K.recycle()

        with ExitStack() as st:
            agg3 = sb(st, "agg3", [NP, NB, ATT_ROW])
            share = sb(st, "share", [NP, NB, HEADS3])
            mend_attention()
            w = sb(st, "w_out", [ATT, FEAT])
            bias = sb(st, "b_out", [NP, FEAT])
            load([(w[:, :], A["L3_gnn_w"].rearrange("h f o -> (h f) o")), (bias[:, :], on_all(A["L3_gnn_bias"]))])

            def begin(c, at):
                weighted = agg3[:, at, 0:ATT].rearrange("p b (h f) -> p b h f", h=HEADS3)
                c.link(nc.vector.tensor_tensor(x[:, at, :], x[:, at, :], bias[:, :].unsqueeze(1).to_broadcast([NP, SET, FEAT]), ALU.add))
                c.step(nc.vector.reciprocal(share[:, at, :], agg3[:, at, ATT:ATT_SUMS]))
                c.step(nc.vector.tensor_tensor(share[:, at, :], share[:, at, :], has_src[:, at].unsqueeze(2).to_broadcast([NP, SET, HEADS3]), ALU.mult))
                c.link(nc.vector.tensor_tensor(weighted, weighted, share[:, at, :].unsqueeze(3).to_broadcast([NP, SET, HEADS3, FEAT]), ALU.mult))

            def finish(c, at, product):
                c.link(nc.vector.scalar_tensor_tensor(x[:, at, :], product, 1.0 / HEADS3, x[:, at, :], ALU.mult, ALU.add))

            def rows_out(at):
                if at.stop < NB:
                    return [(out[at.start * NP:at.stop * NP, :].rearrange("(b l) f -> l b f", l=NP), x[:, at, :])]
                full = (NB - 1) * NP
                return [(out[at.start * NP:full, :].rearrange("(b l) f -> l b f", l=NP), x[:, at.start:NB - 1, :]),
                        (out[full:NODES, :], x[0:TAIL, NB - 1, :])]
            node_stage(begin, finish, FEAT, agg3[:, :, 0:ATT], w[:, :], gather=(sums3, last_src, agg3), stores=rows_out)


_INS = ['x', 'src', 'dst', 'edge_attr3_2x32', 'edge_attr_4', 'edge_attr_8', 'L0_gnn_W1', 'L0_gnn_b1', 'L0_gnn_W2s', 'L0_gnn_b2s',
        'L0_gnn_W2d', 'L0_gnn_b2d', 'L0_gnn_attn', 'L2_gnn_W1', 'L2_gnn_b1', 'L2_gnn_W2', 'L2_gnn_b2', 'L2_gnn_W3', 'L2_gnn_b3',
        'L2_gnn_Ws', 'L2_gnn_Wv', 'L3_gnn_w', 'L3_gnn_fc_w', 'L3_gnn_fc_b', 'L3_gnn_bias']


def kernel(**inputs):
    import numpy as _np
    import concourse.bacc as _bacc
    from concourse import mybir as _mybir
    from concourse.bass_utils import run_bass_kernel_spmd as _run

    nc = _bacc.Bacc("TRN2", target_bir_lowering=False, num_devices=1)
    arrays, args = {}, {}
    for name in _INS:
        a = _np.ascontiguousarray(inputs[name])
        arrays[f"in_{name}"] = a
        args[name] = nc.dram_tensor(f"in_{name}", a.shape, _mybir.dt.from_np(a.dtype), kind="ExternalInput").ap()
    out = nc.dram_tensor("out_x", (NODES, FEAT), F32, kind="ExternalOutput").ap()
    build(nc, args, out)
    r = _run(nc, [arrays], core_ids=[0])
    return r.results[0]["out_x"]
```
